# Optimizing a Trainium2 kernel written in Bass

```python
import numpy as np
import jax
import jax.numpy as jnp

def _softmax(x, axis=-1):
    return jax.nn.softmax(x, axis=axis)

def _gelu(x):
    return jax.nn.gelu(x, approximate=True)

def _silu(x):
    return jax.nn.silu(x)

def _sigmoid(x):
    return jax.nn.sigmoid(x)

def _layernorm(x, axis=-1, eps=1e-05):
    m = jnp.mean(x, axis=axis, keepdims=True)
    v = jnp.var(x, axis=axis, keepdims=True)
    return (x - m) / jnp.sqrt(v + eps)

def _scatter_add(tgt, idx, src, axis=0):
    return tgt.at[idx].add(src)

def _segment_sum(src, seg, n):
    return jax.ops.segment_sum(src, seg, n)
kernel_name = 'mk_flamingo_gated_d4_seqx_r8_ba4da6'

def setup_inputs(seed: int=0):
    np.random.seed(seed)
    _w = jnp.asarray

    def _rec_inputs():
        import jax
        import jax.numpy as jnp
        _rk = jax.random.key(seed)
        x = -7.109e-05 + 0.9999 * jax.random.normal(jax.random.fold_in(_rk, 1), (32, 64, 512), jnp.float32)
        _lenS = 64 - jax.random.randint(jax.random.fold_in(_rk, 7), (32,), 0, max(1, 64 // 4) + 1, jnp.int32)
        _lenS2 = 64 - jax.random.randint(jax.random.fold_in(_rk, 8), (32,), 0, max(1, 64 // 4) + 1, jnp.int32)
        _ctx_4096P = jax.random.normal(jax.random.fold_in(_rk, 11), (32, 16, 512), jnp.float32)
        _ctx_4096c = jax.random.dirichlet(jax.random.fold_in(_rk, 511), 0.3 * jnp.ones((16,), jnp.float32), (32, 64))
        _ctx_4096t = jnp.einsum('bsk,bkd->bsd', _ctx_4096c, _ctx_4096P)
        _ctx_4096t = _ctx_4096t * jax.lax.rsqrt(jnp.mean(jnp.square(_ctx_4096t)) + 1e-12) * 0.953939
        ctx_4096 = -2.6191e-05 + 0.999952 * (_ctx_4096t + 0.3 * jax.random.normal(jax.random.fold_in(_rk, 611), (32, 64, 512), jnp.float32))
        pos_BxS2 = jnp.broadcast_to(jnp.arange(64, dtype=jnp.int32), (32, 64))
        _validS = jnp.arange(64)[None, :] < _lenS[:, None]
        _validS2 = jnp.arange(64)[None, :] < _lenS2[:, None]
        _causal = jnp.tril(jnp.ones((64, 64), dtype=bool))
        mask_BxSxS2_ik0 = jnp.where(jnp.broadcast_to(_validS2[:, None, :], (32, 64, 64)), 0, 1).astype(jnp.int32)
        _g = jax.random.normal(jax.random.fold_in(_rk, 9001), (2, 4), jnp.float32)
        _g = jnp.sign(_g) * jnp.maximum(jnp.abs(_g), 1.0) + (_g == 0) * 1.0
        g_xattn = _g[0]
        g_ffn = _g[1]
        return (x, ctx_4096, pos_BxS2, mask_BxSxS2_ik0, g_xattn, g_ffn)
    x, ctx_4096, pos_BxS2, mask_BxSxS2_ik0, g_xattn, g_ffn = _rec_inputs()

    def _L0_xattn_setup():
        import jax, jax.numpy as jnp
        import numpy as np
        TEXT_DIM = 512
        FEATURE_DIM = 512

        def _xavier_uniform(key, shape):
            fan_in, fan_out = (shape[1], shape[0])
            limit = float(np.sqrt(6.0 / (fan_in + fan_out)))
            return jax.random.uniform(key, shape, jnp.float32, -limit, limit)
        key = jax.random.key(seed)
        k1, k2, k3, k4 = jax.random.split(key, 4)
        text = jax.random.normal(k1, (8, 256, TEXT_DIM), jnp.float32)
        features = jax.random.normal(k2, (8, 72, FEATURE_DIM), jnp.float32)
        Wq = _xavier_uniform(k3, (FEATURE_DIM, TEXT_DIM))
        bq = jnp.zeros((FEATURE_DIM,), jnp.float32)
        Wk = _xavier_uniform(k4, (FEATURE_DIM, FEATURE_DIM))
        bk = jnp.zeros((FEATURE_DIM,), jnp.float32)
        return {'text': text, 'features': features, 'Wq': Wq, 'bq': bq, 'Wk': Wk, 'bk': bk}
    _L0_xattn_all = _L0_xattn_setup()
    _L0_xattn_in = {k: v for k, v in _L0_xattn_all.items() if k in ('Wq', 'bq', 'Wk', 'bk')}
    del _L0_xattn_all

    def _L0_ffn_setup():
        import jax, jax.numpy as jnp
        import numpy as np
        D_IN = 512
        D_OUT = 512
        RANK = 16
        NUM_EXPERTS = 8
        TOP_K = 2
        SCALING = 32.0 / RANK
        key = jax.random.key(seed)
        ks = jax.random.split(key, 6)
        x = jax.random.normal(ks[0], (4, 256, D_IN), dtype=jnp.float32)
        W_base = jax.random.normal(ks[1], (D_OUT, D_IN), dtype=jnp.float32) * (1.0 / np.sqrt(D_IN))
        b_base = jax.random.normal(ks[2], (D_OUT,), dtype=jnp.float32) * 0.01
        W_router = jax.random.normal(ks[3], (NUM_EXPERTS, D_IN), dtype=jnp.float32) * 0.01
        A_stack = jax.random.uniform(ks[4], (NUM_EXPERTS, RANK, D_IN), dtype=jnp.float32, minval=-1.0, maxval=1.0) * (1.0 / np.sqrt(D_IN))
        B_stack = jax.random.normal(ks[5], (NUM_EXPERTS, D_OUT, RANK), dtype=jnp.float32) * 0.02
        return {'x': x, 'W_base': W_base, 'b_base': b_base, 'W_router': W_router, 'A_stack': A_stack, 'B_stack': B_stack}
    _L0_ffn_all = _L0_ffn_setup()
    _L0_ffn_in = {k: v for k, v in _L0_ffn_all.items() if k in ('W_base', 'b_base', 'W_router', 'A_stack', 'B_stack')}
    del _L0_ffn_all

    def _L1_xattn_setup():
        import jax, jax.numpy as jnp
        import numpy as np
        HEADS = 8
        WINDOW = 16

        def _pointwise(W, b, t):
            return jnp.einsum('oc,bct->bot', W, t) + b[None, :, None]
        key = jax.random.key(seed)
        ks = jax.random.split(key, 10)
        B, C, T = (4, 64, 512)
        s = 0.02
        return {'x': jax.random.normal(ks[0], (B, C, T), jnp.float32), 'cond': jax.random.normal(ks[1], (B, C, T), jnp.float32), 'Wq': jax.random.normal(ks[2], (C, C), jnp.float32) * s, 'bq': jnp.zeros((C,), jnp.float32), 'Wk': jax.random.normal(ks[3], (C, C), jnp.float32) * s, 'bk': jnp.zeros((C,), jnp.float32), 'Wv': jax.random.normal(ks[4], (C, C), jnp.float32) * s, 'bv': jnp.zeros((C,), jnp.float32), 'Wo': jax.random.normal(ks[5], (C, C), jnp.float32) * s, 'bo': jnp.zeros((C,), jnp.float32)}
    _L1_xattn_all = _L1_xattn_setup()
    _L1_xattn_in = {k: v for k, v in _L1_xattn_all.items() if k in ('Wq', 'bq', 'Wk', 'bk', 'Wv', 'bv', 'Wo', 'bo')}
    del _L1_xattn_all

    def _L1_ffn_setup():
        import jax, jax.numpy as jnp
        import numpy as np
        SCALING = 32.0 / 16.0
        key = jax.random.key(seed)
        ks = jax.random.split(key, 7)
        B, T, D, O, R, E = (4, 256, 512, 512, 16, 8)
        x = jax.random.normal(ks[0], (B, T, D), dtype=jnp.float32)
        base_W = jax.random.normal(ks[1], (O, D), dtype=jnp.float32) * D ** (-0.5)
        base_b = jax.random.normal(ks[2], (O,), dtype=jnp.float32) * 0.01
        router_W = jax.random.normal(ks[3], (2 * E - 1, D), dtype=jnp.float32) * D ** (-0.5)
        router_b = jax.random.normal(ks[4], (2 * E - 1,), dtype=jnp.float32) * 0.01
        A = jax.random.normal(ks[5], (E, R, D), dtype=jnp.float32) * D ** (-0.5)
        Bm = jax.random.normal(ks[6], (E, O, R), dtype=jnp.float32) * R ** (-0.5)
        assigned_idx = 0
        others = [i for i in range(E) if i != assigned_idx]
        expert_map = jnp.array([assigned_idx] * E + others, dtype=jnp.int32)
        return {'x': x, 'base_W': base_W, 'base_b': base_b, 'router_W': router_W, 'router_b': router_b, 'A': A, 'B': Bm, 'expert_map': expert_map}
    _L1_ffn_all = _L1_ffn_setup()
    _L1_ffn_in = {k: v for k, v in _L1_ffn_all.items() if k in ('base_W', 'base_b', 'router_W', 'router_b', 'A', 'B', 'expert_map')}
    del _L1_ffn_all

    def _L2_xattn_setup():
        import jax, jax.numpy as jnp
        import numpy as np
        B, N, NKV = (2, 256, 256)
        E = 512
        H = 16
        HD = E // H
        LQ = E // 8
        LKV = E // 16
        key = jax.random.key(seed)
        ks = jax.random.split(key, 6)
        Q = jax.random.normal(ks[0], (B, N, E), dtype=jnp.float32)
        K = jax.random.normal(ks[1], (B, NKV, E), dtype=jnp.float32)
        Wq_d = jax.random.normal(ks[2], (E, LQ), dtype=jnp.float32) / np.sqrt(E)
        W_qk = jax.random.normal(ks[3], (LQ, H * LKV), dtype=jnp.float32) / np.sqrt(LQ)
        Wkv_d = jax.random.normal(ks[4], (E, LKV), dtype=jnp.float32) / np.sqrt(E)
        Wv_u = jax.random.normal(ks[5], (LKV, H * HD), dtype=jnp.float32) / np.sqrt(LKV)
        return {'Q': Q, 'K': K, 'Wq_d': Wq_d, 'W_qk': W_qk, 'Wkv_d': Wkv_d, 'Wv_u': Wv_u}
    _L2_xattn_all = _L2_xattn_setup()
    _L2_xattn_in = {k: v for k, v in _L2_xattn_all.items() if k in ('Wq_d', 'W_qk', 'Wkv_d', 'Wv_u')}
    del _L2_xattn_all

    def _L2_ffn_setup():
        import jax, jax.numpy as jnp
        import numpy as np

        @jax.custom_vjp
        def ste_sign(w):
            return jnp.sign(w)

        def _ste_fwd(w):
            return (jnp.sign(w), w)

        def _ste_bwd(w, g):
            mask = ((w > -1) & (w < 1)).astype(g.dtype)
            return (g * mask,)
        ste_sign.defvjp(_ste_fwd, _ste_bwd)
        key = jax.random.key(seed)
        k = jax.random.split(key, 6)
        B, S, H, O, E = (4, 256, 512, 512, 8)
        return {'x': jax.random.normal(k[0], (B, S, H), dtype=jnp.float32), 'weight': jax.random.normal(k[1], (O, H), dtype=jnp.float32) * 0.02, 'bias': jax.random.normal(k[2], (O,), dtype=jnp.float32) * 0.02, 'gate_w': jax.random.normal(k[3], (E, H), dtype=jnp.float32) * 0.02, 'in_channel_scale': jax.random.normal(k[4], (E, H), dtype=jnp.float32), 'out_channel_scale': jax.random.normal(k[5], (E, O), dtype=jnp.float32)}
    _L2_ffn_all = _L2_ffn_setup()
    _L2_ffn_in = {k: v for k, v in _L2_ffn_all.items() if k in ('weight', 'bias', 'gate_w', 'in_channel_scale', 'out_channel_scale')}
    del _L2_ffn_all

    def _L3_xattn_setup():
        import jax, jax.numpy as jnp
        import numpy as np
        B, S, E = (2, 256, 512)
        H, KVH, D = (32, 8, 128)
        GROUPS = H // KVH
        MAX_POS = 512
        ROPE_THETA = 10000.0

        def _rope_tables(max_pos, dim, theta):
            inv_freq = 1.0 / theta ** (jnp.arange(0, dim, 2, dtype=jnp.float32) / dim)
            t = jnp.arange(max_pos, dtype=jnp.float32)
            freqs = jnp.einsum('i,j->ij', t, inv_freq)
            emb = jnp.concatenate([freqs, freqs], axis=-1)
            return (jnp.cos(emb), jnp.sin(emb))

        def _rotate_half(x):
            x1, x2 = (x[..., :x.shape[-1] // 2], x[..., x.shape[-1] // 2:])
            return jnp.concatenate([-x2, x1], axis=-1)
        key = jax.random.key(seed)
        ks = jax.random.split(key, 8)
        scale_w = 1.0 / np.sqrt(E)
        query = jax.random.normal(ks[0], (B, S, E), dtype=jnp.float32)
        k_in = jax.random.normal(ks[1], (B, S, E), dtype=jnp.float32)
        v_in = jax.random.normal(ks[2], (B, S, E), dtype=jnp.float32)
        position_ids = jnp.broadcast_to(jnp.arange(S, dtype=jnp.int64), (B, S))
        src_mask = jnp.tril(jnp.ones((S, S), dtype=jnp.int32))
        src_mask = jnp.broadcast_to(src_mask, (B, S, S))
        Wq = jax.random.normal(ks[3], (E, H * D), dtype=jnp.float32) * scale_w
        Wk = jax.random.normal(ks[4], (E, KVH * D), dtype=jnp.float32) * scale_w
        Wv = jax.random.normal(ks[5], (E, KVH * D), dtype=jnp.float32) * scale_w
        Wo = jax.random.normal(ks[6], (H * D, E), dtype=jnp.float32) * scale_w
        return {'query': query, 'key': k_in, 'value': v_in, 'position_ids': position_ids, 'src_mask': src_mask, 'Wq': Wq, 'Wk': Wk, 'Wv': Wv, 'Wo': Wo}
    _L3_xattn_all = _L3_xattn_setup()
    _L3_xattn_in = {k: v for k, v in _L3_xattn_all.items() if k in ('Wq', 'Wk', 'Wv', 'Wo')}
    del _L3_xattn_all

    def _L3_ffn_setup():
        import jax, jax.numpy as jnp
        import numpy as np
        LORA_R = 16
        SCALE = 16.0 / np.sqrt(16.0)
        NUM_EXPERTS = 4
        TOP_K = 2
        IN_F = 512
        OUT_F = 512
        key = jax.random.key(seed)
        k_x, k_a, k_b, k_r = jax.random.split(key, 4)
        x = jax.random.normal(k_x, (2, 256, IN_F), dtype=jnp.float32)
        A = jax.random.normal(k_a, (NUM_EXPERTS, LORA_R, IN_F), dtype=jnp.float32) * (1.0 / np.sqrt(IN_F))
        B = jax.random.normal(k_b, (NUM_EXPERTS, OUT_F, LORA_R), dtype=jnp.float32) * 0.02
        Wr = jax.random.normal(k_r, (NUM_EXPERTS, IN_F), dtype=jnp.float32) * 0.02
        return {'x': x, 'A': A, 'B': B, 'Wr': Wr}
    _L3_ffn_all = _L3_ffn_setup()
    _L3_ffn_in = {k: v for k, v in _L3_ffn_all.items() if k in ('A', 'B', 'Wr')}
    del _L3_ffn_all
    return {'x': x, 'ctx_4096': ctx_4096, 'pos_BxS2': pos_BxS2, 'mask_BxSxS2_ik0': mask_BxSxS2_ik0, 'g_xattn': g_xattn, 'g_ffn': g_ffn, 'L0_xattn_Wq': _L0_xattn_in['Wq'], 'L0_xattn_bq': _L0_xattn_in['bq'], 'L0_xattn_Wk': _L0_xattn_in['Wk'], 'L0_xattn_bk': _L0_xattn_in['bk'], 'L0_ffn_W_base': _L0_ffn_in['W_base'], 'L0_ffn_b_base': _L0_ffn_in['b_base'], 'L0_ffn_W_router': _L0_ffn_in['W_router'], 'L0_ffn_A_stack': _L0_ffn_in['A_stack'], 'L0_ffn_B_stack': _L0_ffn_in['B_stack'], 'L1_xattn_Wq': _L1_xattn_in['Wq'], 'L1_xattn_bq': _L1_xattn_in['bq'], 'L1_xattn_Wk': _L1_xattn_in['Wk'], 'L1_xattn_bk': _L1_xattn_in['bk'], 'L1_xattn_Wv': _L1_xattn_in['Wv'], 'L1_xattn_bv': _L1_xattn_in['bv'], 'L1_xattn_Wo': _L1_xattn_in['Wo'], 'L1_xattn_bo': _L1_xattn_in['bo'], 'L1_ffn_base_W': _L1_ffn_in['base_W'], 'L1_ffn_base_b': _L1_ffn_in['base_b'], 'L1_ffn_router_W': _L1_ffn_in['router_W'], 'L1_ffn_router_b': _L1_ffn_in['router_b'], 'L1_ffn_A': _L1_ffn_in['A'], 'L1_ffn_B': _L1_ffn_in['B'], 'L1_ffn_expert_map': _L1_ffn_in['expert_map'], 'L2_xattn_Wq_d': _L2_xattn_in['Wq_d'], 'L2_xattn_W_qk': _L2_xattn_in['W_qk'], 'L2_xattn_Wkv_d': _L2_xattn_in['Wkv_d'], 'L2_xattn_Wv_u': _L2_xattn_in['Wv_u'], 'L2_ffn_weight': _L2_ffn_in['weight'], 'L2_ffn_bias': _L2_ffn_in['bias'], 'L2_ffn_gate_w': _L2_ffn_in['gate_w'], 'L2_ffn_in_channel_scale': _L2_ffn_in['in_channel_scale'], 'L2_ffn_out_channel_scale': _L2_ffn_in['out_channel_scale'], 'L3_xattn_Wq': _L3_xattn_in['Wq'], 'L3_xattn_Wk': _L3_xattn_in['Wk'], 'L3_xattn_Wv': _L3_xattn_in['Wv'], 'L3_xattn_Wo': _L3_xattn_in['Wo'], 'L3_ffn_A': _L3_ffn_in['A'], 'L3_ffn_B': _L3_ffn_in['B'], 'L3_ffn_Wr': _L3_ffn_in['Wr']}

def reference(x, ctx_4096, pos_BxS2, mask_BxSxS2_ik0, g_xattn, g_ffn, L0_xattn_Wq, L0_xattn_bq, L0_xattn_Wk, L0_xattn_bk, L0_ffn_W_base, L0_ffn_b_base, L0_ffn_W_router, L0_ffn_A_stack, L0_ffn_B_stack, L1_xattn_Wq, L1_xattn_bq, L1_xattn_Wk, L1_xattn_bk, L1_xattn_Wv, L1_xattn_bv, L1_xattn_Wo, L1_xattn_bo, L1_ffn_base_W, L1_ffn_base_b, L1_ffn_router_W, L1_ffn_router_b, L1_ffn_A, L1_ffn_B, L1_ffn_expert_map, L2_xattn_Wq_d, L2_xattn_W_qk, L2_xattn_Wkv_d, L2_xattn_Wv_u, L2_ffn_weight, L2_ffn_bias, L2_ffn_gate_w, L2_ffn_in_channel_scale, L2_ffn_out_channel_scale, L3_xattn_Wq, L3_xattn_Wk, L3_xattn_Wv, L3_xattn_Wo, L3_ffn_A, L3_ffn_B, L3_ffn_Wr):
    import jax
    import jax.numpy as jnp

    def _L0_xattn_ref(text, features, Wq, bq, Wk, bk):
        import jax, jax.numpy as jnp
        import numpy as np
        TEXT_DIM = 512
        FEATURE_DIM = 512

        def _xavier_uniform(key, shape):
            fan_in, fan_out = (shape[1], shape[0])
            limit = float(np.sqrt(6.0 / (fan_in + fan_out)))
            return jax.random.uniform(key, shape, jnp.float32, -limit, limit)
        Q = jnp.einsum('btx,dx->btd', text, Wq) + bq
        K = jnp.einsum('bpx,dx->bpd', features, Wk) + bk
        scale = 1.0 / jnp.sqrt(jnp.asarray(K.shape[-1], K.dtype))
        scores = jnp.einsum('btd,bpd->btp', Q, K) * scale
        attn = jax.nn.softmax(scores, axis=-1)
        attended = jnp.einsum('btp,bpd->btd', attn, features)
        return attended

    def _L0_ffn_ref(x, W_base, b_base, W_router, A_stack, B_stack):
        import jax, jax.numpy as jnp
        import numpy as np
        D_IN = 512
        D_OUT = 512
        RANK = 16
        NUM_EXPERTS = 8
        TOP_K = 2
        SCALING = 32.0 / RANK
        orig_shape = x.shape
        xf = x.reshape(-1, D_IN)
        logits = xf @ W_router.T
        probs = jax.nn.softmax(logits, axis=-1)
        topk_p, topk_i = jax.lax.top_k(probs, TOP_K)
        topk_p = topk_p / jnp.sum(topk_p, axis=-1, keepdims=True)
        combine = jnp.sum(jax.nn.one_hot(topk_i, NUM_EXPERTS, dtype=xf.dtype) * topk_p[..., None], axis=1)
        h = jnp.einsum('nd,erd->ner', xf, A_stack)
        h = h * combine[..., None]
        lora_out = jnp.einsum('ner,eor->no', h, B_stack) * SCALING
        base_out = xf @ W_base.T + b_base
        out = base_out + lora_out
        return out.reshape(orig_shape[:-1] + (D_OUT,))

    def _L1_xattn_ref(x, cond, Wq, bq, Wk, bk, Wv, bv, Wo, bo):
        import jax, jax.numpy as jnp
        import numpy as np
        HEADS = 8
        WINDOW = 16

        def _pointwise(W, b, t):
            return jnp.einsum('oc,bct->bot', W, t) + b[None, :, None]
        B, C, T = x.shape
        H, W = (HEADS, WINDOW)
        hd = C // H
        scale = hd ** (-0.5)
        pad_left = W // 2
        pad_right = W - pad_left - 1
        q = _pointwise(Wq, bq, x)
        k = _pointwise(Wk, bk, cond)
        v = _pointwise(Wv, bv, cond)
        k = jnp.pad(k, ((0, 0), (0, 0), (pad_left, pad_right)))
        v = jnp.pad(v, ((0, 0), (0, 0), (pad_left, pad_right)))
        idx = jnp.arange(T)[:, None] + jnp.arange(W)[None, :]
        k_win = k[:, :, idx].reshape(B, H, hd, T, W)
        v_win = v[:, :, idx].reshape(B, H, hd, T, W)
        qh = q.reshape(B, H, hd, T)
        dots = jnp.einsum('bhdt,bhdtw->bhtw', qh, k_win) * scale
        attn = jax.nn.softmax(dots, axis=-1)
        out = jnp.einsum('bhtw,bhdtw->bhdt', attn, v_win)
        out = out.reshape(B, C, T)
        return _pointwise(Wo, bo, out)

    def _L1_ffn_ref(x, base_W, base_b, router_W, router_b, A, B, expert_map):
        import jax, jax.numpy as jnp
        import numpy as np
        SCALING = 32.0 / 16.0
        E = A.shape[0]
        base_out = jnp.einsum('btd,od->bto', x, base_W) + base_b
        logits = jnp.einsum('btd,nd->btn', x, router_W) + router_b
        probs = jax.nn.softmax(logits, axis=-1)
        topk_p, topk_i = jax.lax.top_k(probs, E)
        mapped = expert_map[topk_i]
        onehot = (mapped[..., None] == jnp.arange(E)).astype(x.dtype)
        w = jnp.einsum('btk,btke->bte', topk_p, onehot)
        h = jnp.einsum('btd,erd->bter', x, A)
        lora = jnp.einsum('bter,eor->bto', h * w[..., None], B) * SCALING
        return base_out + lora

    def _L2_xattn_ref(Q, K, Wq_d, W_qk, Wkv_d, Wv_u):
        import jax, jax.numpy as jnp
        import numpy as np
        B, N, NKV = (2, 256, 256)
        E = 512
        H = 16
        HD = E // H
        LQ = E // 8
        LKV = E // 16
        b, n, _ = Q.shape
        nkv = K.shape[1]
        C_q = Q @ Wq_d
        C_kv = K @ Wkv_d
        CqWqk = (C_q @ W_qk).reshape(b, n, H, LKV)
        scores = jnp.einsum('bnhl,bkl->bhnk', CqWqk, C_kv) / jnp.sqrt(jnp.asarray(LKV, dtype=Q.dtype))
        attn = jax.nn.softmax(scores, axis=-1)
        V_up = (C_kv @ Wv_u).reshape(b, nkv, H, HD)
        out = jnp.einsum('bhnk,bkhd->bnhd', attn, V_up)
        return out.reshape(b, n, H * HD)

    def _L2_ffn_ref(x, weight, bias, gate_w, in_channel_scale, out_channel_scale):
        import jax, jax.numpy as jnp
        import numpy as np

        @jax.custom_vjp
        def ste_sign(w):
            return jnp.sign(w)

        def _ste_fwd(w):
            return (jnp.sign(w), w)

        def _ste_bwd(w, g):
            mask = ((w > -1) & (w < 1)).astype(g.dtype)
            return (g * mask,)
        ste_sign.defvjp(_ste_fwd, _ste_bwd)
        B, S, H = x.shape
        xf = x.reshape(-1, H)
        router_logits = xf @ gate_w.T
        routing = jax.nn.softmax(router_logits.astype(jnp.float32), axis=1).astype(x.dtype)
        in_scale = routing @ in_channel_scale
        out_scale = routing @ out_channel_scale
        wb = ste_sign(weight)
        out = xf * in_scale @ wb.T * out_scale + bias
        return out.reshape(B, S, -1)

    def _L3_xattn_ref(query, key, value, position_ids, src_mask, Wq, Wk, Wv, Wo):
        import jax, jax.numpy as jnp
        import numpy as np
        B, S, E = (2, 256, 512)
        H, KVH, D = (32, 8, 128)
        GROUPS = H // KVH
        MAX_POS = 512
        ROPE_THETA = 10000.0

        def _rope_tables(max_pos, dim, theta):
            inv_freq = 1.0 / theta ** (jnp.arange(0, dim, 2, dtype=jnp.float32) / dim)
            t = jnp.arange(max_pos, dtype=jnp.float32)
            freqs = jnp.einsum('i,j->ij', t, inv_freq)
            emb = jnp.concatenate([freqs, freqs], axis=-1)
            return (jnp.cos(emb), jnp.sin(emb))

        def _rotate_half(x):
            x1, x2 = (x[..., :x.shape[-1] // 2], x[..., x.shape[-1] // 2:])
            return jnp.concatenate([-x2, x1], axis=-1)
        nb, q_len, _ = query.shape
        q = (query @ Wq).reshape(nb, q_len, H, D).transpose(0, 2, 1, 3)
        k = (key @ Wk).reshape(nb, q_len, KVH, D).transpose(0, 2, 1, 3)
        v = (value @ Wv).reshape(nb, q_len, KVH, D).transpose(0, 2, 1, 3)
        cos_t, sin_t = _rope_tables(MAX_POS, D, ROPE_THETA)
        cos = cos_t[position_ids][:, None]
        sin = sin_t[position_ids][:, None]
        q = q * cos + _rotate_half(q) * sin
        k = k * cos + _rotate_half(k) * sin
        k = jnp.repeat(k, GROUPS, axis=1)
        v = jnp.repeat(v, GROUPS, axis=1)
        scores = jnp.einsum('bhqd,bhkd->bhqk', q, k) / jnp.sqrt(jnp.float32(D))
        mask = src_mask[:, None]
        scores = jnp.where(mask == 0, jnp.float32(-1000000000.0), scores)
        attn = jax.nn.softmax(scores, axis=-1)
        x = jnp.einsum('bhqk,bhkd->bhqd', attn, v)
        x = x.transpose(0, 2, 1, 3).reshape(nb, q_len, H * D)
        return x @ Wo

    def _L3_ffn_ref(x, A, B, Wr):
        import jax, jax.numpy as jnp
        import numpy as np
        LORA_R = 16
        SCALE = 16.0 / np.sqrt(16.0)
        NUM_EXPERTS = 4
        TOP_K = 2
        IN_F = 512
        OUT_F = 512
        orig_shape = x.shape
        flat = x.reshape(-1, orig_shape[-1])
        logits = flat @ Wr.T
        topk_vals, topk_idx = jax.lax.top_k(logits, TOP_K)
        T = flat.shape[0]
        neg_inf = jnp.finfo(logits.dtype).min
        sparse = jnp.full_like(logits, neg_inf)
        rows = jnp.arange(T)[:, None]
        sparse = sparse.at[rows, topk_idx].set(topk_vals)
        gates = jax.nn.softmax(sparse, axis=-1)
        mid = jnp.einsum('tf,erf->ter', flat, A)
        all_deltas = jnp.einsum('ter,eor->teo', mid, B) * SCALE
        delta = jnp.sum(gates[:, :, None] * all_deltas, axis=1)
        return delta.reshape(*orig_shape[:-1], -1)
    x = x + jnp.tanh(g_xattn[0]) * _L0_xattn_ref(_layernorm(x, axis=-1), ctx_4096, L0_xattn_Wq, L0_xattn_bq, L0_xattn_Wk, L0_xattn_bk)
    x = x + jnp.tanh(g_ffn[0]) * _L0_ffn_ref(_layernorm(x, axis=-1), L0_ffn_W_base, L0_ffn_b_base, L0_ffn_W_router, L0_ffn_A_stack, L0_ffn_B_stack)
    x = x + jnp.tanh(g_xattn[1]) * _L1_xattn_ref(_layernorm(x, axis=-1), ctx_4096, L1_xattn_Wq, L1_xattn_bq, L1_xattn_Wk, L1_xattn_bk, L1_xattn_Wv, L1_xattn_bv, L1_xattn_Wo, L1_xattn_bo)
    x = x + jnp.tanh(g_ffn[1]) * _L1_ffn_ref(_layernorm(x, axis=-1), L1_ffn_base_W, L1_ffn_base_b, L1_ffn_router_W, L1_ffn_router_b, L1_ffn_A, L1_ffn_B, L1_ffn_expert_map)
    x = x + jnp.tanh(g_xattn[2]) * _L2_xattn_ref(_layernorm(x, axis=-1), ctx_4096, L2_xattn_Wq_d, L2_xattn_W_qk, L2_xattn_Wkv_d, L2_xattn_Wv_u)
    x = x + jnp.tanh(g_ffn[2]) * _L2_ffn_ref(_layernorm(x, axis=-1), L2_ffn_weight, L2_ffn_bias, L2_ffn_gate_w, L2_ffn_in_channel_scale, L2_ffn_out_channel_scale)
    x = x + jnp.tanh(g_xattn[3]) * _L3_xattn_ref(_layernorm(x, axis=-1), ctx_4096, ctx_4096, pos_BxS2, mask_BxSxS2_ik0, L3_xattn_Wq, L3_xattn_Wk, L3_xattn_Wv, L3_xattn_Wo)
    x = x + jnp.tanh(g_ffn[3]) * _L3_ffn_ref(_layernorm(x, axis=-1), L3_ffn_A, L3_ffn_B, L3_ffn_Wr)
    return x

_drawn_inputs = setup_inputs


def setup_inputs(seed=0):
    import zlib

    import numpy as np

    out = dict(_drawn_inputs(seed))
    spreads = {'L0_xattn_bq': (0.0, 0.38),
     'L0_xattn_bk': (0.0, 2.0),
     'L1_xattn_bq': (0.0, 0.8),
     'L1_xattn_bk': (0.0, 2.0),
     'L1_xattn_bv': (0.0, 0.8),
     'L1_xattn_bo': (0.0, 0.331)}
    factors = {'L0_ffn_b_base': 6.946,
     'L1_xattn_Wq': 8.0,
     'L1_xattn_Wk': 8.0,
     'L1_xattn_Wv': 6.775,
     'L1_xattn_Wo': 5.831,
     'L1_ffn_base_b': 8.0,
     'L1_ffn_router_b': 5.99,
     'L2_ffn_bias': 8.0}
    for name, (base, spread) in spreads.items():
        noise = np.random.default_rng([zlib.crc32(name.encode()), seed]).standard_normal(out[name].shape)
        drawn = base * np.exp(spread * noise) if base else spread * noise
        out[name] = jnp.asarray(drawn.astype(out[name].dtype))
    for name, factor in factors.items():
        out[name] = (out[name] * factor).astype(out[name].dtype)
    return out
```

```python
from contextlib import ExitStack, contextmanager

import numpy as np

import concourse.bass as bass
from concourse import mybir

F32 = mybir.dt.float32
I32 = mybir.dt.int32
HALF = mybir.dt.bfloat16
BF16 = mybir.dt.bfloat16
ALU = mybir.AluOpType
ACT = mybir.ActivationFunctionType
AX = mybir.AxisListType

P = 128
D = 512
C = D // P
SEQ = 64
BATCH = 32
TOKENS = BATCH * SEQ
TILES = TOKENS // P
QUAD = 4
TURNS = TILES // QUAD
EPS = 1e-5

R0, R1, R3 = 8, 15, 4
E01, RANK, E3 = 8, 16, 4
LORA, LORA3 = E01 * RANK, E3 * RANK

WIN, CH, TC = 16, 8, 8
TP = D // TC
PADDED = 8 + D + 8
HALO = TP + WIN

H2, L2K = 16, 32
KV, GROUP, HD = 8, 4, 128
POSITIONS = 512
MASKED = -float(2.0 ** 100)
NEVER = 4.0


def new_semaphore(nc, w, name):
    handle = w["stack"].enter_context(nc.semaphore(name))
    w["semaphores"].append(handle)
    return handle


@contextmanager
def stage(nc, w):
    with ExitStack() as stack:
        w["stack"], w["semaphores"] = stack, []
        yield
        for handle in w["semaphores"]:
            nc.gpsimd.sem_clear(handle)
        nc.all_engine_barrier()


def prepare_weights(nc, io, w):
    with ExitStack() as ctx:
        def sb(name, shape, dt=F32):
            return ctx.enter_context(nc.sbuf_tensor("prep_" + name, shape, dt))

        def sem(name):
            return new_semaphore(nc, w, "prep_" + name)

        raw = {}
        for name, cols in (("W0", D), ("W1", D), ("W2", D), ("R0", R0 + LORA), ("R1", R1 + LORA),
                           ("Wqd", 64), ("Wkv", P), ("R3", R3 + LORA3)):
            raw[name] = sb(name, [P, C, cols])
        wq, wk = sb("Wq", [P, C, D]), sb("Wk", [P, C, D])
        bq, bk = sb("bq", [P, C]), sb("bk", [P, C])
        gates_raw = sb("gates", [P, 8])
        bias_raw = sb("bias", [P, 3, D])
        emap, emap_f = sb("emap", [P, R1], I32), sb("emap_f", [P, R1])
        negative = sb("negative", [P, C, D])
        eight = sb("eight", [P, E01])
        ps = ctx.enter_context(nc.psum_tensor("prep_ps", [P, 8, D], F32))
        loaded, zeroed, made, product_ready = sem("loaded"), sem("zeroed"), sem("made"), sem("product_ready")
        split_high, pool_step, gate_ready = sem("split_high"), sem("pool_step"), sem("gate_ready")
        direct, folded = sem("direct"), sem("folded")

        RAW = [("W0", "W0"), ("R0", "R0"), ("W1", "W1"), ("R1", "R1"), ("Wqd", "Wqd"), ("Wkv", "Wkv"),
               ("R3", "R3")]
        FIRST = 5 * 16
        block = ctx.enter_context(nc.Block())

        @block.sync
        def _(sp):
            sp.dma_start(wq[:, :, :], io["L0_Wq"].rearrange("(c p) n -> p c n", p=P)).then_inc(loaded, 16)
            sp.dma_start(wk[:, :, :], io["L0_Wk"].rearrange("(c p) n -> p c n", p=P)).then_inc(loaded, 16)
            sp.dma_start(bq[:, :], io["L0_bq"]).then_inc(loaded, 16)
            sp.dma_start(bk[:, :], io["L0_bk"]).then_inc(loaded, 16)
            sp.dma_start(gates_raw[:, :], io["gates"].partition_broadcast(P)).then_inc(loaded, 16)
            sp.wait_ge(loaded, FIRST)
            n = FIRST
            for dst, src in RAW + [("W2", "W2")]:
                sp.dma_start(raw[dst][:, :, :], io[src].rearrange("(c p) n -> p c n", p=P)).then_inc(loaded, 16)
                n += 16
                sp.wait_ge(loaded, n)
            for k, name in enumerate(("b0", "b1", "b2")):
                sp.dma_start(bias_raw[:, k, :], io[name].partition_broadcast(P)).then_inc(loaded, 16)
            sp.dma_start(emap[:, :], io["emap"].partition_broadcast(P)).then_inc(loaded, 16)
            for name in ("B0", "B1", "Wqk", "Wvu", "ics", "ocs", "B3"):
                sp.dma_start(w[name][:, :], io[name]).then_inc(direct, 16)
            sp.dma_start(w["gate2"][:, :, :], io["gate2"].rearrange("(c p) n -> p c n", p=P)).then_inc(direct, 16)
            sp.dma_start(w["rb1"][:, :], io["rb1"].partition_broadcast(P)).then_inc(direct, 16)
            sp.wait_ge(zeroed, 1)
            for k in range(4):
                for b in range(2):
                    sp.dma_start(w["L1W"][SEQ * b:SEQ * b + SEQ, k, SEQ * b:SEQ * b + SEQ],
                                 io["L1W"][k]).then_inc(direct, 16)
                    sp.dma_start(w["L1b"][SEQ * b:SEQ * b + SEQ, k:k + 1], io["L1b"][k]).then_inc(direct, 16)
            sp.wait_ge(direct, 16 * (9 + 16))

        @block.gpsimd
        def _(pool):
            st = Steps(pool, pool_step, 12, 0)
            st.link(pool.memset(w["ident"][:, :], 0.0))
            st.link(pool.memset(w["bdmask"][:, :], MASKED))
            st.link(pool.memset(w["power"][:, :], -0.5))
            st.link(pool.memset(w["eps"][:, :], EPS))
            st.link(pool.memset(w["quarter"][:, :], 1.0))
            st.link(pool.iota(w["expert_id"][:, :, :], pattern=[[1, E01], [0, R1]], base=0, channel_multiplier=0,
                              allow_small_or_imprecise_dtypes=True))
            st.link(pool.affine_select(out=w["ident"][:, :], in_=w["ident"][:, :], compare_op=ALU.not_equal,
                                       fill=1.0, base=0, pattern=[[-1, P]], channel_multiplier=1))
            for b in range(2):
                rows = w["bdmask"][SEQ * b:SEQ * b + SEQ, SEQ * b:SEQ * b + SEQ]
                st.link(pool.memset(rows, 0.0))
            st.link(pool.affine_select(out=w["quarter"][:, :], in_=w["quarter"][:, :], compare_op=ALU.is_ge,
                                       fill=0.0, base=0, pattern=[[-L2K, 4]], channel_multiplier=1))
            st.link(pool.affine_select(out=w["quarter"][:, :], in_=w["quarter"][:, :], compare_op=ALU.is_ge,
                                       fill=0.0, base=L2K - 1, pattern=[[L2K, 4]], channel_multiplier=-1))
            st.link(pool.tensor_copy(w["identh"][:, :], w["ident"][:, :]))
            st.close()

        @block.tensor
        def _(pe):
            pe.wait_ge(loaded, FIRST)
            for m in range(C):
                for c in range(C):
                    last = pe.matmul(ps[:, m, :], wq[:, c, m * P:(m + 1) * P], wk[:, c, :],
                                     start=(c == 0), stop=(c == C - 1))
                last.then_inc(product_ready, 1)
            for m in range(C):
                for c in range(C):
                    pe.matmul(ps[:, 4, m:m + 1], wk[:, c, m * P:(m + 1) * P], bq[:, c:c + 1],
                              start=(c == 0), stop=(c == C - 1))
            for m in range(C):
                for c in range(C):
                    pe.matmul(ps[:, 5, m:m + 1], wq[:, c, m * P:(m + 1) * P], bk[:, c:c + 1],
                              start=(c == 0), stop=(c == C - 1))
            for c in range(C):
                last = pe.matmul(ps[:, 6, 0:1], bq[:, c:c + 1].to_broadcast([P, P]), bk[:, c:c + 1],
                                 start=(c == 0), stop=(c == C - 1))
            last.then_inc(product_ready, 1)

        @block.scalar
        def _(act):
            act.wait_ge(loaded, FIRST)
            act.activation(w["gates"][:, :], gates_raw[:, :], ACT.Tanh).then_inc(gate_ready, 1)
            for m in range(C):
                act.wait_ge(product_ready, m + 1)
                act.activation(w["Mh"][:, m, :], ps[:, m, :], ACT.Copy).then_inc(split_high, 1)
            act.wait_ge(product_ready, C + 1)
            act.activation(w["ch"][:, :], ps[:, 5, 0:C], ACT.Copy).then_inc(split_high, 1)
            for k, (name, _) in enumerate(RAW):
                act.wait_ge(loaded, FIRST + 16 * (k + 1))
                act.activation(w[name + "h"][:, :, :], raw[name][:, :, :], ACT.Copy).then_inc(split_high, 1)

        @block.vector
        def _(dve):
            dve.memset(w["L1W"][:, :, :], 0.0).then_inc(zeroed, 1)
            for m in range(C):
                dve.wait_ge(split_high, m + 1)
                dve.tensor_tensor(w["Ml"][:, m, :], ps[:, m, :], w["Mh"][:, m, :], ALU.subtract)
            dve.wait_ge(split_high, C + 1)
            dve.tensor_tensor(w["cl"][:, :], ps[:, 5, 0:C], w["ch"][:, :], ALU.subtract)
            dve.tensor_copy(w["r"][:, :], ps[:, 4, 0:C])
            dve.tensor_copy(w["s"][:, :], ps[:, 6, 0:1])
            for k, (name, _) in enumerate(RAW):
                dve.wait_ge(split_high, C + 2 + k)
                dve.tensor_tensor(w[name + "l"][:, :, :], raw[name][:, :, :], w[name + "h"][:, :, :], ALU.subtract)
            dve.wait_ge(loaded, FIRST + 16 * (len(RAW) + 1))
            dve.tensor_scalar(negative[:, :, :], raw["W2"][:, :, :], 0.0, None, ALU.is_lt).then_inc(made, 1)
            dve.wait_ge(made, 1)
            dve.scalar_tensor_tensor(out=w["sign2"][:, :, :], in0=raw["W2"][:, :, :], scalar=0.0,
                                     in1=negative[:, :, :], op0=ALU.is_gt, op1=ALU.subtract)
            dve.wait_ge(gate_ready, 1)
            dve.wait_ge(loaded, FIRST + 16 * (len(RAW) + 5))
            for k in range(3):
                dve.tensor_scalar(w["gbias"][:, k, :], bias_raw[:, k, :], w["gates"][:, 4 + k:5 + k], None,
                                  ALU.mult)
            dve.tensor_copy(emap_f[:, :], emap[:, :]).then_inc(made, 1)
            dve.wait_ge(made, 2)
            dve.wait_ge(pool_step, 6)
            dve.tensor_tensor(w["route_to"][:, :, :], w["expert_id"][:, :, :],
                              emap_f[:, :].unsqueeze(1).to_broadcast([P, E01, R1]), ALU.is_equal)


class Banks:

    def __init__(self, nc, ctx, w, prefix, plan, before=()):
        used = sorted({bank for _, bank in plan})
        self.filled = {b: new_semaphore(nc, w, f"{prefix}_filled{b}") for b in used}
        self.drained = {b: new_semaphore(nc, w, f"{prefix}_drained{b}") for b in used}
        self.ps = ctx.enter_context(nc.psum_tensor(f"{prefix}_ps", [P, 8, D], F32))
        self.at, self.uses = {}, [0] * 8
        self.before = [0] * 8
        for step, bank in before:
            self.at[step] = (bank, self.before[bank])
            self.before[bank] += 1
        for step, bank in plan:
            self.at[step] = (bank, self.before[bank] + self.uses[bank])
            self.uses[bank] += 1

    def bank(self, *step):
        return self.ps[:, self.at[step][0], :]

    def wait_free(self, eng, turn, *step):
        b, k = self.at[step]
        eng.wait_ge(self.drained[b], turn * self.uses[b] + k)

    def wait_filled(self, eng, turn, *step):
        b, k = self.at[step]
        eng.wait_ge(self.filled[b], turn * self.uses[b] + (k + 1))

    def wait_drained(self, eng, turn, *step):
        b, k = self.at[step]
        eng.wait_ge(self.drained[b], turn * self.uses[b] + (k + 1))

    def wait_all_drained(self, eng, turn, b):
        eng.wait_ge(self.drained[b], turn * self.uses[b] + self.before[b])

    def wait_all_filled(self, eng, turn, b):
        eng.wait_ge(self.filled[b], turn * self.uses[b] + self.before[b])

    def fill(self, ins, *step):
        ins.then_inc(self.filled[self.at[step][0]], 1)

    def drain(self, ins, *step):
        ins.then_inc(self.drained[self.at[step][0]], 1)


class Signal:

    def __init__(self, nc, w, name, per_turn, by=1):
        self.sem, self.per_turn, self.by = new_semaphore(nc, w, name), per_turn, by

    def send(self, ins):
        ins.then_inc(self.sem, self.by)

    def wait(self, eng, turn, k):
        eng.wait_ge(self.sem, turn * (self.per_turn * self.by) + (k + 1) * self.by)


class Steps:

    def __init__(self, eng, sem, per_turn, turn):
        self.eng, self.sem, self.per_turn, self.turn, self.n = eng, sem, per_turn, turn, 0

    def step(self, ins):
        self.n += 1
        ins.then_inc(self.sem, 1)
        return self.n

    def after(self, n, eng=None):
        (eng or self.eng).wait_ge(self.sem, self.turn * self.per_turn + n)

    def link(self, ins):
        self.after(self.step(ins))

    def close(self):
        assert self.n == self.per_turn, ("steps of a turn", self.n)


def three(pe, out, lh, ll, rh, rl, first=True, last=True):
    n = len(lh)
    for c in range(n):
        pe.matmul(out, lh[c], rh[c], start=(first and c == 0), stop=False)
        pe.matmul(out, lh[c], rl[c], start=False, stop=False)
        ins = pe.matmul(out, ll[c], rh[c], start=False, stop=(last and c == n - 1))
    return ins


class Apart:

    def __init__(self, eng, once, n):
        self.eng, self.once, self.n = eng, once, n

    def wait_ge(self, sem, value):
        with self.eng.register() as held:
            self.eng.reg_alu(held, value, 0, ALU.max)
            self.eng.wait_ge(self.once, self.n)
            self.eng.wait_ge(sem, held)


DVE_STEPS, LAST_STEPS, FFN_STEPS = 152, 32, 36


def early_layers(nc, io, w):
    plan = []
    for j in range(QUAD):
        plan.append((("turn", 0, j), j % 2))
    for j in range(QUAD):
        plan.append((("proj0", j), 2 + j % 2))
    for j in range(QUAD):
        plan.append((("score0", j), j % 2))
    for j in range(QUAD):
        plan.append((("prob0", j), 2 + j % 2))
        plan.append((("out0", j), 4 + j))
    for f, layer in ((0, 1), (1, 3)):
        if f == 1:
            for j in range(QUAD):
                plan += [(("q1", j), 0), (("k1", j), 1), (("v1", j), 2)]
            for j in range(QUAD):
                plan += [(("dot1", j, 0), 4 + 2 * (j % 2)), (("dot1", j, 1), 5 + 2 * (j % 2)), (("out1", j), 3)]
        for j in range(QUAD):
            plan.append((("turn", layer, j), j % 2))
        for j in range(QUAD):
            plan += [(("route", f, j), 2 + j % 2), (("base", f, j), 4 + j)]
        for j in range(QUAD):
            plan.append((("hturn", f, j), j % 2))
    for j in range(QUAD):
        plan.append((("turn", 4, j), j % 2))
    for j in range(QUAD + 1):
        if j < QUAD:
            plan += [(("low2", j), 2), (("qup2", j), 3), (("vup2", j), 4)]
            plan += [(("score2", j, 0), 6), (("score2", j, 1), 7)]
        if j >= 1:
            plan += [(("prob2", j - 1, 0), 0), (("prob2", j - 1, 1), 1)]
            plan += [(("out2", j - 1, 0), 5), (("out2", j - 1, 1), 4)]
    for j in range(QUAD):
        plan.append((("turn", 5, j), j % 2))
    for j in range(QUAD):
        plan.append((("gate2", j), 2 + j % 2))
    for j in range(QUAD):
        plan += [(("gturn", j), j % 2), (("scale_in", j), 4 + j % 2), (("scale_out", j), 6 + j % 2)]
    for j in range(QUAD):
        plan.append((("sign2", j), 2 + j % 2))

    with ExitStack() as ctx:
        def sb(name, shape, dt=F32, stack=ctx):
            return stack.enter_context(nc.sbuf_tensor("early_" + name, shape, dt))

        def signal(name, per_turn, by=1):
            return Signal(nc, w, "early_" + name, per_turn, by)

        xin, xq, xn = sb("xin", [P, QUAD, D]), sb("xq", [P, QUAD, D]), sb("xn", [P, QUAD, D])
        xTh, xTl = sb("xTh", [P, QUAD, C, P], HALF), sb("xTl", [P, QUAD, C, P], HALF)
        ctxt = sb("ctxt", [P, QUAD, D])
        cT = sb("cT", [P, QUAD, C, P])
        cTh, cTl = sb("cTh", [P, QUAD, C, P], HALF), sb("cTl", [P, QUAD, C, P], HALF)
        stats, mv, rstd = sb("stats", [P, QUAD, 6]), sb("mv", [P, QUAD, 2]), sb("rstd", [P, QUAD])
        vare = sb("vare", [P, QUAD])
        u, sm, pr, prT = sb("u", [P, QUAD]), sb("sm", [P, QUAD, P]), sb("pr", [P, QUAD, P]), sb("prT", [P, QUAD, P])
        nmax, tot, rec = sb("nmax", [P, QUAD]), sb("tot", [P, QUAD]), sb("rec", [P, QUAD])
        rh = sb("rh", [P, QUAD, R1 + LORA])
        rkeep, rsel = sb("rkeep", [P, QUAD, 16]), sb("rsel", [P, QUAD, 16])
        e0, e1, e2 = sb("e0", [P, QUAD, 14]), sb("e1", [P, QUAD, R1]), sb("e2", [P, QUAD, E01])
        top8, pick0 = sb("top8", [P, QUAD, 8]), sb("pick0", [P, QUAD, 8])
        rmix = sb("rmix", [P, QUAD, E01, R1])
        comb = sb("comb", [P, QUAD, E01])
        hs, hsT = sb("hs", [P, QUAD, LORA]), sb("hsT", [P, QUAD, P])
        kp, vp = sb("kp", [P, 2, PADDED]), sb("vp", [P, 2, PADDED])
        with ExitStack() as mine:
            qs = sb("qs", [P, 2, D], stack=mine)
            qL = sb("qL", [P, 2, CH, TP], stack=mine)
            kL, vL = sb("kL", [P, 2, CH, HALO], stack=mine), sb("vL", [P, 2, CH, HALO], stack=mine)
            prod = [sb(f"prod{h}", [P, CH, TP // 2, WIN], stack=mine) for h in range(2)]
            ee, mx1 = sb("ee", [P, TP, WIN], stack=mine), sb("mx1", [P, TP], stack=mine)
            sum1, rec1 = sb("sum1", [P, TP], stack=mine), sb("rec1", [P, TP], stack=mine)
            oL, oS = sb("oL", [P, 2, CH, TP], stack=mine), sb("oS", [P, 2, D], stack=mine)
            y1 = xn
        aT = sb("aT", [P, 2, C, P])
        aTh, aTl = sb("aTh", [P, QUAD, C, P], HALF), sb("aTl", [P, QUAD, C, P], HALF)
        cqT, ckv = sb("cqT", [64, 2, P]), sb("ckv", [P, 2, 2, 4, SEQ])
        qT2, v2 = sb("qT2", [P, 2, 4, P]), sb("v2", [P, 2, 2, 256])
        s2, p2T = sb("s2", [P, 2, H2, SEQ]), sb("p2T", [P, 2, H2 // 2, P])
        mx2, sum2, rec2 = sb("mx2", [P, 2, H2]), sb("sum2", [P, 2, H2]), sb("rec2", [P, 2, H2])
        o2 = sb("o2", [P, 2, H2, 32])
        rT2, osb = sb("rT2", [E01, QUAD, P]), sb("osb", [P, QUAD, D])
        xTf = sb("xTf", [P, QUAD, C, P])
        scr_q = nc.dram_tensor("scr_q", (QUAD, TC, P, TP), F32).ap()
        scr_k = nc.dram_tensor("scr_k", (QUAD, TC, P, HALO), F32).ap()
        scr_v = nc.dram_tensor("scr_v", (QUAD, TC, P, HALO), F32).ap()
        scr_o = nc.dram_tensor("scr_o", (QUAD, P, CH * TP), F32).ap()

        banks = Banks(nc, ctx, w, "early", plan)
        x_loaded = [signal(f"x_loaded{j}", 1, 16) for j in range(QUAD)]
        ctx_loaded = [signal(f"ctx_loaded{j}", 1, 16) for j in range(QUAD)]
        cT_loaded = [signal(f"cT_loaded{j}", 1, 16) for j in range(QUAD)]
        cT_high, cT_split = signal("cT_high", QUAD), signal("cT_split", QUAD)
        stats_ready, rstd_ready, xn_ready = signal("stats_ready", 24), signal("rstd_ready", 24), signal("xn_ready", 24)
        xT_high = signal("xT_high", 16)
        aT_ready, aT_high, aT_split = signal("aT_ready", 4), signal("aT_high", 4), signal("aT_split", 4)
        sm0_ready, pr0_ready, tot0_ready = signal("sm0_ready", 4), signal("pr0_ready", 4), signal("tot0_ready", 4)
        logit_ready, expo_ready = signal("logit_ready", 12), signal("expo_ready", 12)
        xbias_ready, hs_ready = signal("xbias_ready", 12), signal("hs_ready", 8)
        qkv_written = signal("qkv_written", 4, 48)
        qkv_in = [signal(f"qkv_in{p}", 2, 48) for p in range(2)]
        prod_pool, prod_dve = signal("prod_pool", 8), signal("prod_dve", 4)
        exp1_ready, red1_done = signal("exp1_ready", 4), signal("red1_done", 4)
        oL_ready, o_written = signal("oL_ready", 4), signal("o_written", 4, 16)
        oS_in = [signal(f"oS_in{p}", 2, 16) for p in range(2)]
        y1_ready = signal("y1_ready", 4)
        cq_ready = signal("cq_ready", 4)
        exp2_ready = signal("exp2_ready", 4)
        route2_ready, rT2_ready = signal("route2_ready", 4), signal("rT2_ready", 4)
        xTf_ready, y2_ready, y2_high, y2_split = (signal("xTf_ready", 4), signal("y2_ready", 4),
                                                  signal("y2_high", 4), signal("y2_split", 4))
        x_done = signal("x_done", 4)
        stored = signal("stored", 4, 16)
        dve_step, pads = new_semaphore(nc, w, "early_dve_step"), new_semaphore(nc, w, "early_pads")
        pool_step = new_semaphore(nc, w, "early_pool_step")

        def times_q(j, half):
            q = qL[:, j % 2, :, half * (TP // 2):(half + 1) * (TP // 2)]
            return q.unsqueeze(3).to_broadcast([P, CH, TP // 2, WIN])

        def windows(t, j, half):
            a = t[:, j % 2, :, half * (TP // 2):half * (TP // 2) + WIN]
            return bass.AP(a.tensor, a.offset, [list(a.ap[0]), [HALO, CH], [1, TP // 2], [1, WIN]])

        def weights(half):
            e = ee[:, half * (TP // 2):(half + 1) * (TP // 2), :]
            return e.unsqueeze(1).to_broadcast([P, CH, TP // 2, WIN])

        block = ctx.enter_context(nc.Block())

        @block.sync
        def _(sp):
            apart = Apart(sp, pads, 4)
            def load_x(j, tile):
                x_loaded[j].send(sp.dma_start(xin[:, j, :], io["x"][bass.ts(tile, P), :]))

            def load_ctx(j, tile):
                ctx_loaded[j].send(sp.dma_start(ctxt[:, j, :], io["ctx"][bass.ts(tile, P), :]))

            def load_cT(j, tile):
                src = io["ctxT"].rearrange("(c p) n -> p c n", p=P)
                cT_loaded[j].send(sp.dma_start(cT[:, j, :, :], src[:, :, bass.ts(tile, P)]))

            def body(turn):
                for j in range(QUAD):
                    banks.wait_drained(apart, turn, "q1", j)
                    banks.wait_drained(sp, turn, "k1", j)
                    banks.wait_drained(sp, turn, "v1", j)
                    for scr, src, step in ((scr_q, qs, TP), (scr_k, kp, HALO), (scr_v, vp, HALO)):
                        s = src[:, j % 2, :]
                        windows = bass.AP(s.tensor, s.offset, [[s.ap[0][0], P], [TP, TC], [1, step]])
                        sp.dma_start(scr[j].rearrange("c p t -> p c t"), windows).then_inc(qkv_written.sem, 16)
                    qkv_written.wait(sp, turn, j)
                    if j >= 2:
                        red1_done.wait(sp, turn, j - 2)
                    for scr, dst in ((scr_q, qL), (scr_k, kL), (scr_v, vL)):
                        sp.dma_start(dst[:, j % 2, :, :].rearrange("p d t -> p (d t)"),
                                     scr[j].rearrange("c (g d) t -> (c g) (d t)", d=CH))\
                          .then_inc(qkv_in[j % 2].sem, 16)
                    if j >= 1:
                        back(turn, j - 1)
                back(turn, QUAD - 1)
                for j in range(QUAD):
                    x_done.wait(apart, turn, j)
                    stored.send(sp.dma_start(io["x_mid"][bass.ts(turn * QUAD + j, P), :], xq[:, j, :]))

            def back(turn, j):
                oL_ready.wait(sp, turn, j)
                o_written.send(sp.dma_start(scr_o[j], oL[:, j % 2, :, :].rearrange("p d t -> p (d t)")))
                o_written.wait(sp, turn, j)
                if j >= 2:
                    banks.wait_filled(sp, turn, "out1", j - 2)
                oS_in[j % 2].send(sp.dma_start(
                    oS[:, j % 2, :].rearrange("p (c t) -> p c t", c=TC),
                    scr_o[j].rearrange("(c g) (d t) -> (g d) c t", c=TC, d=CH)))

            sp.wait_ge(pads, 4)
            for j in range(QUAD):
                load_x(j, j)
                load_cT(j, j)
                load_ctx(j, j)
            with sp.Fori(0, TURNS - 1) as turn:
                for j in range(QUAD):
                    banks.wait_drained(apart, turn, "out0", j)
                    load_x(j, turn * QUAD + (QUAD + j))
                    cT_split.wait(apart, turn, j)
                    load_cT(j, turn * QUAD + (QUAD + j))
                body(turn)
                for j in range(QUAD):
                    load_ctx(j, turn * QUAD + (QUAD + j))
            body(TURNS - 1)
            sp.wait_ge(stored.sem, TURNS * QUAD * 16)

        @block.tensor
        def _(pe):
            apart = Apart(pe, pads, 4)
            ident = w["ident"][:, :]

            def chunks(t, j):
                return [t[:, j, c, :] for c in range(C)]

            def turn_tile(turn, layer, j, src=None):
                xn_ready.wait(pe, turn, 4 * layer + j)
                banks.wait_free(pe, turn, "turn", layer, j)
                out = banks.bank("turn", layer, j)
                for c in range(C):
                    last = pe.transpose(out[:, c * P:(c + 1) * P], xn[:, j, c * P:(c + 1) * P], ident)
                banks.fill(last, "turn", layer, j)

            def lora_ffn(turn, f, layer):
                nr, wname, rname, bname = ((R0, "W0", "R0", "B0"), (R1, "W1", "R1", "B1"))[f]
                for j in range(QUAD):
                    turn_tile(turn, layer, j)
                for j in range(QUAD):
                    banks.wait_drained(pe, turn, "turn", layer, j)
                    banks.wait_free(pe, turn, "route", f, j)
                    n = nr + LORA
                    last = three(pe, banks.bank("route", f, j)[:, 0:n], chunks(xTh, j), chunks(xTl, j),
                                 [w[rname + "h"][:, c, :] for c in range(C)],
                                 [w[rname + "l"][:, c, :] for c in range(C)])
                    banks.fill(last, "route", f, j)
                    banks.wait_free(pe, turn, "base", f, j)
                    three(pe, banks.bank("base", f, j), chunks(xTh, j), chunks(xTl, j),
                          [w[wname + "h"][:, c, :] for c in range(C)],
                          [w[wname + "l"][:, c, :] for c in range(C)], last=False)
                for j in range(QUAD):
                    hs_ready.wait(pe, turn, 4 * f + j)
                    banks.wait_free(pe, turn, "hturn", f, j)
                    banks.fill(pe.transpose(banks.bank("hturn", f, j)[:, 0:P], hs[:, j, :], ident), "hturn", f, j)
                for j in range(QUAD):
                    banks.wait_drained(pe, turn, "hturn", f, j)
                    banks.fill(pe.matmul(banks.bank("base", f, j), hsT[:, j, :], w[bname][:, :],
                                         start=False, stop=True), "base", f, j)

            def attention0(turn):
                for j in range(QUAD):
                    turn_tile(turn, 0, j)
                for j in range(QUAD):
                    banks.wait_drained(pe, turn, "turn", 0, j)
                    banks.wait_free(pe, turn, "proj0", j)
                    out = banks.bank("proj0", j)
                    for m in range(C):
                        last = three(pe, out[:, m * P:(m + 1) * P],
                                     [w["Mh"][:, c, m * P:(m + 1) * P] for c in range(C)],
                                     [w["Ml"][:, c, m * P:(m + 1) * P] for c in range(C)],
                                     chunks(xTh, j), chunks(xTl, j))
                    banks.fill(last, "proj0", j)
                for j in range(QUAD):
                    aT_split.wait(pe, turn, j)
                    cT_split.wait(pe, turn, j)
                    banks.wait_free(pe, turn, "score0", j)
                    out = banks.bank("score0", j)
                    three(pe, out[:, P:P + 1], chunks(xTh, j), chunks(xTl, j),
                          [w["ch"][:, c:c + 1] for c in range(C)], [w["cl"][:, c:c + 1] for c in range(C)])
                    last = three(pe, out[:, 0:P], chunks(aTh, j), chunks(aTl, j), chunks(cTh, j), chunks(cTl, j))
                    banks.fill(last, "score0", j)
                for j in range(QUAD):
                    pr0_ready.wait(pe, turn, j)
                    banks.wait_free(pe, turn, "prob0", j)
                    banks.fill(pe.transpose(banks.bank("prob0", j)[:, 0:P], pr[:, j, :], ident), "prob0", j)
                    banks.wait_drained(pe, turn, "prob0", j)
                    ctx_loaded[j].wait(pe, turn, 0)
                    banks.wait_free(pe, turn, "out0", j)
                    banks.fill(pe.matmul(banks.bank("out0", j), prT[:, j, :], ctxt[:, j, :], start=True, stop=True),
                               "out0", j)

            def attention1(turn):
                for j in range(QUAD):
                    for k, (step, src) in enumerate((("q1", xn), ("k1", ctxt), ("v1", ctxt))):
                        if k == 0:
                            xn_ready.wait(pe, turn, 8 + j)
                        banks.wait_free(pe, turn, step, j)
                        banks.fill(pe.matmul(banks.bank(step, j), w["L1W"][:, k, :], src[:, j, :],
                                             start=True, stop=True), step, j)
                for j in range(QUAD):
                    for h in range(2):
                        if h == 0:
                            prod_dve.wait(pe, turn, j)
                        else:
                            prod_pool.wait(pe, turn, 2 * j)
                        banks.wait_free(pe, turn, "dot1", j, h)
                        out = banks.bank("dot1", j, h)
                        for d in range(CH):
                            last = pe.matmul(out, ident, prod[h][:, d, :, :].rearrange("p t w -> p (t w)"),
                                             start=(d == 0), stop=(d == CH - 1))
                        banks.fill(last, "dot1", j, h)
                    if j >= 1:
                        out_proj1(turn, j - 1)
                out_proj1(turn, QUAD - 1)

            def out_proj1(turn, j):
                oS_in[j % 2].wait(pe, turn, j // 2)
                banks.wait_free(pe, turn, "out1", j)
                banks.fill(pe.matmul(banks.bank("out1", j), w["L1W"][:, 3, :], oS[:, j % 2, :],
                                     start=True, stop=True), "out1", j)

            def attention2(turn):
                for j in range(QUAD):
                    turn_tile(turn, 4, j)

                def project(j):
                    s = j % 2
                    if j == 0:
                        for jj in range(QUAD):
                            banks.wait_drained(pe, turn, "turn", 4, jj)
                    banks.wait_free(pe, turn, "low2", j)
                    out = banks.bank("low2", j)
                    three(pe, out[0:64, 0:P], [w["Wqdh"][:, c, :] for c in range(C)],
                          [w["Wqdl"][:, c, :] for c in range(C)], chunks(xTh, j), chunks(xTl, j))
                    last = three(pe, out[:, P:2 * P], [w["Wkvh"][:, c, :] for c in range(C)],
                                 [w["Wkvl"][:, c, :] for c in range(C)], chunks(cTh, j), chunks(cTl, j))
                    banks.fill(last, "low2", j)
                    cq_ready.wait(pe, turn, j)
                    banks.wait_free(pe, turn, "qup2", j)
                    for m in range(4):
                        last = pe.matmul(banks.bank("qup2", j)[:, m * P:(m + 1) * P],
                                         w["Wqk"][:, m * P:(m + 1) * P], cqT[:, s, :], start=True, stop=True)
                    banks.fill(last, "qup2", j)
                    banks.wait_drained(pe, turn, "low2", j)
                    banks.wait_free(pe, turn, "vup2", j)
                    for half in range(2):
                        for b in range(2):
                            last = pe.matmul(banks.bank("vup2", j)[SEQ * half:SEQ * half + SEQ, b * 256:(b + 1) * 256],
                                             ckv[0:32, s, b, 0, :], w["Wvu"][:, half * 256:(half + 1) * 256],
                                             start=True, stop=True)
                    banks.fill(last, "vup2", j)
                    banks.wait_drained(pe, turn, "qup2", j)
                    for half in range(2):
                        banks.wait_free(pe, turn, "score2", j, half)
                        for mm in range(2):
                            for b in range(2):
                                last = pe.matmul(
                                    banks.bank("score2", j, half)[SEQ * b:SEQ * b + SEQ, mm * 256:(mm + 1) * 256],
                                    qT2[:, s, 2 * half + mm, SEQ * b:SEQ * b + SEQ],
                                    ckv[:, s, b, :, :].rearrange("p i k -> p (i k)"), start=True, stop=True)
                        banks.fill(last, "score2", j, half)

                def attend(j):
                    s = j % 2
                    exp2_ready.wait(pe, turn, j)
                    for half in range(2):
                        banks.wait_free(pe, turn, "prob2", j, half)
                        for n in range(4):
                            hp = 4 * half + n
                            src = s2[:, s, 2 * hp:2 * hp + 2, :].rearrange("p h k -> p (h k)")
                            last = pe.transpose(banks.bank("prob2", j, half)[:, n * P:(n + 1) * P], src, ident)
                        banks.fill(last, "prob2", j, half)
                    banks.wait_drained(pe, turn, "vup2", j)
                    banks.wait_drained(pe, turn, "prob2", j, 0)
                    banks.wait_drained(pe, turn, "prob2", j, 1)
                    for half in range(2):
                        banks.wait_free(apart, turn, "out2", j, half)
                        rows = slice(SEQ * half, SEQ * half + SEQ)
                        for b in range(2):
                            for hp in range(H2 // 2):
                                last = pe.matmul(
                                    banks.bank("out2", j, half)[SEQ * b:SEQ * b + SEQ, hp * 32:(hp + 1) * 32],
                                    p2T[rows, s, hp, SEQ * b:SEQ * b + SEQ],
                                    v2[rows, s, b, hp * 32:(hp + 1) * 32], start=True, stop=True)
                        banks.fill(last, "out2", j, half)

                for j in range(QUAD + 1):
                    if j < QUAD:
                        project(j)
                    if j >= 1:
                        attend(j - 1)

            def ffn2(turn):
                for j in range(QUAD):
                    turn_tile(turn, 5, j)
                for j in range(QUAD):
                    banks.wait_drained(pe, turn, "turn", 5, j)
                    banks.wait_free(pe, turn, "gate2", j)
                    for c in range(C):
                        last = pe.matmul(banks.bank("gate2", j)[:, 0:E01], xTf[:, j, c, :], w["gate2"][:, c, :],
                                         start=(c == 0), stop=(c == C - 1))
                    banks.fill(last, "gate2", j)
                for j in range(QUAD):
                    route2_ready.wait(pe, turn, j)
                    banks.wait_free(pe, turn, "gturn", j)
                    banks.fill(pe.transpose(banks.bank("gturn", j)[0:E01, 0:P], comb[:, j, :], ident), "gturn", j)
                    banks.wait_drained(pe, turn, "gturn", j)
                    banks.wait_free(pe, turn, "scale_in", j)
                    for c in range(C):
                        last = pe.matmul(banks.bank("scale_in", j)[:, c * P:(c + 1) * P],
                                         w["ics"][:, c * P:(c + 1) * P], rT2[:, j, :], start=True, stop=True)
                    banks.fill(last, "scale_in", j)
                    banks.wait_free(pe, turn, "scale_out", j)
                    banks.fill(pe.matmul(banks.bank("scale_out", j), rT2[:, j, :], w["ocs"][:, :],
                                         start=True, stop=True), "scale_out", j)
                for j in range(QUAD):
                    y2_split.wait(pe, turn, j)
                    banks.wait_free(pe, turn, "sign2", j)
                    for c in range(C):
                        pe.matmul(banks.bank("sign2", j), xTh[:, j, c, :], w["sign2"][:, c, :],
                                  start=(c == 0), stop=False)
                        last = pe.matmul(banks.bank("sign2", j), xTl[:, j, c, :], w["sign2"][:, c, :],
                                         start=False, stop=(c == C - 1))
                    banks.fill(last, "sign2", j)

            with pe.Fori(0, TURNS) as turn:
                attention0(turn)
                lora_ffn(turn, 0, 1)
                attention1(turn)
                lora_ffn(turn, 1, 3)
                attention2(turn)
                ffn2(turn)

        @block.scalar
        def _(act):
            def high(turn, layer, n):
                for j in range(QUAD):
                    banks.wait_filled(act, turn, "turn", layer, j)
                    xT_high.send(act.activation(xTh[:, j, :, :].rearrange("p c n -> p (c n)"),
                                                banks.bank("turn", layer, j), ACT.Copy))

            def route_exp(turn, f, e, nr):
                step, n = (("route", 0), nr + LORA) if f == 0 else (("route", 1), nr + LORA) if f == 1 else (("gate2",), nr)
                for j in range(QUAD):
                    banks.wait_filled(act, turn, *step, j)
                    banks.drain(act.activation(rh[:, j, 0:n], banks.bank(*step, j)[:, 0:n], ACT.Copy), *step, j)
                for j in range(QUAD):
                    logit_ready.wait(act, turn, 4 * f + j)
                    expo_ready.send(act.activation(e[:, j, 0:nr], rh[:, j, 0:nr], ACT.Exp,
                                                   bias=nmax[:, j:j + 1], accum_out=tot[:, j:j + 1]))

            def hsT_copy(turn, f):
                for j in range(QUAD):
                    banks.wait_filled(act, turn, "hturn", f, j)
                    banks.drain(act.activation(hsT[:, j, :], banks.bank("hturn", f, j)[:, 0:P], ACT.Copy),
                                "hturn", f, j)

            def y1_copy(turn, j):
                banks.wait_filled(act, turn, "out1", j)
                banks.drain(act.activation(y1[:, j, :], banks.bank("out1", j), ACT.Identity,
                                           bias=w["L1b"][:, 3:4]), "out1", j)

            def attention2_before(turn, j):
                s = j % 2
                banks.wait_filled(act, turn, "low2", j)
                cq_ready.send(act.activation(cqT[:, s, :], banks.bank("low2", j)[0:64, 0:P], ACT.Copy))
                banks.wait_filled(act, turn, "qup2", j)
                banks.drain(act.activation(qT2[:, s, :, :].rearrange("p m n -> p (m n)"), banks.bank("qup2", j),
                                           ACT.Copy), "qup2", j)
                banks.wait_filled(act, turn, "vup2", j)
                banks.drain(act.activation(v2[:, s, :, :].rearrange("p b n -> p (b n)"), banks.bank("vup2", j),
                                           ACT.Copy), "vup2", j)
                banks.wait_drained(act, turn, "score2", j, 0)
                banks.wait_drained(act, turn, "score2", j, 1)
                flat = s2[:, s, :, :].rearrange("p h k -> p (h k)")
                exp2_ready.send(act.activation(flat, flat, ACT.Exp, scale=float(L2K) ** -0.5))

            def attention2_after(turn, j):
                for half in range(2):
                    banks.wait_filled(act, turn, "prob2", j, half)
                    banks.drain(act.activation(p2T[:, j % 2, 4 * half:4 * half + 4, :].rearrange("p h n -> p (h n)"),
                                               banks.bank("prob2", j, half), ACT.Copy), "prob2", j, half)

            act.wait_ge(pads, 4)
            with act.Fori(0, TURNS) as turn:
                for j in range(QUAD):
                    cT_loaded[j].wait(act, turn, 0)
                    cT_high.send(act.activation(cTh[:, j, :, :], cT[:, j, :, :], ACT.Copy))
                high(turn, 0, 0)
                for j in range(QUAD):
                    banks.wait_drained(act, turn, "proj0", j)
                    aT_high.send(act.activation(aTh[:, j, :, :], aT[:, j % 2, :, :], ACT.Copy))
                for j in range(QUAD):
                    sm0_ready.wait(act, turn, j)
                    pr0_ready.send(act.activation(pr[:, j, :], sm[:, j, :], ACT.Exp, bias=nmax[:, j:j + 1],
                                                  scale=float(D) ** -0.5, accum_out=tot[:, j:j + 1]))
                for j in range(QUAD):
                    banks.wait_filled(act, turn, "prob0", j)
                    banks.drain(act.activation(prT[:, j, :], banks.bank("prob0", j)[:, 0:P], ACT.Copy), "prob0", j)
                high(turn, 1, 1)
                route_exp(turn, 0, e0, R0)
                hsT_copy(turn, 0)
                for j in range(QUAD):
                    if j >= 2:
                        qkv_written.wait(act, turn, j - 2)
                    for k, (step, dst, lo) in enumerate((("q1", qs, 0), ("k1", kp, 8), ("v1", vp, 8))):
                        banks.wait_filled(act, turn, step, j)
                        banks.drain(act.activation(dst[:, j % 2, lo:lo + D], banks.bank(step, j), ACT.Identity,
                                                   bias=w["L1b"][:, k:k + 1]), step, j)
                for j in range(QUAD):
                    banks.wait_drained(act, turn, "dot1", j, 0)
                    banks.wait_drained(act, turn, "dot1", j, 1)
                    exp1_ready.send(act.activation(ee[:, :, :], ee[:, :, :], ACT.Exp, scale=float(CH) ** -0.5))
                    if j >= 1:
                        y1_copy(turn, j - 1)
                y1_copy(turn, QUAD - 1)
                high(turn, 3, 2)
                route_exp(turn, 1, e1, R1)
                hsT_copy(turn, 1)
                high(turn, 4, 3)
                for j in range(QUAD + 1):
                    if j < QUAD:
                        attention2_before(turn, j)
                    if j >= 1:
                        attention2_after(turn, j - 1)
                for j in range(QUAD):
                    banks.wait_filled(act, turn, "turn", 5, j)
                    banks.drain(act.activation(xTf[:, j, :, :].rearrange("p c n -> p (c n)"),
                                               banks.bank("turn", 5, j), ACT.Copy), "turn", 5, j)
                route_exp(turn, 2, e2, E01)
                for j in range(QUAD):
                    banks.wait_filled(act, turn, "gturn", j)
                    banks.drain(act.activation(rT2[:, j, :], banks.bank("gturn", j)[0:E01, 0:P], ACT.Copy),
                                "gturn", j)
                    banks.wait_filled(act, turn, "scale_out", j)
                    banks.drain(act.activation(osb[:, j, :], banks.bank("scale_out", j), ACT.Copy,
                                               scale=w["gates"][:, 6:7]), "scale_out", j)
                    banks.wait_drained(act, turn, "scale_in", j)
                    y2_high.send(act.activation(xTh[:, j, :, :], xTf[:, j, :, :], ACT.Copy))

        @block.gpsimd
        def _(pool):
            def rstd_of(turn, layer):
                for j in range(QUAD):
                    stats_ready.wait(pool, turn, 4 * layer + j)
                    pool.tensor_tensor(vare[:, j:j + 1], mv[:, j, 1:2], w["eps"][:, :], ALU.add)\
                        .then_inc(pool_step, 1)
                    pool.wait_ge(pool_step, turn * 24 + (4 * layer + j + 1))
                    rstd_ready.send(pool.tensor_tensor(rstd[:, j:j + 1], vare[:, j:j + 1], w["power"][:, 0:1],
                                                       ALU.pow))

            def add_bias(turn, f, layer):
                for j in range(QUAD):
                    xn_ready.wait(pool, turn, 4 * layer + j)
                    xbias_ready.send(pool.tensor_tensor(xq[:, j, :], xq[:, j, :], w["gbias"][:, f, :], ALU.add))

            for t in (kp, vp):
                pool.memset(t[:, :, :], 0.0).then_inc(pads, 1)
            pool.memset(e0[:, :, :], NEVER).then_inc(pads, 1)
            pool.memset(pick0[:, :, :], NEVER).then_inc(pads, 1)
            with pool.Fori(0, TURNS) as turn:
                for j in range(QUAD):
                    cT_high.wait(pool, turn, j)
                    cT_split.send(pool.tensor_tensor(cTl[:, j, :, :], cT[:, j, :, :], cTh[:, j, :, :], ALU.subtract))
                rstd_of(turn, 0)
                for j in range(QUAD):
                    aT_high.wait(pool, turn, j)
                    aT_split.send(pool.tensor_tensor(aTl[:, j, :, :], aT[:, j % 2, :, :], aTh[:, j, :, :],
                                                     ALU.subtract))
                rstd_of(turn, 1)
                add_bias(turn, 0, 1)
                rstd_of(turn, 2)
                for j in range(QUAD):
                    qkv_in[j % 2].wait(pool, turn, j // 2)
                    if j >= 1:
                        red1_done.wait(pool, turn, j - 1)
                    prod_pool.send(pool.tensor_tensor(prod[1][:, :, :, :], times_q(j, 1), windows(kL, j, 1), ALU.mult))
                    exp1_ready.wait(pool, turn, j)
                    prod_pool.send(pool.tensor_tensor(prod[1][:, :, :, :], weights(1), windows(vL, j, 1), ALU.mult))
                rstd_of(turn, 3)
                add_bias(turn, 1, 3)
                rstd_of(turn, 4)
                rstd_of(turn, 5)
                add_bias(turn, 2, 5)
                for j in range(QUAD):
                    y2_high.wait(pool, turn, j)
                    y2_split.send(pool.tensor_tensor(xTl[:, j, :, :], xTf[:, j, :, :], xTh[:, j, :, :], ALU.subtract))

        @block.vector
        def _(dve):
            apart = Apart(dve, pads, 4)
            dve.wait_ge(pads, 4)
            with dve.Fori(0, TURNS) as turn:
                st = Steps(dve, dve_step, DVE_STEPS, turn)

                def each(make, after=None):
                    made = []
                    for j in range(QUAD):
                        if after:
                            st.after(after[j], apart)
                        made.append(st.step(make(j)))
                    return made

                def normalise(layer, x, x_stands):
                    def one(j):
                        x_stands(j)
                        return dve.bn_stats(stats[:, j, :], x[:, j, :])
                    got = each(one)
                    for j in range(QUAD):
                        st.after(got[j], apart)
                        stats_ready.send(dve.bn_aggr(mv[:, j, :], stats[:, j, :]))
                    for j in range(QUAD):
                        rstd_ready.wait(dve, turn, 4 * layer + j)
                        xn_ready.send(dve.tensor_scalar(xn[:, j, :], x[:, j, :], mv[:, j, 0:1], rstd[:, j:j + 1],
                                                        ALU.subtract, ALU.mult))

                def low(layer, n):
                    for j in range(QUAD):
                        xT_high.wait(dve, turn, 4 * n + j)
                        banks.drain(dve.tensor_tensor(xTl[:, j, :, :].rearrange("p c n -> p (c n)"),
                                                      banks.bank("turn", layer, j),
                                                      xTh[:, j, :, :].rearrange("p c n -> p (c n)"), ALU.subtract),
                                    "turn", layer, j)

                def logits(f, step, nr, add=None):
                    for j in range(QUAD):
                        banks.wait_drained(dve, turn, *step, j)
                        if add is not None:
                            st.link(dve.tensor_tensor(rh[:, j, 0:nr], rh[:, j, 0:nr], add, ALU.add))
                        logit_ready.send(dve.tensor_reduce(nmax[:, j:j + 1], rh[:, j, 0:nr], AX.X, ALU.max,
                                                           negate=True))

                def expo(f, j, eng=dve):
                    expo_ready.wait(eng, turn, 4 * f + j)

                def lora(f, nr):
                    for j in range(QUAD):
                        hs_ready.send(dve.tensor_tensor(
                            hs[:, j, :].rearrange("p (e r) -> p e r", r=RANK),
                            rh[:, j, nr:nr + LORA].rearrange("p (e r) -> p e r", r=RANK),
                            comb[:, j, :].unsqueeze(2).to_broadcast([P, E01, RANK]), ALU.mult))

                def add_ffn(f):
                    for j in range(QUAD):
                        banks.wait_filled(dve, turn, "base", f, j)
                        xbias_ready.wait(dve, turn, 4 * f + j)
                        banks.drain(dve.scalar_tensor_tensor(
                            out=xq[:, j, :], in0=banks.bank("base", f, j), scalar=w["gates"][:, 4 + f:5 + f],
                            in1=xq[:, j, :], op0=ALU.mult, op1=ALU.add), "base", f, j)

                normalise(0, xin, lambda j: x_loaded[j].wait(dve, turn, 0))
                low(0, 0)
                for j in range(QUAD):
                    banks.wait_filled(dve, turn, "proj0", j)
                    if j >= 2:
                        aT_split.wait(dve, turn, j - 2)
                    banks.drain(dve.tensor_tensor(aT[:, j % 2, :, :],
                                                  banks.bank("proj0", j).rearrange("p (c n) -> p c n", c=C),
                                                  w["r"][:, :].unsqueeze(2).to_broadcast([P, C, P]), ALU.add),
                                "proj0", j)

                def row_term(j):
                    banks.wait_filled(dve, turn, "score0", j)
                    return dve.tensor_tensor(u[:, j:j + 1], banks.bank("score0", j)[:, P:P + 1], w["s"][:, :], ALU.add)
                for j in range(QUAD):
                    st.link(row_term(j))
                    banks.drain(dve.scalar_tensor_tensor(
                        out=sm[:, j, :], in0=banks.bank("score0", j)[:, 0:P], scalar=u[:, j:j + 1],
                        in1=w["bdmask"][:, :], op0=ALU.add, op1=ALU.add), "score0", j)

                def largest(j):
                    banks.wait_drained(dve, turn, "score0", j)
                    return dve.tensor_reduce(nmax[:, j:j + 1], sm[:, j, :], AX.X, ALU.max, negate=True)
                got = each(largest)
                for j in range(QUAD):
                    st.after(got[j])
                    sm0_ready.send(dve.tensor_scalar(nmax[:, j:j + 1], nmax[:, j:j + 1], float(D) ** -0.5, None,
                                                     ALU.mult))

                def over_sum(j):
                    pr0_ready.wait(dve, turn, j)
                    return dve.reciprocal(rec[:, j:j + 1], tot[:, j:j + 1])
                got = each(over_sum)
                got = each(lambda j: dve.tensor_scalar(rec[:, j:j + 1], rec[:, j:j + 1], w["gates"][:, 0:1], None,
                                                       ALU.mult), got)
                for j in range(QUAD):
                    st.after(got[j])
                    banks.wait_filled(dve, turn, "out0", j)
                    dve.wait_ge(stored.sem, turn * (QUAD * 16))
                    banks.drain(dve.scalar_tensor_tensor(
                        out=xq[:, j, :], in0=banks.bank("out0", j), scalar=rec[:, j:j + 1], in1=xin[:, j, :],
                        op0=ALU.mult, op1=ALU.add), "out0", j)

                normalise(1, xq, lambda j: banks.wait_drained(dve, turn, "out0", j))
                low(1, 1)
                logits(0, ("route", 0), R0)

                def top(e, f):
                    def one(j):
                        expo(f, j, apart)
                        return dve.max(top8[:, j, :], e[:, j, 0:(R0, R1)[f]])
                    return each(one)
                got = top(e0, 0)
                each(lambda j: dve.tensor_tensor(tot[:, j:j + 1], top8[:, j, 0:1], top8[:, j, 1:2], ALU.add), got)
                got = each(lambda j: dve.tensor_copy(pick0[:, j, 0:2], top8[:, j, 0:2]), got)
                got = each(lambda j: dve.reciprocal(rec[:, j:j + 1], tot[:, j:j + 1]), got)
                got = each(lambda j: dve.match_replace(rkeep[:, j, 0:14], pick0[:, j, :], e0[:, j, :], 0.0), got)
                got = each(lambda j: dve.tensor_tensor(rsel[:, j, 0:R0], e0[:, j, 0:R0], rkeep[:, j, 0:R0],
                                                       ALU.subtract), got)
                got = each(lambda j: dve.tensor_scalar(comb[:, j, :], rsel[:, j, 0:R0], rec[:, j:j + 1], 2.0,
                                                       ALU.mult, ALU.mult), got)
                st.after(got[-1])
                lora(0, R0)
                add_ffn(0)

                normalise(2, xq, lambda j: banks.wait_drained(dve, turn, "base", 0, j))
                for j in range(QUAD):
                    qkv_in[j % 2].wait(dve, turn, j // 2)
                    if j >= 1:
                        st.after(got_sum)
                    prod_dve.send(dve.tensor_tensor(prod[0][:, :, :, :], times_q(j, 0), windows(kL, j, 0), ALU.mult))
                    for h in range(2):
                        banks.wait_filled(dve, turn, "dot1", j, h)
                        at = slice(h * (TP // 2), (h + 1) * (TP // 2))
                        dots = banks.bank("dot1", j, h).rearrange("p (t w) -> p t w", w=WIN)
                        st.link(dve.tensor_reduce(mx1[:, at], dots, AX.X, ALU.max))
                        ins = dve.tensor_tensor(ee[:, at, :], dots,
                                                mx1[:, at].unsqueeze(2).to_broadcast([P, TP // 2, WIN]), ALU.subtract)
                        banks.drain(ins, "dot1", j, h)
                    exp1_ready.wait(dve, turn, j)
                    mine = st.step(dve.tensor_tensor(prod[0][:, :, :, :], weights(0), windows(vL, j, 0), ALU.mult))
                    st.link(dve.tensor_reduce(sum1[:, :], ee[:, :, :], AX.X, ALU.add))
                    st.link(dve.reciprocal(rec1[:, :], sum1[:, :]))
                    if j >= 2:
                        o_written.wait(dve, turn, j - 2)
                    got_sum = st.step(dve.tensor_reduce(oL[:, j % 2, :, 0:TP // 2], prod[0][:, :, :, :], AX.X, ALU.add))
                    prod_pool.wait(dve, turn, 2 * j + 1)
                    red1_done.send(dve.tensor_reduce(oL[:, j % 2, :, TP // 2:TP], prod[1][:, :, :, :], AX.X, ALU.add))
                    red1_done.wait(dve, turn, j)
                    oL_ready.send(dve.tensor_tensor(oL[:, j % 2, :, :], oL[:, j % 2, :, :],
                                                    rec1[:, :].unsqueeze(1).to_broadcast([P, CH, TP]), ALU.mult))

                def add1(j):
                    banks.wait_drained(dve, turn, "out1", j)
                    return dve.scalar_tensor_tensor(out=xq[:, j, :], in0=y1[:, j, :], scalar=w["gates"][:, 1:2],
                                                    in1=xq[:, j, :], op0=ALU.mult, op1=ALU.add)
                added = each(add1)

                normalise(3, xq, lambda j: st.after(added[j]))
                low(3, 2)
                logits(1, ("route", 1), R1, w["rb1"][:, :])
                got = top(e1, 1)
                got = each(lambda j: dve.match_replace(rkeep[:, j, 0:R1], top8[:, j, :], e1[:, j, :], 0.0), got)
                got = each(lambda j: dve.tensor_tensor(rsel[:, j, 0:R1], e1[:, j, :], rkeep[:, j, 0:R1],
                                                       ALU.subtract), got)
                got = each(lambda j: dve.tensor_tensor(rmix[:, j, :, :],
                                                       rsel[:, j, 0:R1].unsqueeze(1).to_broadcast([P, E01, R1]),
                                                       w["route_to"][:, :, :], ALU.mult), got)
                each(lambda j: dve.reciprocal(rec[:, j:j + 1], tot[:, j:j + 1]))
                got = each(lambda j: dve.tensor_reduce(comb[:, j, :], rmix[:, j, :, :], AX.X, ALU.add), got)
                got = each(lambda j: dve.tensor_scalar(comb[:, j, :], comb[:, j, :], rec[:, j:j + 1], 2.0,
                                                       ALU.mult, ALU.mult), got)
                st.after(got[-1])
                lora(1, R1)
                add_ffn(1)

                normalise(4, xq, lambda j: banks.wait_drained(dve, turn, "base", 1, j))
                low(4, 3)

                def attention2_before(j):
                    s = j % 2
                    cq_ready.wait(dve, turn, j)
                    low_keys = banks.bank("low2", j)[:, P:2 * P].rearrange("p (b k) -> p b k", b=2)
                    banks.drain(dve.tensor_tensor(
                        ckv[:, s, :, :, :], low_keys.unsqueeze(2).to_broadcast([P, 2, 4, SEQ]),
                        w["quarter"][:, :].unsqueeze(1).unsqueeze(3).to_broadcast([P, 2, 4, SEQ]), ALU.mult), "low2", j)
                    for half in range(2):
                        heads = slice(8 * half, 8 * half + 8)
                        banks.wait_filled(dve, turn, "score2", j, half)
                        scores = banks.bank("score2", j, half).rearrange("p (h k) -> p h k", k=SEQ)
                        st.link(dve.tensor_reduce(mx2[:, s, heads], scores, AX.X, ALU.max))
                        banks.drain(dve.tensor_tensor(s2[:, s, heads, :], scores,
                                                      mx2[:, s, heads].unsqueeze(2).to_broadcast([P, 8, SEQ]),
                                                      ALU.subtract), "score2", j, half)

                def attention2_after(j):
                    s = j % 2
                    exp2_ready.wait(dve, turn, j)
                    st.link(dve.tensor_reduce(sum2[:, s, :], s2[:, s, :, :], AX.X, ALU.add))
                    st.link(dve.reciprocal(rec2[:, s, :], sum2[:, s, :]))
                    for half in range(2):
                        banks.wait_filled(dve, turn, "out2", j, half)
                        mine = o2[:, s, :, :].rearrange("p (a b) k -> p a b k", b=2)[:, :, half, :]
                        over = rec2[:, s, :].rearrange("p (a b) -> p a b", b=2)[:, :, half]
                        banks.drain(dve.tensor_tensor(
                            mine, banks.bank("out2", j, half)[:, 0:256].rearrange("p (a k) -> p a k", k=32),
                            over.unsqueeze(2).to_broadcast([P, 8, 32]), ALU.mult), "out2", j, half)
                    banks.wait_drained(dve, turn, "out2", j, 0)
                    banks.wait_drained(dve, turn, "out2", j, 1)
                    return st.step(dve.scalar_tensor_tensor(
                        out=xq[:, j, :], in0=o2[:, s, :, :].rearrange("p h k -> p (h k)"),
                        scalar=w["gates"][:, 2:3], in1=xq[:, j, :], op0=ALU.mult, op1=ALU.add))
                added = []
                for j in range(QUAD + 1):
                    if j < QUAD:
                        attention2_before(j)
                    if j >= 1:
                        added.append(attention2_after(j - 1))

                normalise(5, xq, lambda j: st.after(added[j]))
                logits(2, ("gate2",), E01)

                def over_all(j):
                    expo(2, j)
                    return dve.reciprocal(rec[:, j:j + 1], tot[:, j:j + 1])
                got = each(over_all)
                for j in range(QUAD):
                    st.after(got[j])
                    route2_ready.send(dve.tensor_scalar(comb[:, j, :], e2[:, j, :], rec[:, j:j + 1], None, ALU.mult))
                for j in range(QUAD):
                    banks.wait_filled(dve, turn, "scale_in", j)
                    flat = xTf[:, j, :, :].rearrange("p c n -> p (c n)")
                    banks.drain(dve.tensor_tensor(flat, banks.bank("scale_in", j), flat, ALU.mult), "scale_in", j)
                for j in range(QUAD):
                    banks.wait_filled(dve, turn, "sign2", j)
                    banks.drain(dve.tensor_tensor(osb[:, j, :], banks.bank("sign2", j), osb[:, j, :], ALU.mult),
                                "sign2", j)
                for j in range(QUAD):
                    banks.wait_drained(dve, turn, "sign2", j)
                    xbias_ready.wait(dve, turn, 8 + j)
                    x_done.send(dve.tensor_tensor(xq[:, j, :], xq[:, j, :], osb[:, j, :], ALU.add))
                st.close()


def prepare_last(nc, io, w):
    plan = []
    for j in range(QUAD):
        plan.append((("turn", j), j))
    plan += [(("cos",), 4), (("sin",), 5)]
    with ExitStack() as ctx:
        def sb(name, shape, dt=F32):
            return ctx.enter_context(nc.sbuf_tensor("pl_" + name, shape, dt))

        def signal(name, per_turn, by=1):
            return Signal(nc, w, "pl_" + name, per_turn, by)

        xn, cT = sb("xn", [P, QUAD, D]), sb("cT", [P, C, QUAD * P])
        stats, mv = sb("stats", [P, QUAD, 6]), sb("mv", [P, QUAD, 2])
        vare, rstd = sb("vare", [P, QUAD]), sb("rstd", [P, QUAD])
        mask_raw = sb("mask", [P, TILES, SEQ], I32)
        pos_raw, pos = sb("pos_raw", [P, TOKENS], I32), sb("pos", [P, TOKENS])
        wrap = sb("wrap", [P, TOKENS])
        row = sb("row", [P, C])
        one_hot = sb("one_hot", [P, C, QUAD * P])
        table = sb("table", [P, 2, C, P])
        banks = Banks(nc, ctx, w, "pl", plan)
        x_loaded = new_semaphore(nc, w, "pl_x_loaded")
        tables_loaded = new_semaphore(nc, w, "pl_tables_loaded")
        row_ready = new_semaphore(nc, w, "pl_row_ready")
        once = new_semaphore(nc, w, "pl_once")
        cT_loaded, cT_high, cT_low = signal("cT_loaded", 1, 16), signal("cT_high", 1), signal("cT_low", 1)
        stats_ready, rstd_ready, xn_ready = signal("stats_ready", 4), signal("rstd_ready", 4), signal("xn_ready", 4)
        xT_high, hot_ready = signal("xT_high", 4), signal("hot_ready", 4)
        dve_step = new_semaphore(nc, w, "pl_dve_step")
        pool_step = new_semaphore(nc, w, "pl_pool_step")
        block = ctx.enter_context(nc.Block())
        PER = QUAD * P

        @block.sync
        def _(sp):
            sp.dma_start(w["X"][:, :, :], io["x_mid"].rearrange("(t p) n -> p t n", p=P)).then_inc(x_loaded, 16)
            sp.dma_start(pos_raw[:, :], io["pos"].partition_broadcast(P)).then_inc(tables_loaded, 16)
            sp.dma_start(table[:, 0, :, :], io["cos"].rearrange("(c p) n -> p c n", p=P)).then_inc(tables_loaded, 16)
            sp.dma_start(table[:, 1, :, :], io["sin"].rearrange("(c p) n -> p c n", p=P)).then_inc(tables_loaded, 16)
            sp.dma_start(mask_raw[:, :, :], io["mask"].rearrange("(t p) n -> p t n", p=P)).then_inc(tables_loaded, 16)
            src = io["ctxT"].rearrange("(c p) n -> p c n", p=P)
            cT_loaded.send(sp.dma_start(cT[:, :, :], src[:, :, 0:PER]))
            with sp.Fori(0, TURNS - 1) as turn:
                cT_low.wait(sp, turn, 0)
                cT_loaded.send(sp.dma_start(cT[:, :, :], src[:, :, bass.ts(turn + 1, PER)]))

        @block.gpsimd
        def _(pool):
            pool.iota(row[:, :], pattern=[[P, C]], base=0, channel_multiplier=1,
                      allow_small_or_imprecise_dtypes=True).then_inc(row_ready, 1)
            with pool.Fori(0, TURNS) as turn:
                for j in range(QUAD):
                    stats_ready.wait(pool, turn, j)
                    pool.tensor_tensor(vare[:, j:j + 1], mv[:, j, 1:2], w["eps"][:, :], ALU.add)\
                        .then_inc(pool_step, 1)
                    pool.wait_ge(pool_step, turn * QUAD + (j + 1))
                    rstd_ready.send(pool.tensor_tensor(rstd[:, j:j + 1], vare[:, j:j + 1], w["power"][:, 0:1],
                                                       ALU.pow))
                cT_high.wait(pool, turn, 0)
                cT_low.send(pool.tensor_tensor(w["cTl"][:, :, bass.ts(turn, PER)], cT[:, :, :],
                                               w["cTh"][:, :, bass.ts(turn, PER)], ALU.subtract))

        @block.tensor
        def _(pe):
            with pe.Fori(0, TURNS) as turn:
                for j in range(QUAD):
                    xn_ready.wait(pe, turn, j)
                    banks.wait_free(pe, turn, "turn", j)
                    for c in range(C):
                        last = pe.transpose(banks.bank("turn", j)[:, c * P:(c + 1) * P],
                                            xn[:, j, c * P:(c + 1) * P], w["ident"][:, :])
                    banks.fill(last, "turn", j)
                for k, step in enumerate(("cos", "sin")):
                    hot_ready.wait(pe, turn, QUAD - 1)
                    banks.wait_free(pe, turn, step)
                    for c in range(C):
                        last = pe.matmul(banks.bank(step), table[:, k, c, :], one_hot[:, c, :],
                                         start=(c == 0), stop=(c == C - 1))
                    banks.fill(last, step)

        @block.scalar
        def _(act):
            with act.Fori(0, TURNS) as turn:
                cT_loaded.wait(act, turn, 0)
                cT_high.send(act.activation(w["cTh"][:, :, bass.ts(turn, PER)], cT[:, :, :], ACT.Copy))
                for j in range(QUAD):
                    banks.wait_filled(act, turn, "turn", j)
                    xT_high.send(act.activation(w["xTh"][:, :, bass.ts(turn * QUAD + j, P)],
                                                banks.bank("turn", j).rearrange("p (c n) -> p c n", c=C), ACT.Copy))
                for k, step in enumerate(("cos", "sin")):
                    banks.wait_filled(act, turn, step)
                    banks.drain(act.activation(w[step][:, bass.ts(turn, PER)], banks.bank(step), ACT.Copy), step)

        @block.vector
        def _(dve):
            apart = Apart(dve, row_ready, 1)
            dve.wait_ge(tables_loaded, 64)
            dve.tensor_copy(pos[:, :], pos_raw[:, :]).then_inc(once, 1)
            dve.wait_ge(once, 1)
            dve.tensor_scalar(wrap[:, :], pos[:, :], 0.0, float(POSITIONS), ALU.is_lt, ALU.mult).then_inc(once, 1)
            dve.wait_ge(once, 2)
            dve.tensor_tensor(pos[:, :], pos[:, :], wrap[:, :], ALU.add).then_inc(once, 1)
            dve.wait_ge(once, 3)
            dve.tensor_scalar(pos[:, :], pos[:, :], 0.0, float(POSITIONS - 1), ALU.max, ALU.min).then_inc(once, 1)
            dve.tensor_scalar(w["mask"][:, :, :], mask_raw[:, :, :], 0.0, MASKED, ALU.is_equal, ALU.mult)
            dve.wait_ge(once, 4)
            dve.wait_ge(x_loaded, 16)
            dve.wait_ge(row_ready, 1)
            with dve.Fori(0, TURNS) as turn:
                for j in range(QUAD):
                    dve.bn_stats(stats[:, j, :], w["X"][:, bass.ds(turn * QUAD + j, 1), :]).then_inc(dve_step, 1)
                for j in range(QUAD):
                    apart.wait_ge(dve_step, turn * QUAD + (j + 1))
                    stats_ready.send(dve.bn_aggr(mv[:, j, :], stats[:, j, :]))
                banks.wait_free(dve, turn, "cos")
                banks.wait_free(dve, turn, "sin")
                for c in range(C):
                    hot_ready.send(dve.tensor_scalar(one_hot[:, c, :], pos[:, bass.ts(turn, PER)],
                                                     row[:, c:c + 1], None, ALU.is_equal))
                for j in range(QUAD):
                    rstd_ready.wait(dve, turn, j)
                    xn_ready.send(dve.tensor_scalar(xn[:, j, :], w["X"][:, bass.ds(turn * QUAD + j, 1), :],
                                                    mv[:, j, 0:1], rstd[:, j:j + 1], ALU.subtract, ALU.mult))
                for j in range(QUAD):
                    xT_high.wait(dve, turn, j)
                    banks.drain(dve.tensor_tensor(w["xTl"][:, :, bass.ts(turn * QUAD + j, P)],
                                                  banks.bank("turn", j).rearrange("p (c n) -> p c n", c=C),
                                                  w["xTh"][:, :, bass.ts(turn * QUAD + j, P)], ALU.subtract),
                                "turn", j)


def last_attention(nc, io, w):
    PER = QUAD * P
    before = [(("q", "first", 0), 0), (("k", "first"), 1), (("q", "first", 1), 0), (("q", "first", 2), 1),
              (("q", "first", 3), 0), (("v", "first"), 1)]
    plan = []
    for n in range(QUAD):
        for u in range(QUAD):
            plan += [(("score", n, u), 2 + u % 2), (("q", n, u), (0, 0, 1, 0)[u]), (("turn", n, u), 4)]
            if u == 0:
                plan.append((("k", n), 1))
            if u == QUAD - 1:
                plan.append((("v", n), 1))
            plan += [(("even", n, u), 5), (("odd", n, u), 6), (("out", n, u), 7)]
    with ExitStack() as ctx:
        def sb(name, shape, dt=F32):
            return ctx.enter_context(nc.sbuf_tensor("la_" + name, shape, dt))

        def signal(name, per_turn, by=1):
            return Signal(nc, w, "la_" + name, per_turn, by)

        raw_q, raw_kv, raw_o = sb("raw_q", [P, C, GROUP * HD]), sb("raw_kv", [P, 2, C, HD]), sb("raw_o", [P, GROUP, D])
        wqh, wql = sb("wqh", [P, C, GROUP * HD], HALF), sb("wql", [P, C, GROUP * HD], HALF)
        woh, wol = sb("woh", [P, GROUP, D], HALF), sb("wol", [P, GROUP, D], HALF)
        wkvh, wkvl = sb("wkvh", [P, 2, C, HD], HALF), sb("wkvl", [P, 2, C, HD], HALF)
        q, k = sb("q", [P, 2, GROUP, PER]), sb("k", [P, 2, PER])
        straight = sb("straight", [P, 2, PER])
        rot = sb("rot", [P, 2, PER])
        v2 = sb("v2", [P, 2, QUAD, 2, HD])
        s, p, pT = sb("s", [P, 2, GROUP, SEQ]), sb("p", [P, 2, GROUP, SEQ]), sb("pT", [P, 2, 2, P])
        mx, tot, rec = sb("mx", [P, 2, GROUP]), sb("tot", [P, 2, GROUP]), sb("rec", [P, 2, GROUP])
        oTh, oTl = sb("oTh", [P, 2, GROUP, P], HALF), sb("oTl", [P, 2, GROUP, P], HALF)

        banks = Banks(nc, ctx, w, "la", plan, before)
        q_loaded, o_loaded = signal("q_loaded", 1, 48), signal("o_loaded", 1, 16)
        q_high, q_low, o_high, o_low = signal("q_high", 1), signal("q_low", 1), signal("o_high", 1), signal("o_low", 1)
        rope_sum = signal("rope_sum", 20)
        exp_ready, rec_ready, p_ready = signal("exp_ready", 16), signal("rec_ready", 16), signal("p_ready", 16)
        oT_high = signal("oT_high", 32)
        dve_step = new_semaphore(nc, w, "la_dve_step")
        block = ctx.enter_context(nc.Block())

        def tokens(n):
            return slice(n * PER, (n + 1) * PER)

        ROTATIONS = [("q", 0), ("k", None), ("q", 1), ("q", 2), ("q", 3)]

        def use_of(n, i):
            kind, u = ROTATIONS[i]
            return (kind, n) if kind == "k" else (kind, n, u)

        @block.sync
        def _(sp):
            def load_qkv(head):
                sp.dma_start(raw_q[:, :, :], io["Wq3"].rearrange("(c p) n -> p c n", p=P)[:, :, bass.ts(head, GROUP * HD)])\
                  .then_inc(q_loaded.sem, 16)
                for i, name in enumerate(("Wk3", "Wv3")):
                    sp.dma_start(raw_kv[:, i, :, :],
                                 io[name].rearrange("(c p) n -> p c n", p=P)[:, :, bass.ts(head, HD)])\
                      .then_inc(q_loaded.sem, 16)

            def load_o(head):
                rows = io["Wo3"][bass.ts(head, GROUP * HD), :]
                o_loaded.send(sp.dma_start(raw_o[:, :, :], rows.rearrange("(h p) n -> p h n", p=P)))

            load_qkv(0)
            load_o(0)
            with sp.Fori(0, KV - 1) as turn:
                q_low.wait(sp, turn, 0)
                load_qkv(turn + 1)
                o_low.wait(sp, turn, 0)
                load_o(turn + 1)

        @block.tensor
        def _(pe):
            def xs(t, n):
                return [t[:, c, tokens(n)] for c in range(C)]

            def project_q(turn, step, n, u):
                banks.wait_free(pe, turn, *step)
                cols = slice(u * HD, (u + 1) * HD)
                banks.fill(three(pe, banks.bank(*step), [wqh[:, c, cols] for c in range(C)],
                                 [wql[:, c, cols] for c in range(C)], xs(w["xTh"], n), xs(w["xTl"], n)), *step)

            def project_k(turn, step, n):
                banks.wait_free(pe, turn, *step)
                banks.fill(three(pe, banks.bank(*step), [wkvh[:, 0, c, :] for c in range(C)],
                                 [wkvl[:, 0, c, :] for c in range(C)], xs(w["cTh"], n), xs(w["cTl"], n)), *step)

            def project_v(turn, step, n):
                banks.wait_free(pe, turn, *step)
                for t in range(QUAD):
                    cols = slice(n * PER + t * P, n * PER + (t + 1) * P)
                    last = three(pe, banks.bank(*step)[:, t * HD:(t + 1) * HD],
                                 [w["cTh"][:, c, cols] for c in range(C)], [w["cTl"][:, c, cols] for c in range(C)],
                                 [wkvh[:, 1, c, :] for c in range(C)], [wkvl[:, 1, c, :] for c in range(C)])
                banks.fill(last, *step)

            def out_projection(turn, n, u):
                for half in range(2):
                    banks.wait_drained(pe, turn, ("even", "odd")[half], n, u)
                if (n, u) == (0, 0):
                    o_low.wait(pe, turn, 0)
                banks.wait_free(pe, turn, "out", n, u)
                banks.fill(three(pe, banks.bank("out", n, u), [oTh[:, u % 2, h, :] for h in range(GROUP)],
                                 [oTl[:, u % 2, h, :] for h in range(GROUP)], [woh[:, h, :] for h in range(GROUP)],
                                 [wol[:, h, :] for h in range(GROUP)]), "out", n, u)

            def unit(turn, n, u, more):
                m = n % 2
                if u == 0:
                    rope_sum.wait(pe, turn, 5 * n + 4)
                banks.wait_free(pe, turn, "score", n, u)
                out = banks.bank("score", n, u)[:, 0:GROUP * SEQ]
                pe.matmul(out, w["identh"][:, :],
                          w["mask"][:, n * QUAD + u, :].unsqueeze(1).to_broadcast([P, GROUP, SEQ]),
                          start=True, stop=True, skip_group_check=True)
                for b in range(2):
                    cols = slice(u * P + b * SEQ, u * P + (b + 1) * SEQ)
                    for h in range(GROUP):
                        last = pe.matmul(out[SEQ * b:SEQ * b + SEQ, h * SEQ:(h + 1) * SEQ], q[:, m, h, cols],
                                         k[:, m, cols], start=False, stop=True, skip_group_check=True)
                banks.fill(last, "score", n, u)
                if more:
                    if n == QUAD - 1 and u == 0:
                        q_low.wait(pe, turn, 1)
                    project_q(turn, ("q", n, u), (n + 1) % QUAD, u)
                p_ready.wait(pe, turn, QUAD * n + u)
                banks.wait_free(pe, turn, "turn", n, u)
                for hp in range(2):
                    last = pe.transpose(banks.bank("turn", n, u)[:, hp * P:(hp + 1) * P],
                                        p[:, u % 2, 2 * hp:2 * hp + 2, :].rearrange("p h k -> p (h k)"),
                                        w["ident"][:, :])
                banks.fill(last, "turn", n, u)
                if (n, u) != (0, 0):
                    out_projection(turn, n if u else n - 1, (u - 1) % QUAD)
                if more and u == 0:
                    project_k(turn, ("k", n), (n + 1) % QUAD)
                if more and u == QUAD - 1:
                    project_v(turn, ("v", n), (n + 1) % QUAD)
                banks.wait_drained(pe, turn, "turn", n, u)
                if (n, u) == (0, 0):
                    banks.wait_all_drained(pe, turn, 1)
                elif u == 0:
                    banks.wait_drained(pe, turn, "v", n - 1)
                for half, name in enumerate(("even", "odd")):
                    banks.wait_free(pe, turn, name, n, u)
                    rows = slice(SEQ * half, SEQ * half + SEQ)
                    out = banks.bank(name, n, u)[:, 0:2 * P].rearrange("p (h t) -> p h t", h=2)
                    for b in range(2):
                        cols = slice(SEQ * b, SEQ * b + SEQ)
                        last = pe.matmul(out[:, :, cols], v2[rows, m, u, b, :], pT[rows, u % 2, :, cols],
                                         start=True, stop=True)
                    banks.fill(last, name, n, u)

            def body(turn, more):
                for n in range(QUAD):
                    for u in range(QUAD):
                        unit(turn, n, u, more or n < QUAD - 1)
                out_projection(turn, QUAD - 1, QUAD - 1)

            q_low.wait(pe, 0, 0)
            project_q(0, ("q", "first", 0), 0, 0)
            project_k(0, ("k", "first"), 0)
            for u in range(1, QUAD):
                project_q(0, ("q", "first", u), 0, u)
            project_v(0, ("v", "first"), 0)
            with pe.Fori(0, KV - 1) as turn:
                body(turn, True)
            body(KV - 1, False)

        @block.scalar
        def _(act):
            def split_qkv(turn):
                act.activation(wqh[:, :, :], raw_q[:, :, :], ACT.Copy)
                q_high.send(act.activation(wkvh[:, :, :, :], raw_kv[:, :, :, :], ACT.Copy))

            def copy_v(turn, step, m):
                banks.wait_filled(act, turn, *step)
                for half in range(2):
                    for b in range(2):
                        src = banks.bank(*step)[SEQ * b:SEQ * b + SEQ, :].rearrange("p (t n) -> p t n", t=QUAD)
                        last = act.activation(v2[SEQ * half:SEQ * half + SEQ, m, :, b, :], src, ACT.Copy)
                banks.drain(last, *step)

            def body(turn, more):
                o_loaded.wait(act, turn, 0)
                banks.wait_all_filled(act, turn, 7)
                o_high.send(act.activation(woh[:, :, :], raw_o[:, :, :], ACT.Copy))
                for n in range(QUAD):
                    for u in range(QUAD):
                        flat = s[:, u % 2, :, :].rearrange("p h k -> p (h k)")
                        banks.wait_drained(act, turn, "score", n, u)
                        exp_ready.send(act.activation(flat, flat, ACT.Exp, scale=float(HD) ** -0.5))
                        banks.wait_filled(act, turn, "turn", n, u)
                        banks.drain(act.activation(pT[:, u % 2, :, :].rearrange("p h k -> p (h k)"),
                                                   banks.bank("turn", n, u)[:, 0:2 * P], ACT.Copy), "turn", n, u)
                        if (more or n < QUAD - 1) and u == QUAD - 1:
                            copy_v(turn, ("v", n), (n + 1) % 2)
                        for half, name in enumerate(("even", "odd")):
                            banks.wait_filled(act, turn, name, n, u)
                            oT_high.send(act.activation(
                                oTh[:, u % 2, :, :].rearrange("p (a b) t -> p a b t", b=2)[:, :, half, :],
                                banks.bank(name, n, u)[:, 0:2 * P].rearrange("p (h t) -> p h t", h=2), ACT.Copy))
                        if more and (n, u) == (QUAD - 2, QUAD - 1):
                            q_loaded.wait(act, turn, 1)
                            split_qkv(turn)

            q_loaded.wait(act, 0, 0)
            split_qkv(0)
            copy_v(0, ("v", "first"), 0)
            with act.Fori(0, KV - 1) as turn:
                body(turn, True)
            body(KV - 1, False)

        @block.gpsimd
        def _(pool):
            def add_rotation(turn, step, slot, dst):
                banks.wait_drained(pool, turn, *step)
                rope_sum.send(pool.tensor_tensor(dst, straight[:, slot, :], rot[:, slot, :], ALU.add))

            def low_qkv():
                pool.tensor_tensor(wql[:, :, :], raw_q[:, :, :], wqh[:, :, :], ALU.subtract)
                q_low.send(pool.tensor_tensor(wkvl[:, :, :, :], raw_kv[:, :, :, :], wkvh[:, :, :, :], ALU.subtract))

            def rotated(i, m):
                kind, u = ROTATIONS[i]
                return k[:, m, :] if kind == "k" else q[:, m, u, :]

            def body(turn, more):
                o_high.wait(pool, turn, 0)
                o_low.send(pool.tensor_tensor(wol[:, :, :], raw_o[:, :, :], woh[:, :, :], ALU.subtract))
                for n in range(QUAD):
                    for u in range(QUAD):
                        rec_ready.wait(pool, turn, QUAD * n + u)
                        p_ready.send(pool.tensor_tensor(p[:, u % 2, :, :], s[:, u % 2, :, :],
                                                        rec[:, u % 2, :].unsqueeze(2).to_broadcast([P, GROUP, SEQ]),
                                                        ALU.mult))
                        if more or n < QUAD - 1:
                            for i in ((0, 1), (2,), (3,), (4,))[u]:
                                add_rotation(turn, use_of(n, i), (5 * n + i + 5) % 2, rotated(i, (n + 1) % 2))
                            if more and n == QUAD - 2 and u == QUAD - 1:
                                q_high.wait(pool, turn, 1)
                                low_qkv()

            q_high.wait(pool, 0, 0)
            low_qkv()
            for i in range(5):
                add_rotation(0, use_of("first", i), i % 2, rotated(i, 0))
            with pool.Fori(0, KV - 1) as turn:
                body(turn, True)
            body(KV - 1, False)

        @block.vector
        def _(dve):
            def rotate(turn, k_at, slot, step, n):
                if k_at >= 2:
                    rope_sum.wait(dve, turn, k_at - 2)
                banks.wait_filled(dve, turn, *step)
                src = banks.bank(*step)
                dve.tensor_tensor(straight[:, slot, :], src, w["cos"][:, tokens(n)], ALU.mult)
                dve.tensor_tensor(rot[0:64, slot, :], src[64:128, :], w["sin"][64:128, tokens(n)], ALU.mult)
                banks.drain(dve.tensor_tensor(rot[64:128, slot, :], src[0:64, :], w["sin"][0:64, tokens(n)],
                                              ALU.mult), *step)

            def lows(turn, n, u):
                for half, name in enumerate(("even", "odd")):
                    oT_high.wait(dve, turn, 2 * (QUAD * n + u) + half)
                    mine = [t[:, u % 2, :, :].rearrange("p (a b) t -> p a b t", b=2)[:, :, half, :] for t in (oTl, oTh)]
                    banks.drain(dve.tensor_tensor(
                        mine[0], banks.bank(name, n, u)[:, 0:2 * P].rearrange("p (h t) -> p h t", h=2), mine[1],
                        ALU.subtract), name, n, u)

            def add_out(turn, n, u):
                banks.wait_filled(dve, turn, "out", n, u)
                tile = w["X"][:, n * QUAD + u, :]
                banks.drain(dve.scalar_tensor_tensor(out=tile, in0=banks.bank("out", n, u),
                                                     scalar=w["gates"][:, 3:4], in1=tile, op0=ALU.mult, op1=ALU.add),
                            "out", n, u)

            def body(turn, more):
                st = Steps(dve, dve_step, LAST_STEPS, turn)
                banks.wait_all_drained(dve, turn, 7)
                for n in range(QUAD):
                    for u in range(QUAD):
                        if (n, u) != (0, 0):
                            prev = (n, u - 1) if u else (n - 1, QUAD - 1)
                            lows(turn, *prev)
                        slot = u % 2
                        banks.wait_filled(dve, turn, "score", n, u)
                        scores = banks.bank("score", n, u)[:, 0:GROUP * SEQ].rearrange("p (h k) -> p h k", k=SEQ)
                        st.link(dve.tensor_reduce(mx[:, slot, :], scores, AX.X, ALU.max))
                        banks.drain(dve.tensor_tensor(s[:, slot, :, :], scores,
                                                      mx[:, slot, :].unsqueeze(2).to_broadcast([P, GROUP, SEQ]),
                                                      ALU.subtract), "score", n, u)
                        exp_ready.wait(dve, turn, QUAD * n + u)
                        st.link(dve.tensor_reduce(tot[:, slot, :], s[:, slot, :, :], AX.X, ALU.add))
                        rec_ready.send(dve.reciprocal(rec[:, slot, :], tot[:, slot, :]))
                        some = more or n < QUAD - 1
                        turns = ((0, 1), (2,), (3,), (4,))[u] if some else ()
                        for i in turns:
                            if i == 1 and (n, u) != (0, 0):
                                add_out(turn, *prev)
                            rotate(turn, 5 * n + i + 5, (5 * n + i + 5) % 2, use_of(n, i), (n + 1) % QUAD)
                        if (n, u) != (0, 0) and 1 not in turns:
                            add_out(turn, *prev)
                lows(turn, QUAD - 1, QUAD - 1)
                add_out(turn, QUAD - 1, QUAD - 1)
                st.close()

            for i in range(5):
                rotate(0, i, i % 2, use_of("first", i), 0)
            with dve.Fori(0, KV - 1) as turn:
                body(turn, True)
            body(KV - 1, False)




def last_ffn(nc, io, w):
    plan = [(("turn", j), j % 2) for j in range(QUAD)]
    plan += [(("route", j), 2 + j % 2) for j in range(QUAD)]
    for j in range(QUAD):
        plan += [(("hturn", j), j % 2), (("out", j), 4 + j)]
    with ExitStack() as ctx:
        def sb(name, shape, dt=F32):
            return ctx.enter_context(nc.sbuf_tensor("lf_" + name, shape, dt))

        def signal(name, per_turn, by=1):
            return Signal(nc, w, "lf_" + name, per_turn, by)

        xn, xout = sb("xn", [P, QUAD, D]), sb("xout", [P, QUAD, D])
        stats, mv = sb("stats", [P, QUAD, 6]), sb("mv", [P, QUAD, 2])
        vare, rstd = sb("vare", [P, QUAD]), sb("rstd", [P, QUAD])
        xTh, xTl = sb("xTh", [P, QUAD, C, P], HALF), sb("xTl", [P, QUAD, C, P], HALF)
        e, pick = sb("e", [P, QUAD, 10]), sb("pick", [P, QUAD, 8])
        low4 = sb("low4", [P, QUAD, 8])
        top8, keep = sb("top8", [P, QUAD, 8]), sb("keep", [P, QUAD, 10])
        rh = sb("rh", [P, QUAD, R3 + LORA3])
        sel, comb = sb("sel", [P, QUAD, R3]), sb("comb", [P, QUAD, R3])
        nmax, tot, rec = sb("nmax", [P, QUAD]), sb("tot", [P, QUAD]), sb("rec", [P, QUAD])
        hs, hsT = sb("hs", [P, QUAD, LORA3]), sb("hsT", [LORA3, QUAD, P])
        banks = Banks(nc, ctx, w, "lf", plan)
        stats_ready, rstd_ready, xn_ready = signal("stats_ready", 4), signal("rstd_ready", 4), signal("xn_ready", 4)
        xT_high, logit_ready, expo_ready = signal("xT_high", 4), signal("logit_ready", 4), signal("expo_ready", 4)
        stored, hs_ready = signal("stored", 4, 16), signal("hs_ready", 4)
        dve_step = new_semaphore(nc, w, "lf_dve_step")
        pool_step = new_semaphore(nc, w, "lf_pool_step")
        pads = new_semaphore(nc, w, "lf_pads")
        block = ctx.enter_context(nc.Block())

        @block.sync
        def _(sp):
            with sp.Fori(0, TURNS) as turn:
                for j in range(QUAD):
                    banks.wait_drained(sp, turn, "out", j)
                    stored.send(sp.dma_start(io["out"][bass.ts(turn * QUAD + j, P), :], xout[:, j, :]))
            sp.wait_ge(stored.sem, TURNS * QUAD * 16)

        @block.gpsimd
        def _(pool):
            pool.memset(e[:, :, :], NEVER).then_inc(pads, 1)
            pool.memset(pick[:, :, :], NEVER).then_inc(pads, 1)
            pool.memset(low4[:, :, :], 0.0).then_inc(pads, 1)
            with pool.Fori(0, TURNS) as turn:
                for j in range(QUAD):
                    stats_ready.wait(pool, turn, j)
                    pool.tensor_tensor(vare[:, j:j + 1], mv[:, j, 1:2], w["eps"][:, :], ALU.add)\
                        .then_inc(pool_step, 1)
                    pool.wait_ge(pool_step, turn * QUAD + (j + 1))
                    rstd_ready.send(pool.tensor_tensor(rstd[:, j:j + 1], vare[:, j:j + 1], w["power"][:, 0:1],
                                                       ALU.pow))

        @block.tensor
        def _(pe):
            apart = Apart(pe, pads, 3)
            with pe.Fori(0, TURNS) as turn:
                for j in range(QUAD):
                    xn_ready.wait(pe, turn, j)
                    banks.wait_free(pe, turn, "turn", j)
                    for c in range(C):
                        last = pe.transpose(banks.bank("turn", j)[:, c * P:(c + 1) * P],
                                            xn[:, j, c * P:(c + 1) * P], w["ident"][:, :])
                    banks.fill(last, "turn", j)
                for j in range(QUAD):
                    banks.wait_drained(pe, turn, "turn", j)
                    banks.wait_free(pe, turn, "route", j)
                    banks.fill(three(pe, banks.bank("route", j)[:, 0:R3 + LORA3],
                                     [xTh[:, j, c, :] for c in range(C)], [xTl[:, j, c, :] for c in range(C)],
                                     [w["R3h"][:, c, :] for c in range(C)], [w["R3l"][:, c, :] for c in range(C)]),
                               "route", j)
                for j in range(QUAD):
                    hs_ready.wait(pe, turn, j)
                    banks.wait_free(apart, turn, "hturn", j)
                    banks.fill(pe.transpose(banks.bank("hturn", j)[0:LORA3, 0:P], hs[:, j, :], w["ident"][:, :]),
                               "hturn", j)
                    banks.wait_drained(pe, turn, "hturn", j)
                    banks.wait_free(pe, turn, "out", j)
                    banks.fill(pe.matmul(banks.bank("out", j), hsT[:, j, :], w["B3"][:, :], start=True, stop=True),
                               "out", j)

        @block.scalar
        def _(act):
            act.wait_ge(pads, 3)
            with act.Fori(0, TURNS) as turn:
                for j in range(QUAD):
                    banks.wait_filled(act, turn, "turn", j)
                    xT_high.send(act.activation(xTh[:, j, :, :].rearrange("p c n -> p (c n)"), banks.bank("turn", j),
                                                ACT.Copy))
                for j in range(QUAD):
                    banks.wait_filled(act, turn, "route", j)
                    banks.drain(act.activation(rh[:, j, :], banks.bank("route", j)[:, 0:R3 + LORA3], ACT.Copy),
                                "route", j)
                for j in range(QUAD):
                    logit_ready.wait(act, turn, j)
                    expo_ready.send(act.activation(e[:, j, 0:R3], rh[:, j, 0:R3], ACT.Exp, bias=nmax[:, j:j + 1]))
                for j in range(QUAD):
                    banks.wait_filled(act, turn, "hturn", j)
                    banks.drain(act.activation(hsT[:, j, :], banks.bank("hturn", j)[0:LORA3, 0:P], ACT.Copy),
                                "hturn", j)

        @block.vector
        def _(dve):
            apart = Apart(dve, pads, 3)
            dve.wait_ge(pads, 3)
            with dve.Fori(0, TURNS) as turn:
                st = Steps(dve, dve_step, FFN_STEPS, turn)

                def each(make, after=None):
                    made = []
                    for j in range(QUAD):
                        if after:
                            st.after(after[j], apart)
                        made.append(st.step(make(j)))
                    return made

                def x_of(j):
                    return w["X"][:, bass.ds(turn * QUAD + j, 1), :]
                got = each(lambda j: dve.bn_stats(stats[:, j, :], x_of(j)))
                for j in range(QUAD):
                    st.after(got[j], apart)
                    stats_ready.send(dve.bn_aggr(mv[:, j, :], stats[:, j, :]))
                for j in range(QUAD):
                    rstd_ready.wait(dve, turn, j)
                    xn_ready.send(dve.tensor_scalar(xn[:, j, :], x_of(j), mv[:, j, 0:1], rstd[:, j:j + 1],
                                                    ALU.subtract, ALU.mult))
                for j in range(QUAD):
                    xT_high.wait(dve, turn, j)
                    banks.drain(dve.tensor_tensor(xTl[:, j, :, :].rearrange("p c n -> p (c n)"),
                                                  banks.bank("turn", j),
                                                  xTh[:, j, :, :].rearrange("p c n -> p (c n)"), ALU.subtract),
                                "turn", j)

                for j in range(QUAD):
                    banks.wait_drained(dve, turn, "route", j)
                    logit_ready.send(dve.tensor_reduce(nmax[:, j:j + 1], rh[:, j, 0:R3], AX.X, ALU.max, negate=True))

                def copy4(j):
                    expo_ready.wait(dve, turn, j)
                    return dve.tensor_copy(low4[:, j, 0:R3], e[:, j, 0:R3])
                got = each(copy4)
                got = each(lambda j: dve.max(top8[:, j, :], low4[:, j, :]), got)
                each(lambda j: dve.tensor_tensor(tot[:, j:j + 1], top8[:, j, 0:1], top8[:, j, 1:2], ALU.add), got)
                got = each(lambda j: dve.tensor_copy(pick[:, j, 0:2], top8[:, j, 0:2]), got)
                got = each(lambda j: dve.reciprocal(rec[:, j:j + 1], tot[:, j:j + 1]), got)
                got = each(lambda j: dve.match_replace(keep[:, j, :], pick[:, j, :], e[:, j, :], 0.0), got)
                got = each(lambda j: dve.tensor_tensor(sel[:, j, :], e[:, j, 0:R3], keep[:, j, 0:R3],
                                                       ALU.subtract), got)
                got = each(lambda j: dve.tensor_scalar(comb[:, j, :], sel[:, j, :], rec[:, j:j + 1], 4.0,
                                                       ALU.mult, ALU.mult), got)
                for j in range(QUAD):
                    st.after(got[j])
                    hs_ready.send(dve.tensor_tensor(
                        hs[:, j, :].rearrange("p (e r) -> p e r", r=RANK),
                        rh[:, j, R3:R3 + LORA3].rearrange("p (e r) -> p e r", r=RANK),
                        comb[:, j, :].unsqueeze(2).to_broadcast([P, E3, RANK]), ALU.mult))
                for j in range(QUAD):
                    banks.wait_filled(dve, turn, "out", j)
                    dve.wait_ge(stored.sem, turn * (QUAD * 16))
                    banks.drain(dve.scalar_tensor_tensor(
                        out=xout[:, j, :].unsqueeze(1), in0=banks.bank("out", j).unsqueeze(1),
                        scalar=w["gates"][:, 7:8], in1=x_of(j), op0=ALU.mult, op1=ALU.add), "out", j)
                st.close()


def build(nc, io):
    with ExitStack() as whole:
        def keep(stack, name, shape, dt=F32):
            w[name] = stack.enter_context(nc.sbuf_tensor("w_" + name, shape, dt))

        w = {}
        for name, shape, dt in (("gates", [P, 8], F32), ("ident", [P, P], F32), ("identh", [P, P], BF16),
                                ("power", [P, 1], F32), ("eps", [P, 1], F32), ("R3h", [P, C, R3 + LORA3], HALF),
                                ("R3l", [P, C, R3 + LORA3], HALF), ("B3", [LORA3, D], F32)):
            keep(whole, name, shape, dt)
        io["x_mid"] = nc.dram_tensor("x_mid", (TOKENS, D), F32).ap()
        with ExitStack() as early:
            for name, cols in (("M", D), ("W0", D), ("W1", D), ("R0", R0 + LORA), ("R1", R1 + LORA), ("Wqd", 64),
                               ("Wkv", P)):
                for half in "hl":
                    keep(early, name + half, [P, C, cols], HALF)
            for name, shape, dt in (
                    ("ch", [P, C], HALF), ("cl", [P, C], HALF), ("r", [P, C], F32), ("s", [P, 1], F32),
                    ("bdmask", [P, P], F32), ("B0", [LORA, D], F32), ("B1", [LORA, D], F32),
                    ("L1W", [P, 4, P], F32), ("L1b", [P, 4], F32), ("rb1", [P, R1], F32),
                    ("route_to", [P, E01, R1], F32), ("expert_id", [P, E01, R1], F32), ("gbias", [P, 3, D], F32),
                    ("Wqk", [64, D], F32), ("Wvu", [L2K, D], F32), ("quarter", [P, 4], F32),
                    ("gate2", [P, C, E01], F32), ("ics", [E01, D], F32), ("ocs", [E01, D], F32),
                    ("sign2", [P, C, D], BF16)):
                keep(early, name, shape, dt)
            with stage(nc, w):
                prepare_weights(nc, io, w)
            with stage(nc, w):
                early_layers(nc, io, w)
        keep(whole, "X", [P, TILES, D])
        with ExitStack() as attention:
            for name in ("xTh", "xTl", "cTh", "cTl"):
                keep(attention, name, [P, C, TOKENS], HALF)
            keep(attention, "cos", [P, TOKENS])
            keep(attention, "sin", [P, TOKENS])
            keep(attention, "mask", [P, TILES, SEQ], BF16)
            with stage(nc, w):
                prepare_last(nc, io, w)
            with stage(nc, w):
                last_attention(nc, io, w)
        with stage(nc, w):
            last_ffn(nc, io, w)


def rope_tables():
    inv = (1.0 / np.float32(10000.0) ** (np.arange(0, HD, 2, dtype=np.float32) / np.float32(HD))).astype(np.float32)
    angle = np.arange(POSITIONS, dtype=np.float32)[:, None] * inv[None, :]
    cos, sin = np.cos(angle).astype(np.float32), np.sin(angle).astype(np.float32)
    return np.concatenate([cos, cos], 1), np.concatenate([sin, -sin], 1)


def layout(i):
    a = {k: np.asarray(v) for k, v in i.items()}
    cos, sin = rope_tables()
    two = (TOKENS, D)
    return {
        "x": a["x"].reshape(two), "ctx": a["ctx_4096"].reshape(two), "ctxT": a["ctx_4096"].reshape(two).T,
        "pos": a["pos_BxS2"].reshape(TOKENS), "mask": a["mask_BxSxS2_ik0"].reshape(TOKENS, SEQ),
        "gates": np.concatenate([a["g_xattn"], a["g_ffn"]]),
        "L0_Wq": a["L0_xattn_Wq"], "L0_Wk": a["L0_xattn_Wk"],
        "L0_bq": a["L0_xattn_bq"].reshape(C, P).T, "L0_bk": a["L0_xattn_bk"].reshape(C, P).T,
        "W0": a["L0_ffn_W_base"].T, "b0": a["L0_ffn_b_base"],
        "R0": np.concatenate([a["L0_ffn_W_router"], a["L0_ffn_A_stack"].reshape(LORA, D)]).T,
        "B0": a["L0_ffn_B_stack"].transpose(0, 2, 1).reshape(LORA, D),
        "L1W": np.stack([a["L1_xattn_" + n].T for n in ("Wq", "Wk", "Wv", "Wo")]),
        "L1b": np.stack([a["L1_xattn_" + n].reshape(SEQ, 1) for n in ("bq", "bk", "bv", "bo")]),
        "W1": a["L1_ffn_base_W"].T, "b1": a["L1_ffn_base_b"], "rb1": a["L1_ffn_router_b"],
        "R1": np.concatenate([a["L1_ffn_router_W"], a["L1_ffn_A"].reshape(LORA, D)]).T,
        "B1": a["L1_ffn_B"].transpose(0, 2, 1).reshape(LORA, D), "emap": a["L1_ffn_expert_map"],
        "Wqd": a["L2_xattn_Wq_d"], "Wkv": np.tile(a["L2_xattn_Wkv_d"], (1, 4)), "Wqk": a["L2_xattn_W_qk"],
        "Wvu": a["L2_xattn_Wv_u"].reshape(L2K, 8, 2, 32).transpose(0, 2, 1, 3).reshape(L2K, D),
        "W2": a["L2_ffn_weight"].T, "b2": a["L2_ffn_bias"], "gate2": a["L2_ffn_gate_w"].T,
        "ics": a["L2_ffn_in_channel_scale"], "ocs": a["L2_ffn_out_channel_scale"],
        "Wq3": a["L3_xattn_Wq"], "Wk3": a["L3_xattn_Wk"], "Wv3": a["L3_xattn_Wv"], "Wo3": a["L3_xattn_Wo"],
        "R3": np.concatenate([a["L3_ffn_Wr"], a["L3_ffn_A"].reshape(LORA3, D)]).T,
        "B3": a["L3_ffn_B"].transpose(0, 2, 1).reshape(LORA3, D),
        "cos": cos, "sin": sin,
    }


def kernel(**inputs):
    import concourse.bacc as bacc
    from concourse.bass_utils import run_bass_kernel_spmd

    nc = bacc.Bacc("TRN2", target_bir_lowering=False, num_devices=1)
    arrays, io = {}, {}
    for name, a in layout(inputs).items():
        a = np.ascontiguousarray(a)
        arrays["in_" + name] = a
        io[name] = nc.dram_tensor("in_" + name, a.shape, mybir.dt.from_np(a.dtype), kind="ExternalInput").ap()
    io["out"] = nc.dram_tensor("out_0", (TOKENS, D), F32, kind="ExternalOutput").ap()
    build(nc, io)
    result = run_bass_kernel_spmd(nc, [arrays], core_ids=[0])
    return result.results[0]["out_0"].reshape(BATCH, SEQ, D)
```

```python
from contextlib import ExitStack, contextmanager

import numpy as np

import concourse.bass as bass
from concourse import mybir

F32 = mybir.dt.float32
I32 = mybir.dt.int32
HALF = mybir.dt.bfloat16
BF16 = mybir.dt.bfloat16
ALU = mybir.AluOpType
ACT = mybir.ActivationFunctionType
AX = mybir.AxisListType

P = 128
D = 512
C = D // P
SEQ = 64
BATCH = 32
TOKENS = BATCH * SEQ
TILES = TOKENS // P
QUAD = 4
TURNS = TILES // QUAD
EPS = 1e-5

R0, R1, R3 = 8, 15, 4
E01, RANK, E3 = 8, 16, 4
LORA, LORA3 = E01 * RANK, E3 * RANK

WIN, CH, TC = 16, 8, 8
TP = D // TC
PADDED = 8 + D + 8
HALO = TP + WIN

H2, L2K = 16, 32
KV, GROUP, HD = 8, 4, 128
POSITIONS = 512
MASKED = -float(2.0 ** 100)
NEVER = 4.0


def new_semaphore(nc, w, name):
    handle = w["stack"].enter_context(nc.semaphore(name))
    w["semaphores"].append(handle)
    return handle


@contextmanager
def stage(nc, w):
    with ExitStack() as stack:
        w["stack"], w["semaphores"] = stack, []
        yield
        for handle in w["semaphores"]:
            nc.gpsimd.sem_clear(handle)
        nc.all_engine_barrier()


def prepare_weights(nc, io, w):
    with ExitStack() as ctx:
        def sb(name, shape, dt=F32):
            return ctx.enter_context(nc.sbuf_tensor("prep_" + name, shape, dt))

        def sem(name):
            return new_semaphore(nc, w, "prep_" + name)

        raw = {}
        for name, cols in (("W0", D), ("W1", D), ("W2", D), ("R0", R0 + LORA), ("R1", R1 + LORA),
                           ("Wqd", 64), ("Wkv", P), ("R3", R3 + LORA3)):
            raw[name] = sb(name, [P, C, cols])
        wq, wk = sb("Wq", [P, C, D]), sb("Wk", [P, C, D])
        bq, bk = sb("bq", [P, C]), sb("bk", [P, C])
        gates_raw = sb("gates", [P, 8])
        bias_raw = sb("bias", [P, 3, D])
        emap, emap_f = sb("emap", [P, R1], I32), sb("emap_f", [P, R1])
        negative = sb("negative", [P, C, D])
        eight = sb("eight", [P, E01])
        ps = ctx.enter_context(nc.psum_tensor("prep_ps", [P, 8, D], F32))
        loaded, zeroed, made, product_ready = sem("loaded"), sem("zeroed"), sem("made"), sem("product_ready")
        split_high, pool_step, gate_ready = sem("split_high"), sem("pool_step"), sem("gate_ready")
        direct, folded = sem("direct"), sem("folded")

        RAW = [("W0", "W0"), ("R0", "R0"), ("W1", "W1"), ("R1", "R1"), ("Wqd", "Wqd"), ("Wkv", "Wkv"),
               ("R3", "R3")]
        FIRST = 5 * 16
        block = ctx.enter_context(nc.Block())

        @block.sync
        def _(sp):
            sp.dma_start(wq[:, :, :], io["L0_Wq"].rearrange("(c p) n -> p c n", p=P)).then_inc(loaded, 16)
            sp.dma_start(wk[:, :, :], io["L0_Wk"].rearrange("(c p) n -> p c n", p=P)).then_inc(loaded, 16)
            sp.dma_start(bq[:, :], io["L0_bq"]).then_inc(loaded, 16)
            sp.dma_start(bk[:, :], io["L0_bk"]).then_inc(loaded, 16)
            sp.dma_start(gates_raw[:, :], io["gates"].partition_broadcast(P)).then_inc(loaded, 16)
            sp.wait_ge(loaded, FIRST)
            n = FIRST
            for dst, src in RAW + [("W2", "W2")]:
                sp.dma_start(raw[dst][:, :, :], io[src].rearrange("(c p) n -> p c n", p=P)).then_inc(loaded, 16)
                n += 16
                sp.wait_ge(loaded, n)
            for k, name in enumerate(("b0", "b1", "b2")):
                sp.dma_start(bias_raw[:, k, :], io[name].partition_broadcast(P)).then_inc(loaded, 16)
            sp.dma_start(emap[:, :], io["emap"].partition_broadcast(P)).then_inc(loaded, 16)
            for name in ("B0", "B1", "Wqk", "Wvu", "ics", "ocs", "B3"):
                sp.dma_start(w[name][:, :], io[name]).then_inc(direct, 16)
            sp.dma_start(w["gate2"][:, :, :], io["gate2"].rearrange("(c p) n -> p c n", p=P)).then_inc(direct, 16)
            sp.dma_start(w["rb1"][:, :], io["rb1"].partition_broadcast(P)).then_inc(direct, 16)
            sp.wait_ge(zeroed, 1)
            for k in range(4):
                for b in range(2):
                    sp.dma_start(w["L1W"][SEQ * b:SEQ * b + SEQ, k, SEQ * b:SEQ * b + SEQ],
                                 io["L1W"][k]).then_inc(direct, 16)
                    sp.dma_start(w["L1b"][SEQ * b:SEQ * b + SEQ, k:k + 1], io["L1b"][k]).then_inc(direct, 16)
            sp.wait_ge(direct, 16 * (9 + 16))

        @block.gpsimd
        def _(pool):
            st = Steps(pool, pool_step, 12, 0)
            st.link(pool.memset(w["ident"][:, :], 0.0))
            st.link(pool.memset(w["bdmask"][:, :], MASKED))
            st.link(pool.memset(w["power"][:, :], -0.5))
            st.link(pool.memset(w["eps"][:, :], EPS))
            st.link(pool.memset(w["quarter"][:, :], 1.0))
            st.link(pool.iota(w["expert_id"][:, :, :], pattern=[[1, E01], [0, R1]], base=0, channel_multiplier=0,
                              allow_small_or_imprecise_dtypes=True))
            st.link(pool.affine_select(out=w["ident"][:, :], in_=w["ident"][:, :], compare_op=ALU.not_equal,
                                       fill=1.0, base=0, pattern=[[-1, P]], channel_multiplier=1))
            for b in range(2):
                rows = w["bdmask"][SEQ * b:SEQ * b + SEQ, SEQ * b:SEQ * b + SEQ]
                st.link(pool.memset(rows, 0.0))
            st.link(pool.affine_select(out=w["quarter"][:, :], in_=w["quarter"][:, :], compare_op=ALU.is_ge,
                                       fill=0.0, base=0, pattern=[[-L2K, 4]], channel_multiplier=1))
            st.link(pool.affine_select(out=w["quarter"][:, :], in_=w["quarter"][:, :], compare_op=ALU.is_ge,
                                       fill=0.0, base=L2K - 1, pattern=[[L2K, 4]], channel_multiplier=-1))
            st.link(pool.tensor_copy(w["identh"][:, :], w["ident"][:, :]))
            st.close()

        @block.tensor
        def _(pe):
            pe.wait_ge(loaded, FIRST)
            for m in range(C):
                for c in range(C):
                    last = pe.matmul(ps[:, m, :], wq[:, c, m * P:(m + 1) * P], wk[:, c, :],
                                     start=(c == 0), stop=(c == C - 1))
                last.then_inc(product_ready, 1)
            for m in range(C):
                for c in range(C):
                    pe.matmul(ps[:, 4, m:m + 1], wk[:, c, m * P:(m + 1) * P], bq[:, c:c + 1],
                              start=(c == 0), stop=(c == C - 1))
            for m in range(C):
                for c in range(C):
                    pe.matmul(ps[:, 5, m:m + 1], wq[:, c, m * P:(m + 1) * P], bk[:, c:c + 1],
                              start=(c == 0), stop=(c == C - 1))
            for c in range(C):
                last = pe.matmul(ps[:, 6, 0:1], bq[:, c:c + 1].to_broadcast([P, P]), bk[:, c:c + 1],
                                 start=(c == 0), stop=(c == C - 1))
            last.then_inc(product_ready, 1)

        @block.scalar
        def _(act):
            act.wait_ge(loaded, FIRST)
            act.activation(w["gates"][:, :], gates_raw[:, :], ACT.Tanh).then_inc(gate_ready, 1)
            for m in range(C):
                act.wait_ge(product_ready, m + 1)
                act.activation(w["Mh"][:, m, :], ps[:, m, :], ACT.Copy).then_inc(split_high, 1)
            act.wait_ge(product_ready, C + 1)
            act.activation(w["ch"][:, :], ps[:, 5, 0:C], ACT.Copy).then_inc(split_high, 1)
            for k, (name, _) in enumerate(RAW):
                act.wait_ge(loaded, FIRST + 16 * (k + 1))
                act.activation(w[name + "h"][:, :, :], raw[name][:, :, :], ACT.Copy).then_inc(split_high, 1)

        @block.vector
        def _(dve):
            dve.memset(w["L1W"][:, :, :], 0.0).then_inc(zeroed, 1)
            for m in range(C):
                dve.wait_ge(split_high, m + 1)
                dve.tensor_tensor(w["Ml"][:, m, :], ps[:, m, :], w["Mh"][:, m, :], ALU.subtract)
            dve.wait_ge(split_high, C + 1)
            dve.tensor_tensor(w["cl"][:, :], ps[:, 5, 0:C], w["ch"][:, :], ALU.subtract)
            dve.tensor_copy(w["r"][:, :], ps[:, 4, 0:C])
            dve.tensor_copy(w["s"][:, :], ps[:, 6, 0:1])
            for k, (name, _) in enumerate(RAW):
                dve.wait_ge(split_high, C + 2 + k)
                dve.tensor_tensor(w[name + "l"][:, :, :], raw[name][:, :, :], w[name + "h"][:, :, :], ALU.subtract)
            dve.wait_ge(loaded, FIRST + 16 * (len(RAW) + 1))
            dve.tensor_scalar(negative[:, :, :], raw["W2"][:, :, :], 0.0, None, ALU.is_lt).then_inc(made, 1)
            dve.wait_ge(made, 1)
            dve.scalar_tensor_tensor(out=w["sign2"][:, :, :], in0=raw["W2"][:, :, :], scalar=0.0,
                                     in1=negative[:, :, :], op0=ALU.is_gt, op1=ALU.subtract)
            dve.wait_ge(gate_ready, 1)
            dve.wait_ge(loaded, FIRST + 16 * (len(RAW) + 5))
            for k in range(3):
                dve.tensor_scalar(w["gbias"][:, k, :], bias_raw[:, k, :], w["gates"][:, 4 + k:5 + k], None,
                                  ALU.mult)
            dve.tensor_copy(emap_f[:, :], emap[:, :]).then_inc(made, 1)
            dve.wait_ge(made, 2)
            dve.wait_ge(pool_step, 6)
            dve.tensor_tensor(w["route_to"][:, :, :], w["expert_id"][:, :, :],
                              emap_f[:, :].unsqueeze(1).to_broadcast([P, E01, R1]), ALU.is_equal)


class Banks:

    def __init__(self, nc, ctx, w, prefix, plan, before=()):
        used = sorted({bank for _, bank in plan})
        self.filled = {b: new_semaphore(nc, w, f"{prefix}_filled{b}") for b in used}
        self.drained = {b: new_semaphore(nc, w, f"{prefix}_drained{b}") for b in used}
        self.ps = ctx.enter_context(nc.psum_tensor(f"{prefix}_ps", [P, 8, D], F32))
        self.at, self.uses = {}, [0] * 8
        self.before = [0] * 8
        for step, bank in before:
            self.at[step] = (bank, self.before[bank])
            self.before[bank] += 1
        for step, bank in plan:
            self.at[step] = (bank, self.before[bank] + self.uses[bank])
            self.uses[bank] += 1

    def open(self, pool):
        for b in self.filled:
            pool.sem_inc(self.filled[b], 1)
            pool.sem_inc(self.drained[b], 1)

    def bank(self, *step):
        return self.ps[:, self.at[step][0], :]

    def wait_free(self, eng, turn, *step):
        b, k = self.at[step]
        eng.wait_ge(self.drained[b], turn * self.uses[b] + (k + 1))

    def wait_filled(self, eng, turn, *step):
        b, k = self.at[step]
        eng.wait_ge(self.filled[b], turn * self.uses[b] + (k + 2))

    def wait_drained(self, eng, turn, *step):
        b, k = self.at[step]
        eng.wait_ge(self.drained[b], turn * self.uses[b] + (k + 2))

    def wait_all_drained(self, eng, turn, b):
        eng.wait_ge(self.drained[b], turn * self.uses[b] + (self.before[b] + 1))

    def wait_all_filled(self, eng, turn, b):
        eng.wait_ge(self.filled[b], turn * self.uses[b] + (self.before[b] + 1))

    def fill(self, ins, *step):
        ins.then_inc(self.filled[self.at[step][0]], 1)

    def drain(self, ins, *step):
        ins.then_inc(self.drained[self.at[step][0]], 1)


class Signal:

    def __init__(self, nc, w, name, per_turn, by=1):
        self.sem, self.per_turn, self.by = new_semaphore(nc, w, name), per_turn, by

    def send(self, ins):
        ins.then_inc(self.sem, self.by)

    def wait(self, eng, turn, k):
        eng.wait_ge(self.sem, turn * (self.per_turn * self.by) + (k + 1) * self.by)


class Steps:

    def __init__(self, eng, sem, per_turn, turn):
        self.eng, self.sem, self.per_turn, self.turn, self.n = eng, sem, per_turn, turn, 0

    def step(self, ins):
        self.n += 1
        ins.then_inc(self.sem, 1)
        return self.n

    def after(self, n, eng=None):
        (eng or self.eng).wait_ge(self.sem, self.turn * self.per_turn + n)

    def link(self, ins):
        self.after(self.step(ins))

    def close(self):
        assert self.n == self.per_turn, ("steps of a turn", self.n)


def three(pe, out, lh, ll, rh, rl, first=True, last=True):
    n = len(lh)
    for c in range(n):
        pe.matmul(out, lh[c], rh[c], start=(first and c == 0), stop=False)
        pe.matmul(out, lh[c], rl[c], start=False, stop=False)
        ins = pe.matmul(out, ll[c], rh[c], start=False, stop=(last and c == n - 1))
    return ins


class Apart:

    def __init__(self, eng, once, n):
        self.eng, self.once, self.n = eng, once, n

    def wait_ge(self, sem, value):
        with self.eng.register() as held:
            self.eng.reg_alu(held, value, 0, ALU.max)
            self.eng.wait_ge(self.once, self.n)
            self.eng.wait_ge(sem, held)


DVE_STEPS, LAST_STEPS, FFN_STEPS = 156, 32, 36


def early_layers(nc, io, w):
    plan = []
    for j in range(QUAD):
        plan.append((("turn", 0, j), j % 2))
    for j in range(QUAD):
        plan.append((("proj0", j), 2 + j % 2))
    for j in range(QUAD):
        plan.append((("score0", j), j % 2))
    for j in range(QUAD):
        plan.append((("prob0", j), 2 + j % 2))
        plan.append((("out0", j), 4 + j))
    for f, layer in ((0, 1), (1, 3)):
        if f == 1:
            for j in range(QUAD):
                plan += [(("q1", j), 0), (("k1", j), 1), (("v1", j), 2)]
            for j in range(QUAD):
                plan += [(("dot1", j, 0), 4 + 2 * (j % 2)), (("dot1", j, 1), 5 + 2 * (j % 2)), (("out1", j), 3)]
        for j in range(QUAD):
            plan.append((("turn", layer, j), j % 2))
        for j in range(QUAD):
            plan += [(("route", f, j), 2 + j % 2), (("base", f, j), 4 + j)]
        for j in range(QUAD):
            plan.append((("hturn", f, j), j % 2))
    for j in range(QUAD):
        plan.append((("turn", 4, j), j % 2))
    for j in range(QUAD + 1):
        if j < QUAD:
            plan += [(("low2", j), 2), (("qup2", j), 3), (("vup2", j), 4)]
            plan += [(("score2", j, 0), 6), (("score2", j, 1), 7)]
        if j >= 1:
            plan += [(("prob2", j - 1, 0), 0), (("prob2", j - 1, 1), 1)]
            plan += [(("out2", j - 1, 0), 5), (("out2", j - 1, 1), 4)]
    for j in range(QUAD):
        plan.append((("turn", 5, j), j % 2))
    for j in range(QUAD):
        plan.append((("gate2", j), 2 + j % 2))
    for j in range(QUAD):
        plan += [(("gturn", j), (0, 1, 3, 2)[j]), (("scale_in", j), 4 + j % 2), (("scale_out", j), 6 + j % 2)]
    for j in range(QUAD):
        plan.append((("sign2", j), 2 + j % 2))

    with ExitStack() as ctx:
        def sb(name, shape, dt=F32, stack=ctx):
            return stack.enter_context(nc.sbuf_tensor("early_" + name, shape, dt))

        def signal(name, per_turn, by=1):
            return Signal(nc, w, "early_" + name, per_turn, by)

        xq, xn = sb("xq", [P, QUAD, D]), sb("xn", [P, QUAD, D])
        ctxt = sb("ctxt", [P, QUAD, D])
        cTh, cTl = sb("cTh", [P, QUAD, C, P], HALF), sb("cTl", [P, QUAD, C, P], HALF)
        stats, mv, rstd = sb("stats", [P, QUAD, 6]), sb("mv", [P, QUAD, 2]), sb("rstd", [P, QUAD])
        vare = sb("vare", [P, QUAD])
        u = sb("u", [P, QUAD])
        nmax, tot, rec = sb("nmax", [P, QUAD]), sb("tot", [P, QUAD]), sb("rec", [P, QUAD])
        rh = sb("rh", [P, QUAD, R1 + LORA])
        rkeep, rsel = sb("rkeep", [P, QUAD, 16]), sb("rsel", [P, QUAD, 16])
        e0, e1, e2 = sb("e0", [P, QUAD, 14]), sb("e1", [P, QUAD, R1]), sb("e2", [P, QUAD, E01])
        top8, pick0 = sb("top8", [P, QUAD, 8]), sb("pick0", [P, QUAD, 8])
        rmix = sb("rmix", [P, QUAD, E01, R1])
        comb = sb("comb", [P, QUAD, E01])
        hs, hsT = sb("hs", [P, QUAD, LORA]), sb("hsT", [P, QUAD, P])
        kp, vp = sb("kp", [P, 2, PADDED]), sb("vp", [P, 2, PADDED])
        with ExitStack() as mine:
            qs = sb("qs", [P, 2, D], stack=mine)
            qL = sb("qL", [P, 2, CH, TP], stack=mine)
            kL, vL = sb("kL", [P, 2, CH, HALO], stack=mine), sb("vL", [P, 2, CH, HALO], stack=mine)
            qk = [sb(f"qk{h}", [P, CH, TP // 2, WIN], stack=mine) for h in range(2)]
            pv = [sb(f"pv{h}", [P, CH, TP // 2, WIN], stack=mine) for h in range(2)]
            ee, mx1 = sb("ee", [P, TP, WIN], stack=mine), sb("mx1", [P, TP], stack=mine)
            sum1, rec1 = sb("sum1", [P, TP], stack=mine), sb("rec1", [P, TP], stack=mine)
            oL, oS = sb("oL", [P, 2, CH, TP], stack=mine), sb("oS", [P, 2, D], stack=mine)
            y1 = xn
        xin = sb("xin", [P, QUAD, D])
        cT = sb("cT", [P, QUAD, C, P])
        xTh, xTl = sb("xTh", [P, QUAD, C, P], HALF), sb("xTl", [P, QUAD, C, P], HALF)
        sm, pr, prT = sb("sm", [P, QUAD, P]), sb("pr", [P, QUAD, P]), sb("prT", [P, QUAD, P])
        aT = sb("aT", [P, 2, C, P])
        aTh, aTl = sb("aTh", [P, QUAD, C, P], HALF), sb("aTl", [P, QUAD, C, P], HALF)
        cqT, ckv = sb("cqT", [64, 2, P]), sb("ckv", [P, 2, 2, 4, SEQ])
        qT2, v2 = sb("qT2", [P, 2, 4, P]), sb("v2", [P, 2, 2, 256])
        s2, p2T = sb("s2", [P, 2, H2, SEQ]), sb("p2T", [P, 2, H2 // 2, P])
        mx2, sum2, rec2 = sb("mx2", [P, 2, H2]), sb("sum2", [P, 2, H2]), sb("rec2", [P, 2, H2])
        o2 = sb("o2", [P, 2, H2, 32])
        rT2, osb = sb("rT2", [E01, QUAD, P]), sb("osb", [P, QUAD, D])
        xTf = sb("xTf", [P, QUAD, C, P])
        scr_q = nc.dram_tensor("scr_q", (QUAD, TC, P, TP), F32).ap()
        scr_k = nc.dram_tensor("scr_k", (QUAD, TC, P, HALO), F32).ap()
        scr_v = nc.dram_tensor("scr_v", (QUAD, TC, P, HALO), F32).ap()
        scr_o = nc.dram_tensor("scr_o", (QUAD, P, CH * TP), F32).ap()

        banks = Banks(nc, ctx, w, "early", plan)
        x_loaded = [signal(f"x_loaded{j}", 1, 16) for j in range(QUAD)]
        ctx_loaded = [signal(f"ctx_loaded{j}", 1, 16) for j in range(QUAD)]
        cT_loaded = [signal(f"cT_loaded{j}", 1, 16) for j in range(QUAD)]
        cT_high, cT_split = signal("cT_high", QUAD), signal("cT_split", QUAD)
        stats_ready, rstd_ready, xn_ready = signal("stats_ready", 24), signal("rstd_ready", 24), signal("xn_ready", 24)
        xT_high = signal("xT_high", 16)
        aT_ready, aT_high, aT_split = signal("aT_ready", 4), signal("aT_high", 4), signal("aT_split", 4)
        sm0_ready, pr0_ready, tot0_ready = signal("sm0_ready", 4), signal("pr0_ready", 4), signal("tot0_ready", 4)
        logit_ready, expo_ready = signal("logit_ready", 12), signal("expo_ready", 12)
        xbias_ready, hs_ready = signal("xbias_ready", 12), signal("hs_ready", 8)
        qkv_written = signal("qkv_written", 4, 48)
        qkv_in = [signal(f"qkv_in{p}", 2, 48) for p in range(2)]
        qk_dve, qk_pool, pv_pool = signal("qk_dve", 4), signal("qk_pool", 4), signal("pv_pool", 4)
        exp1_ready = signal("exp1_ready", 4)
        oL_ready, o_written = signal("oL_ready", 4), signal("o_written", 4, 16)
        oS_in = [signal(f"oS_in{p}", 2, 16) for p in range(2)]
        y1_ready = signal("y1_ready", 4)
        cq_ready = signal("cq_ready", 4)
        exp2_ready = signal("exp2_ready", 4)
        route2_ready, rT2_ready = signal("route2_ready", 4), signal("rT2_ready", 4)
        xTf_ready, y2_ready, y2_high, y2_split = (signal("xTf_ready", 4), signal("y2_ready", 4),
                                                  signal("y2_high", 4), signal("y2_split", 4))
        x_done = signal("x_done", 4)
        stored = signal("stored", 4, 16)
        dve_step, pads = new_semaphore(nc, w, "early_dve_step"), new_semaphore(nc, w, "early_pads")
        pool_step = new_semaphore(nc, w, "early_pool_step")

        def times_q(j, half):
            q = qL[:, j % 2, :, half * (TP // 2):(half + 1) * (TP // 2)]
            return q.unsqueeze(3).to_broadcast([P, CH, TP // 2, WIN])

        def windows(t, j, half):
            a = t[:, j % 2, :, half * (TP // 2):half * (TP // 2) + WIN]
            return bass.AP(a.tensor, a.offset, [list(a.ap[0]), [HALO, CH], [1, TP // 2], [1, WIN]])

        def weights(half):
            e = ee[:, half * (TP // 2):(half + 1) * (TP // 2), :]
            return e.unsqueeze(1).to_broadcast([P, CH, TP // 2, WIN])

        block = ctx.enter_context(nc.Block())

        @block.sync
        def _(sp):
            apart = Apart(sp, pads, 4)
            def load_x(j, tile):
                x_loaded[j].send(sp.dma_start(xin[:, j, :], io["x"][bass.ts(tile, P), :]))

            def load_ctx(j, tile):
                ctx_loaded[j].send(sp.dma_start(ctxt[:, j, :], io["ctx"][bass.ts(tile, P), :]))

            def load_cT(j, tile):
                src = io["ctxT"].rearrange("(c p) n -> p c n", p=P)
                cT_loaded[j].send(sp.dma_start(cT[:, j, :, :], src[:, :, bass.ts(tile, P)]))

            def attention1(turn):
                out_by_channel(turn, 0)
                in_by_time(turn, 0)
                out_by_channel(turn, 1)
                in_by_time(turn, 1)
                out_by_channel(turn, 2)
                for j in range(QUAD):
                    oL_ready.wait(apart, turn, j)
                    if j + 2 < QUAD:
                        in_by_time(turn, j + 2)
                    back(turn, j)
                    if j + 3 < QUAD:
                        out_by_channel(turn, j + 3)

            def store(turn):
                for j in range(QUAD):
                    x_done.wait(apart, turn, j)
                    stored.send(sp.dma_start(io["x_mid"][bass.ts(turn * QUAD + j, P), :], xq[:, j, :]))

            def out_by_channel(turn, j):
                banks.wait_drained(apart, turn, "q1", j)
                banks.wait_drained(sp, turn, "k1", j)
                banks.wait_drained(sp, turn, "v1", j)
                for scr, src, step in ((scr_q, qs, TP), (scr_k, kp, HALO), (scr_v, vp, HALO)):
                    s = src[:, j % 2, :]
                    windows = bass.AP(s.tensor, s.offset, [[s.ap[0][0], P], [TP, TC], [1, step]])
                    sp.dma_start(scr[j].rearrange("c p t -> p c t"), windows).then_inc(qkv_written.sem, 16)

            def in_by_time(turn, j):
                qkv_written.wait(sp, turn, j)
                for scr, dst in ((scr_q, qL), (scr_k, kL), (scr_v, vL)):
                    sp.dma_start(dst[:, j % 2, :, :].rearrange("p d t -> p (d t)"),
                                 scr[j].rearrange("c (g d) t -> (c g) (d t)", d=CH))\
                      .then_inc(qkv_in[j % 2].sem, 16)

            def back(turn, j):
                o_written.send(sp.dma_start(scr_o[j], oL[:, j % 2, :, :].rearrange("p d t -> p (d t)")))
                o_written.wait(sp, turn, j)
                if j >= 2:
                    banks.wait_filled(sp, turn, "out1", j - 2)
                oS_in[j % 2].send(sp.dma_start(
                    oS[:, j % 2, :].rearrange("p (c t) -> p c t", c=TC),
                    scr_o[j].rearrange("(c g) (d t) -> (g d) c t", c=TC, d=CH)))

            sp.wait_ge(pads, 4)
            for j in range(QUAD):
                load_x(j, j)
                load_cT(j, j)
                load_ctx(j, j)
            with sp.Fori(0, TURNS - 1) as turn:
                attention1(turn)
                banks.wait_filled(apart, turn, "out1", QUAD - 1)
                for j in range(QUAD):
                    load_x(j, turn * QUAD + (QUAD + j))
                    load_cT(j, turn * QUAD + (QUAD + j))
                    load_ctx(j, turn * QUAD + (QUAD + j))
                store(turn)
            attention1(TURNS - 1)
            store(TURNS - 1)
            sp.wait_ge(stored.sem, TURNS * QUAD * 16 + 1)

        @block.tensor
        def _(pe):
            apart = Apart(pe, pads, 4)
            ident = w["ident"][:, :]

            def chunks(t, j):
                return [t[:, j, c, :] for c in range(C)]

            def turn_tile(turn, layer, j, src=None):
                xn_ready.wait(pe, turn, 4 * layer + j)
                banks.wait_free(pe, turn, "turn", layer, j)
                out = banks.bank("turn", layer, j)
                for c in range(C):
                    last = pe.transpose(out[:, c * P:(c + 1) * P], xn[:, j, c * P:(c + 1) * P], ident)
                banks.fill(last, "turn", layer, j)

            def lora_ffn(turn, f, layer):
                nr, wname, rname, bname = ((R0, "W0", "R0", "B0"), (R1, "W1", "R1", "B1"))[f]
                for j in range(QUAD):
                    turn_tile(turn, layer, j)
                for j in range(QUAD):
                    banks.wait_drained(pe, turn, "turn", layer, j)
                    banks.wait_free(pe, turn, "route", f, j)
                    n = nr + LORA
                    last = three(pe, banks.bank("route", f, j)[:, 0:n], chunks(xTh, j), chunks(xTl, j),
                                 [w[rname + "h"][:, c, :] for c in range(C)],
                                 [w[rname + "l"][:, c, :] for c in range(C)])
                    banks.fill(last, "route", f, j)
                for j in range(QUAD):
                    banks.wait_free(pe, turn, "base", f, j)
                    three(pe, banks.bank("base", f, j), chunks(xTh, j), chunks(xTl, j),
                          [w[wname + "h"][:, c, :] for c in range(C)],
                          [w[wname + "l"][:, c, :] for c in range(C)], last=False)
                for j in range(QUAD):
                    hs_ready.wait(pe, turn, 4 * f + j)
                    banks.wait_free(pe, turn, "hturn", f, j)
                    banks.fill(pe.transpose(banks.bank("hturn", f, j)[:, 0:P], hs[:, j, :], ident), "hturn", f, j)
                for j in range(QUAD):
                    banks.wait_drained(pe, turn, "hturn", f, j)
                    banks.fill(pe.matmul(banks.bank("base", f, j), hsT[:, j, :], w[bname][:, :],
                                         start=False, stop=True), "base", f, j)

            def attention0(turn):
                for j in range(QUAD):
                    turn_tile(turn, 0, j)
                for j in range(QUAD):
                    banks.wait_drained(pe, turn, "turn", 0, j)
                    banks.wait_free(pe, turn, "proj0", j)
                    out = banks.bank("proj0", j)
                    for m in range(C):
                        last = three(pe, out[:, m * P:(m + 1) * P],
                                     [w["Mh"][:, c, m * P:(m + 1) * P] for c in range(C)],
                                     [w["Ml"][:, c, m * P:(m + 1) * P] for c in range(C)],
                                     chunks(xTh, j), chunks(xTl, j))
                    banks.fill(last, "proj0", j)
                for j in range(QUAD):
                    aT_split.wait(pe, turn, j)
                    cT_split.wait(pe, turn, j)
                    banks.wait_free(pe, turn, "score0", j)
                    out = banks.bank("score0", j)
                    three(pe, out[:, P:P + 1], chunks(xTh, j), chunks(xTl, j),
                          [w["ch"][:, c:c + 1] for c in range(C)], [w["cl"][:, c:c + 1] for c in range(C)])
                    last = three(pe, out[:, 0:P], chunks(aTh, j), chunks(aTl, j), chunks(cTh, j), chunks(cTl, j))
                    banks.fill(last, "score0", j)
                for j in range(QUAD):
                    pr0_ready.wait(pe, turn, j)
                    banks.wait_free(pe, turn, "prob0", j)
                    banks.fill(pe.transpose(banks.bank("prob0", j)[:, 0:P], pr[:, j, :], ident), "prob0", j)
                    banks.wait_drained(pe, turn, "prob0", j)
                    ctx_loaded[j].wait(pe, turn, 0)
                    banks.wait_free(pe, turn, "out0", j)
                    banks.fill(pe.matmul(banks.bank("out0", j), prT[:, j, :], ctxt[:, j, :], start=True, stop=True),
                               "out0", j)

            def attention1(turn):
                for j in range(QUAD):
                    for k, (step, src) in enumerate((("q1", xn), ("k1", ctxt), ("v1", ctxt))):
                        if k == 0:
                            xn_ready.wait(pe, turn, 8 + j)
                        banks.wait_free(pe, turn, step, j)
                        banks.fill(pe.matmul(banks.bank(step, j), w["L1W"][:, k, :], src[:, j, :],
                                             start=True, stop=True), step, j)
                dots1(turn, 0)
                for j in range(QUAD):
                    if j + 1 < QUAD:
                        dots1(turn, j + 1)
                    if j >= 1:
                        out_proj1(turn, j - 1)
                out_proj1(turn, QUAD - 1)

            def dots1(turn, j):
                for h in range(2):
                    (qk_dve, qk_pool)[h].wait(pe, turn, j)
                    banks.wait_free(pe, turn, "dot1", j, h)
                    out = banks.bank("dot1", j, h)
                    for d in range(CH):
                        last = pe.matmul(out, ident, qk[h][:, d, :, :].rearrange("p t w -> p (t w)"),
                                         start=(d == 0), stop=(d == CH - 1))
                    banks.fill(last, "dot1", j, h)

            def out_proj1(turn, j):
                oS_in[j % 2].wait(pe, turn, j // 2)
                banks.wait_free(pe, turn, "out1", j)
                banks.fill(pe.matmul(banks.bank("out1", j), w["L1W"][:, 3, :], oS[:, j % 2, :],
                                     start=True, stop=True), "out1", j)

            def attention2(turn):
                for j in range(QUAD):
                    turn_tile(turn, 4, j)

                def project(j):
                    s = j % 2
                    if j == 0:
                        for jj in range(QUAD):
                            banks.wait_drained(pe, turn, "turn", 4, jj)
                    banks.wait_free(pe, turn, "low2", j)
                    out = banks.bank("low2", j)
                    three(pe, out[0:64, 0:P], [w["Wqdh"][:, c, :] for c in range(C)],
                          [w["Wqdl"][:, c, :] for c in range(C)], chunks(xTh, j), chunks(xTl, j))
                    last = three(pe, out[:, P:2 * P], [w["Wkvh"][:, c, :] for c in range(C)],
                                 [w["Wkvl"][:, c, :] for c in range(C)], chunks(cTh, j), chunks(cTl, j))
                    banks.fill(last, "low2", j)
                    cq_ready.wait(pe, turn, j)
                    banks.wait_free(pe, turn, "qup2", j)
                    for m in range(4):
                        last = pe.matmul(banks.bank("qup2", j)[:, m * P:(m + 1) * P],
                                         w["Wqk"][:, m * P:(m + 1) * P], cqT[:, s, :], start=True, stop=True)
                    banks.fill(last, "qup2", j)
                    banks.wait_drained(pe, turn, "low2", j)
                    banks.wait_free(pe, turn, "vup2", j)
                    for half in range(2):
                        for b in range(2):
                            last = pe.matmul(banks.bank("vup2", j)[SEQ * half:SEQ * half + SEQ, b * 256:(b + 1) * 256],
                                             ckv[0:32, s, b, 0, :], w["Wvu"][:, half * 256:(half + 1) * 256],
                                             start=True, stop=True)
                    banks.fill(last, "vup2", j)
                    banks.wait_drained(pe, turn, "qup2", j)
                    for half in range(2):
                        banks.wait_free(pe, turn, "score2", j, half)
                        for mm in range(2):
                            for b in range(2):
                                last = pe.matmul(
                                    banks.bank("score2", j, half)[SEQ * b:SEQ * b + SEQ, mm * 256:(mm + 1) * 256],
                                    qT2[:, s, 2 * half + mm, SEQ * b:SEQ * b + SEQ],
                                    ckv[:, s, b, :, :].rearrange("p i k -> p (i k)"), start=True, stop=True)
                        banks.fill(last, "score2", j, half)

                def attend(j):
                    s = j % 2
                    exp2_ready.wait(pe, turn, j)
                    for half in range(2):
                        banks.wait_free(pe, turn, "prob2", j, half)
                        for n in range(4):
                            hp = 4 * half + n
                            src = s2[:, s, 2 * hp:2 * hp + 2, :].rearrange("p h k -> p (h k)")
                            last = pe.transpose(banks.bank("prob2", j, half)[:, n * P:(n + 1) * P], src, ident)
                        banks.fill(last, "prob2", j, half)
                    banks.wait_drained(pe, turn, "vup2", j)
                    banks.wait_drained(pe, turn, "prob2", j, 0)
                    banks.wait_drained(pe, turn, "prob2", j, 1)
                    for half in range(2):
                        banks.wait_free(apart, turn, "out2", j, half)
                        rows = slice(SEQ * half, SEQ * half + SEQ)
                        for b in range(2):
                            for hp in range(H2 // 2):
                                last = pe.matmul(
                                    banks.bank("out2", j, half)[SEQ * b:SEQ * b + SEQ, hp * 32:(hp + 1) * 32],
                                    p2T[rows, s, hp, SEQ * b:SEQ * b + SEQ],
                                    v2[rows, s, b, hp * 32:(hp + 1) * 32], start=True, stop=True)
                        banks.fill(last, "out2", j, half)

                for j in range(QUAD + 1):
                    if j < QUAD:
                        project(j)
                    if j >= 1:
                        attend(j - 1)

            def ffn2(turn):
                for j in range(QUAD):
                    turn_tile(turn, 5, j)
                for j in range(QUAD):
                    banks.wait_drained(pe, turn, "turn", 5, j)
                    banks.wait_free(pe, turn, "gate2", j)
                    for c in range(C):
                        last = pe.matmul(banks.bank("gate2", j)[:, 0:E01], xTf[:, j, c, :], w["gate2"][:, c, :],
                                         start=(c == 0), stop=(c == C - 1))
                    banks.fill(last, "gate2", j)
                for j in range(QUAD):
                    route2_ready.wait(pe, turn, j)
                    banks.wait_free(pe, turn, "gturn", j)
                    banks.fill(pe.transpose(banks.bank("gturn", j)[0:E01, 0:P], comb[:, j, :], ident), "gturn", j)
                for j in range(QUAD):
                    banks.wait_drained(pe, turn, "gturn", j)
                    banks.wait_free(pe, turn, "scale_in", j)
                    for c in range(C):
                        last = pe.matmul(banks.bank("scale_in", j)[:, c * P:(c + 1) * P],
                                         w["ics"][:, c * P:(c + 1) * P], rT2[:, j, :], start=True, stop=True)
                    banks.fill(last, "scale_in", j)
                    banks.wait_free(pe, turn, "scale_out", j)
                    banks.fill(pe.matmul(banks.bank("scale_out", j), rT2[:, j, :], w["ocs"][:, :],
                                         start=True, stop=True), "scale_out", j)
                for j in range(QUAD):
                    y2_split.wait(pe, turn, j)
                    banks.wait_free(pe, turn, "sign2", j)
                    for c in range(C):
                        pe.matmul(banks.bank("sign2", j), xTh[:, j, c, :], w["sign2"][:, c, :],
                                  start=(c == 0), stop=False)
                        last = pe.matmul(banks.bank("sign2", j), xTl[:, j, c, :], w["sign2"][:, c, :],
                                         start=False, stop=(c == C - 1))
                    banks.fill(last, "sign2", j)

            with pe.Fori(0, TURNS) as turn:
                attention0(turn)
                lora_ffn(turn, 0, 1)
                attention1(turn)
                lora_ffn(turn, 1, 3)
                attention2(turn)
                ffn2(turn)

        @block.scalar
        def _(act):
            def high(turn, layer, n):
                for j in range(QUAD):
                    banks.wait_filled(act, turn, "turn", layer, j)
                    xT_high.send(act.activation(xTh[:, j, :, :].rearrange("p c n -> p (c n)"),
                                                banks.bank("turn", layer, j), ACT.Copy))

            def route_exp(turn, f, e, nr):
                step, n = (("route", 0), nr + LORA) if f == 0 else (("route", 1), nr + LORA) if f == 1 else (("gate2",), nr)
                for j in range(QUAD):
                    banks.wait_filled(act, turn, *step, j)
                    banks.drain(act.activation(rh[:, j, 0:n], banks.bank(*step, j)[:, 0:n], ACT.Copy), *step, j)
                for j in range(QUAD):
                    logit_ready.wait(act, turn, 4 * f + j)
                    expo_ready.send(act.activation(e[:, j, 0:nr], rh[:, j, 0:nr], ACT.Exp,
                                                   bias=nmax[:, j:j + 1], accum_out=tot[:, j:j + 1]))

            def hsT_copy(turn, f):
                for j in range(QUAD):
                    banks.wait_filled(act, turn, "hturn", f, j)
                    banks.drain(act.activation(hsT[:, j, :], banks.bank("hturn", f, j)[:, 0:P], ACT.Copy),
                                "hturn", f, j)

            def y1_copy(turn, j):
                banks.wait_filled(act, turn, "out1", j)
                banks.drain(act.activation(y1[:, j, :], banks.bank("out1", j), ACT.Identity,
                                           bias=w["L1b"][:, 3:4]), "out1", j)

            def attention2_before(turn, j):
                s = j % 2
                banks.wait_filled(act, turn, "low2", j)
                cq_ready.send(act.activation(cqT[:, s, :], banks.bank("low2", j)[0:64, 0:P], ACT.Copy))
                banks.wait_filled(act, turn, "qup2", j)
                banks.drain(act.activation(qT2[:, s, :, :].rearrange("p m n -> p (m n)"), banks.bank("qup2", j),
                                           ACT.Copy), "qup2", j)
                banks.wait_filled(act, turn, "vup2", j)
                banks.drain(act.activation(v2[:, s, :, :].rearrange("p b n -> p (b n)"), banks.bank("vup2", j),
                                           ACT.Copy), "vup2", j)
                banks.wait_drained(act, turn, "score2", j, 0)
                banks.wait_drained(act, turn, "score2", j, 1)
                flat = s2[:, s, :, :].rearrange("p h k -> p (h k)")
                exp2_ready.send(act.activation(flat, flat, ACT.Exp, scale=float(L2K) ** -0.5))

            def attention2_after(turn, j):
                for half in range(2):
                    banks.wait_filled(act, turn, "prob2", j, half)
                    banks.drain(act.activation(p2T[:, j % 2, 4 * half:4 * half + 4, :].rearrange("p h n -> p (h n)"),
                                               banks.bank("prob2", j, half), ACT.Copy), "prob2", j, half)

            act.wait_ge(pads, 4)
            with act.Fori(0, TURNS) as turn:
                for j in range(QUAD):
                    cT_loaded[j].wait(act, turn, 0)
                    cT_high.send(act.activation(cTh[:, j, :, :], cT[:, j, :, :], ACT.Copy))
                high(turn, 0, 0)
                for j in range(QUAD):
                    banks.wait_drained(act, turn, "proj0", j)
                    aT_high.send(act.activation(aTh[:, j, :, :], aT[:, j % 2, :, :], ACT.Copy))
                for j in range(QUAD):
                    sm0_ready.wait(act, turn, j)
                    pr0_ready.send(act.activation(pr[:, j, :], sm[:, j, :], ACT.Exp, bias=nmax[:, j:j + 1],
                                                  scale=float(D) ** -0.5, accum_out=tot[:, j:j + 1]))
                for j in range(QUAD):
                    banks.wait_filled(act, turn, "prob0", j)
                    banks.drain(act.activation(prT[:, j, :], banks.bank("prob0", j)[:, 0:P], ACT.Copy), "prob0", j)
                high(turn, 1, 1)
                route_exp(turn, 0, e0, R0)
                hsT_copy(turn, 0)
                for j in range(QUAD):
                    if j >= 2:
                        qkv_written.wait(act, turn, j - 2)
                    for k, (step, dst, lo) in enumerate((("q1", qs, 0), ("k1", kp, 8), ("v1", vp, 8))):
                        banks.wait_filled(act, turn, step, j)
                        banks.drain(act.activation(dst[:, j % 2, lo:lo + D], banks.bank(step, j), ACT.Identity,
                                                   bias=w["L1b"][:, k:k + 1]), step, j)
                for j in range(QUAD):
                    banks.wait_drained(act, turn, "dot1", j, 0)
                    banks.wait_drained(act, turn, "dot1", j, 1)
                    exp1_ready.send(act.activation(ee[:, :, :], ee[:, :, :], ACT.Exp, scale=float(CH) ** -0.5))
                    if j >= 1:
                        y1_copy(turn, j - 1)
                y1_copy(turn, QUAD - 1)
                high(turn, 3, 2)
                route_exp(turn, 1, e1, R1)
                hsT_copy(turn, 1)
                high(turn, 4, 3)
                for j in range(QUAD + 1):
                    if j < QUAD:
                        attention2_before(turn, j)
                    if j >= 1:
                        attention2_after(turn, j - 1)
                for j in range(QUAD):
                    banks.wait_filled(act, turn, "turn", 5, j)
                    banks.drain(act.activation(xTf[:, j, :, :].rearrange("p c n -> p (c n)"),
                                               banks.bank("turn", 5, j), ACT.Copy), "turn", 5, j)
                route_exp(turn, 2, e2, E01)
                for j in range(QUAD):
                    banks.wait_filled(act, turn, "gturn", j)
                    banks.drain(act.activation(rT2[:, j, :], banks.bank("gturn", j)[0:E01, 0:P], ACT.Copy),
                                "gturn", j)
                for j in range(QUAD):
                    banks.wait_filled(act, turn, "scale_out", j)
                    banks.drain(act.activation(osb[:, j, :], banks.bank("scale_out", j), ACT.Copy,
                                               scale=w["gates"][:, 6:7]), "scale_out", j)
                    banks.wait_drained(act, turn, "scale_in", j)
                    y2_high.send(act.activation(xTh[:, j, :, :], xTf[:, j, :, :], ACT.Copy))

        @block.gpsimd
        def _(pool):
            banks.open(pool)
            pool.sem_inc(stored.sem, 1)
            def rstd_of(turn, layer):
                for j in range(QUAD):
                    stats_ready.wait(pool, turn, 4 * layer + j)
                    pool.tensor_tensor(vare[:, j:j + 1], mv[:, j, 1:2], w["eps"][:, :], ALU.add)\
                        .then_inc(pool_step, 1)
                    pool.wait_ge(pool_step, turn * 24 + (4 * layer + j + 1))
                    rstd_ready.send(pool.tensor_tensor(rstd[:, j:j + 1], vare[:, j:j + 1], w["power"][:, 0:1],
                                                       ALU.pow))

            def add_bias(turn, f, layer):
                for j in range(QUAD):
                    xn_ready.wait(pool, turn, 4 * layer + j)
                    xbias_ready.send(pool.tensor_tensor(xq[:, j, :], xq[:, j, :], w["gbias"][:, f, :], ALU.add))

            for t in (kp, vp):
                pool.memset(t[:, :, :], 0.0).then_inc(pads, 1)
            pool.memset(e0[:, :, :], NEVER).then_inc(pads, 1)
            pool.memset(pick0[:, :, :], NEVER).then_inc(pads, 1)
            with pool.Fori(0, TURNS) as turn:
                for j in range(QUAD):
                    cT_high.wait(pool, turn, j)
                    cT_split.send(pool.tensor_tensor(cTl[:, j, :, :], cT[:, j, :, :], cTh[:, j, :, :], ALU.subtract))
                rstd_of(turn, 0)
                for j in range(QUAD):
                    aT_high.wait(pool, turn, j)
                    aT_split.send(pool.tensor_tensor(aTl[:, j, :, :], aT[:, j % 2, :, :], aTh[:, j, :, :],
                                                     ALU.subtract))
                rstd_of(turn, 1)
                add_bias(turn, 0, 1)
                rstd_of(turn, 2)
                def times_k(j):
                    qkv_in[j % 2].wait(pool, turn, j // 2)
                    if j >= 1:
                        banks.wait_filled(pool, turn, "dot1", j - 1, 1)
                    qk_pool.send(pool.tensor_tensor(qk[1][:, :, :, :], times_q(j, 1), windows(kL, j, 1), ALU.mult))
                times_k(0)
                for j in range(QUAD):
                    if j + 1 < QUAD:
                        times_k(j + 1)
                    exp1_ready.wait(pool, turn, j)
                    if j >= 1:
                        oL_ready.wait(pool, turn, j - 1)
                    pv_pool.send(pool.tensor_tensor(pv[1][:, :, :, :], weights(1), windows(vL, j, 1), ALU.mult))
                rstd_of(turn, 3)
                add_bias(turn, 1, 3)
                rstd_of(turn, 4)
                rstd_of(turn, 5)
                add_bias(turn, 2, 5)
                for j in range(QUAD):
                    y2_high.wait(pool, turn, j)
                    y2_split.send(pool.tensor_tensor(xTl[:, j, :, :], xTf[:, j, :, :], xTh[:, j, :, :], ALU.subtract))

        @block.vector
        def _(dve):
            apart = Apart(dve, pads, 4)
            dve.wait_ge(pads, 4)
            with dve.Fori(0, TURNS) as turn:
                st = Steps(dve, dve_step, DVE_STEPS, turn)

                def each(make, after=None):
                    made = []
                    for j in range(QUAD):
                        if after:
                            st.after(after[j], apart)
                        made.append(st.step(make(j)))
                    return made

                def normalise(layer, x, x_stands, update=None):
                    for j in range(QUAD + 1):
                        if j < QUAD:
                            if update:
                                update(j)
                            x_stands(j)
                            n = st.step(dve.bn_stats(stats[:, j, :], x[:, j, :]))
                            st.after(n, apart)
                            stats_ready.send(dve.bn_aggr(mv[:, j, :], stats[:, j, :]))
                        if j >= 1:
                            rstd_ready.wait(dve, turn, 4 * layer + j - 1)
                            xn_ready.send(dve.tensor_scalar(xn[:, j - 1, :], x[:, j - 1, :], mv[:, j - 1, 0:1],
                                                            rstd[:, j - 1:j], ALU.subtract, ALU.mult))

                def low(layer, n):
                    for j in range(QUAD):
                        xT_high.wait(dve, turn, 4 * n + j)
                        banks.drain(dve.tensor_tensor(xTl[:, j, :, :].rearrange("p c n -> p (c n)"),
                                                      banks.bank("turn", layer, j),
                                                      xTh[:, j, :, :].rearrange("p c n -> p (c n)"), ALU.subtract),
                                    "turn", layer, j)

                def logits(f, step, nr, add=None):
                    for j in range(QUAD):
                        banks.wait_drained(dve, turn, *step, j)
                        if add is not None:
                            st.link(dve.tensor_tensor(rh[:, j, 0:nr], rh[:, j, 0:nr], add, ALU.add))
                        logit_ready.send(dve.tensor_reduce(nmax[:, j:j + 1], rh[:, j, 0:nr], AX.X, ALU.max,
                                                           negate=True))

                def expo(f, j, eng=dve):
                    expo_ready.wait(eng, turn, 4 * f + j)

                def lora(f, nr):
                    for j in range(QUAD):
                        hs_ready.send(dve.tensor_tensor(
                            hs[:, j, :].rearrange("p (e r) -> p e r", r=RANK),
                            rh[:, j, nr:nr + LORA].rearrange("p (e r) -> p e r", r=RANK),
                            comb[:, j, :].unsqueeze(2).to_broadcast([P, E01, RANK]), ALU.mult))

                def add_ffn(f, j):
                    banks.wait_filled(dve, turn, "base", f, j)
                    xbias_ready.wait(dve, turn, 4 * f + j)
                    banks.drain(dve.scalar_tensor_tensor(
                        out=xq[:, j, :], in0=banks.bank("base", f, j), scalar=w["gates"][:, 4 + f:5 + f],
                        in1=xq[:, j, :], op0=ALU.mult, op1=ALU.add), "base", f, j)

                normalise(0, xin, lambda j: x_loaded[j].wait(dve, turn, 0))
                low(0, 0)
                for j in range(QUAD):
                    banks.wait_filled(dve, turn, "proj0", j)
                    if j >= 2:
                        aT_split.wait(dve, turn, j - 2)
                    banks.drain(dve.tensor_tensor(aT[:, j % 2, :, :],
                                                  banks.bank("proj0", j).rearrange("p (c n) -> p c n", c=C),
                                                  w["r"][:, :].unsqueeze(2).to_broadcast([P, C, P]), ALU.add),
                                "proj0", j)

                def row_term(j):
                    banks.wait_filled(dve, turn, "score0", j)
                    return dve.tensor_tensor(u[:, j:j + 1], banks.bank("score0", j)[:, P:P + 1], w["s"][:, :], ALU.add)
                for j in range(QUAD):
                    st.link(row_term(j))
                    banks.drain(dve.scalar_tensor_tensor(
                        out=sm[:, j, :], in0=banks.bank("score0", j)[:, 0:P], scalar=u[:, j:j + 1],
                        in1=w["bdmask"][:, :], op0=ALU.add, op1=ALU.add), "score0", j)

                def largest(j):
                    banks.wait_drained(dve, turn, "score0", j)
                    return dve.tensor_reduce(nmax[:, j:j + 1], sm[:, j, :], AX.X, ALU.max, negate=True)
                got = each(largest)
                for j in range(QUAD):
                    st.after(got[j])
                    sm0_ready.send(dve.tensor_scalar(nmax[:, j:j + 1], nmax[:, j:j + 1], float(D) ** -0.5, None,
                                                     ALU.mult))

                def over_sum(j):
                    pr0_ready.wait(dve, turn, j)
                    return dve.reciprocal(rec[:, j:j + 1], tot[:, j:j + 1])
                got = each(over_sum)
                got = each(lambda j: dve.tensor_scalar(rec[:, j:j + 1], rec[:, j:j + 1], w["gates"][:, 0:1], None,
                                                       ALU.mult), got)
                def add0(j):
                    st.after(got[j])
                    banks.wait_filled(dve, turn, "out0", j)
                    dve.wait_ge(stored.sem, turn * (QUAD * 16) + 1)
                    banks.drain(dve.scalar_tensor_tensor(
                        out=xq[:, j, :], in0=banks.bank("out0", j), scalar=rec[:, j:j + 1], in1=xin[:, j, :],
                        op0=ALU.mult, op1=ALU.add), "out0", j)

                normalise(1, xq, lambda j: banks.wait_drained(dve, turn, "out0", j), add0)
                low(1, 1)
                logits(0, ("route", 0), R0)

                def top(e, f):
                    def one(j):
                        expo(f, j, apart)
                        return dve.max(top8[:, j, :], e[:, j, 0:(R0, R1)[f]])
                    return each(one)
                got = top(e0, 0)
                each(lambda j: dve.tensor_tensor(tot[:, j:j + 1], top8[:, j, 0:1], top8[:, j, 1:2], ALU.add), got)
                got = each(lambda j: dve.tensor_copy(pick0[:, j, 0:2], top8[:, j, 0:2]), got)
                got = each(lambda j: dve.reciprocal(rec[:, j:j + 1], tot[:, j:j + 1]), got)
                got = each(lambda j: dve.match_replace(rkeep[:, j, 0:14], pick0[:, j, :], e0[:, j, :], 0.0), got)
                got = each(lambda j: dve.tensor_tensor(rsel[:, j, 0:R0], e0[:, j, 0:R0], rkeep[:, j, 0:R0],
                                                       ALU.subtract), got)
                got = each(lambda j: dve.tensor_scalar(comb[:, j, :], rsel[:, j, 0:R0], rec[:, j:j + 1], 2.0,
                                                       ALU.mult, ALU.mult), got)
                st.after(got[-1])
                lora(0, R0)


                normalise(2, xq, lambda j: banks.wait_drained(dve, turn, "base", 0, j), lambda j: add_ffn(0, j))
                def times_k(j):
                    qkv_in[j % 2].wait(dve, turn, j // 2)
                    if j >= 1:
                        banks.wait_filled(dve, turn, "dot1", j - 1, 0)
                    qk_dve.send(dve.tensor_tensor(qk[0][:, :, :, :], times_q(j, 0), windows(kL, j, 0), ALU.mult))
                times_k(0)
                for j in range(QUAD):
                    for h in range(2):
                        banks.wait_filled(dve, turn, "dot1", j, h)
                        at = slice(h * (TP // 2), (h + 1) * (TP // 2))
                        dots = banks.bank("dot1", j, h).rearrange("p (t w) -> p t w", w=WIN)
                        st.link(dve.tensor_reduce(mx1[:, at], dots, AX.X, ALU.max))
                        ins = dve.tensor_tensor(ee[:, at, :], dots,
                                                mx1[:, at].unsqueeze(2).to_broadcast([P, TP // 2, WIN]), ALU.subtract)
                        banks.drain(ins, "dot1", j, h)
                    if j + 1 < QUAD:
                        times_k(j + 1)
                    exp1_ready.wait(dve, turn, j)
                    st.step(dve.tensor_tensor(pv[0][:, :, :, :], weights(0), windows(vL, j, 0), ALU.mult))
                    st.link(dve.tensor_reduce(sum1[:, :], ee[:, :, :], AX.X, ALU.add))
                    st.link(dve.reciprocal(rec1[:, :], sum1[:, :]))
                    if j >= 2:
                        o_written.wait(dve, turn, j - 2)
                    st.link(dve.tensor_reduce(oL[:, j % 2, :, 0:TP // 2], pv[0][:, :, :, :], AX.X, ALU.add))
                    pv_pool.wait(dve, turn, j)
                    st.link(dve.tensor_reduce(oL[:, j % 2, :, TP // 2:TP], pv[1][:, :, :, :], AX.X, ALU.add))
                    oL_ready.send(dve.tensor_tensor(oL[:, j % 2, :, :], oL[:, j % 2, :, :],
                                                    rec1[:, :].unsqueeze(1).to_broadcast([P, CH, TP]), ALU.mult))

                def add1(j):
                    banks.wait_drained(dve, turn, "out1", j)
                    st.link(dve.scalar_tensor_tensor(out=xq[:, j, :], in0=y1[:, j, :], scalar=w["gates"][:, 1:2],
                                                     in1=xq[:, j, :], op0=ALU.mult, op1=ALU.add))

                normalise(3, xq, lambda j: None, add1)
                low(3, 2)
                logits(1, ("route", 1), R1, w["rb1"][:, :])
                got = top(e1, 1)
                got = each(lambda j: dve.match_replace(rkeep[:, j, 0:R1], top8[:, j, :], e1[:, j, :], 0.0), got)
                got = each(lambda j: dve.tensor_tensor(rsel[:, j, 0:R1], e1[:, j, :], rkeep[:, j, 0:R1],
                                                       ALU.subtract), got)
                got = each(lambda j: dve.tensor_tensor(rmix[:, j, :, :],
                                                       rsel[:, j, 0:R1].unsqueeze(1).to_broadcast([P, E01, R1]),
                                                       w["route_to"][:, :, :], ALU.mult), got)
                each(lambda j: dve.reciprocal(rec[:, j:j + 1], tot[:, j:j + 1]))
                got = each(lambda j: dve.tensor_reduce(comb[:, j, :], rmix[:, j, :, :], AX.X, ALU.add), got)
                got = each(lambda j: dve.tensor_scalar(comb[:, j, :], comb[:, j, :], rec[:, j:j + 1], 2.0,
                                                       ALU.mult, ALU.mult), got)
                st.after(got[-1])
                lora(1, R1)


                normalise(4, xq, lambda j: banks.wait_drained(dve, turn, "base", 1, j), lambda j: add_ffn(1, j))
                low(4, 3)

                def attention2_before(j):
                    s = j % 2
                    cq_ready.wait(dve, turn, j)
                    low_keys = banks.bank("low2", j)[:, P:2 * P].rearrange("p (b k) -> p b k", b=2)
                    banks.drain(dve.tensor_tensor(
                        ckv[:, s, :, :, :], low_keys.unsqueeze(2).to_broadcast([P, 2, 4, SEQ]),
                        w["quarter"][:, :].unsqueeze(1).unsqueeze(3).to_broadcast([P, 2, 4, SEQ]), ALU.mult), "low2", j)
                    for half in range(2):
                        heads = slice(8 * half, 8 * half + 8)
                        banks.wait_filled(dve, turn, "score2", j, half)
                        scores = banks.bank("score2", j, half).rearrange("p (h k) -> p h k", k=SEQ)
                        st.link(dve.tensor_reduce(mx2[:, s, heads], scores, AX.X, ALU.max))
                        banks.drain(dve.tensor_tensor(s2[:, s, heads, :], scores,
                                                      mx2[:, s, heads].unsqueeze(2).to_broadcast([P, 8, SEQ]),
                                                      ALU.subtract), "score2", j, half)

                def attention2_after(j):
                    s = j % 2
                    exp2_ready.wait(dve, turn, j)
                    st.link(dve.tensor_reduce(sum2[:, s, :], s2[:, s, :, :], AX.X, ALU.add))
                    st.link(dve.reciprocal(rec2[:, s, :], sum2[:, s, :]))
                    for half in range(2):
                        banks.wait_filled(dve, turn, "out2", j, half)
                        mine = o2[:, s, :, :].rearrange("p (a b) k -> p a b k", b=2)[:, :, half, :]
                        over = rec2[:, s, :].rearrange("p (a b) -> p a b", b=2)[:, :, half]
                        banks.drain(dve.tensor_tensor(
                            mine, banks.bank("out2", j, half)[:, 0:256].rearrange("p (a k) -> p a k", k=32),
                            over.unsqueeze(2).to_broadcast([P, 8, 32]), ALU.mult), "out2", j, half)
                    banks.wait_drained(dve, turn, "out2", j, 0)
                    banks.wait_drained(dve, turn, "out2", j, 1)
                    return st.step(dve.scalar_tensor_tensor(
                        out=xq[:, j, :], in0=o2[:, s, :, :].rearrange("p h k -> p (h k)"),
                        scalar=w["gates"][:, 2:3], in1=xq[:, j, :], op0=ALU.mult, op1=ALU.add))
                added = []
                for j in range(QUAD + 1):
                    if j < QUAD:
                        attention2_before(j)
                    if j >= 1:
                        added.append(attention2_after(j - 1))

                normalise(5, xq, lambda j: st.after(added[j]))
                logits(2, ("gate2",), E01)

                def over_all(j):
                    expo(2, j)
                    return dve.reciprocal(rec[:, j:j + 1], tot[:, j:j + 1])
                got = each(over_all)
                for j in range(QUAD):
                    st.after(got[j])
                    route2_ready.send(dve.tensor_scalar(comb[:, j, :], e2[:, j, :], rec[:, j:j + 1], None, ALU.mult))
                for j in range(QUAD):
                    banks.wait_filled(dve, turn, "scale_in", j)
                    flat = xTf[:, j, :, :].rearrange("p c n -> p (c n)")
                    banks.drain(dve.tensor_tensor(flat, banks.bank("scale_in", j), flat, ALU.mult), "scale_in", j)
                for j in range(QUAD):
                    banks.wait_filled(dve, turn, "sign2", j)
                    banks.drain(dve.tensor_tensor(osb[:, j, :], banks.bank("sign2", j), osb[:, j, :], ALU.mult),
                                "sign2", j)
                for j in range(QUAD):
                    banks.wait_drained(dve, turn, "sign2", j)
                    xbias_ready.wait(dve, turn, 8 + j)
                    x_done.send(dve.tensor_tensor(xq[:, j, :], xq[:, j, :], osb[:, j, :], ALU.add))
                st.close()


def prepare_last(nc, io, w):
    plan = []
    for j in range(QUAD):
        plan.append((("turn", j), j))
    plan += [(("cos",), 4), (("sin",), 5)]
    with ExitStack() as ctx:
        def sb(name, shape, dt=F32):
            return ctx.enter_context(nc.sbuf_tensor("pl_" + name, shape, dt))

        def signal(name, per_turn, by=1):
            return Signal(nc, w, "pl_" + name, per_turn, by)

        xn, cT = sb("xn", [P, QUAD, D]), sb("cT", [P, C, QUAD * P])
        stats, mv = sb("stats", [P, QUAD, 6]), sb("mv", [P, QUAD, 2])
        vare, rstd = sb("vare", [P, QUAD]), sb("rstd", [P, QUAD])
        mask_raw = sb("mask", [P, TILES, SEQ], I32)
        pos_raw, pos = sb("pos_raw", [P, TOKENS], I32), sb("pos", [P, TOKENS])
        wrap = sb("wrap", [P, TOKENS])
        row = sb("row", [P, C])
        one_hot = sb("one_hot", [P, C, QUAD * P])
        table = sb("table", [P, 2, C, P])
        banks = Banks(nc, ctx, w, "pl", plan)
        x_loaded = new_semaphore(nc, w, "pl_x_loaded")
        tables_loaded = new_semaphore(nc, w, "pl_tables_loaded")
        row_ready = new_semaphore(nc, w, "pl_row_ready")
        once = new_semaphore(nc, w, "pl_once")
        cT_loaded, cT_high, cT_low = signal("cT_loaded", 1, 16), signal("cT_high", 1), signal("cT_low", 1)
        stats_ready, rstd_ready, xn_ready = signal("stats_ready", 4), signal("rstd_ready", 4), signal("xn_ready", 4)
        xT_high, hot_ready = signal("xT_high", 4), signal("hot_ready", 4)
        dve_step = new_semaphore(nc, w, "pl_dve_step")
        pool_step = new_semaphore(nc, w, "pl_pool_step")
        block = ctx.enter_context(nc.Block())
        PER = QUAD * P

        @block.sync
        def _(sp):
            sp.dma_start(w["X"][:, :, :], io["x_mid"].rearrange("(t p) n -> p t n", p=P)).then_inc(x_loaded, 16)
            sp.dma_start(pos_raw[:, :], io["pos"].partition_broadcast(P)).then_inc(tables_loaded, 16)
            sp.dma_start(table[:, 0, :, :], io["cos"].rearrange("(c p) n -> p c n", p=P)).then_inc(tables_loaded, 16)
            sp.dma_start(table[:, 1, :, :], io["sin"].rearrange("(c p) n -> p c n", p=P)).then_inc(tables_loaded, 16)
            sp.dma_start(mask_raw[:, :, :], io["mask"].rearrange("(t p) n -> p t n", p=P)).then_inc(tables_loaded, 16)
            src = io["ctxT"].rearrange("(c p) n -> p c n", p=P)
            cT_loaded.send(sp.dma_start(cT[:, :, :], src[:, :, 0:PER]))
            with sp.Fori(0, TURNS - 1) as turn:
                cT_low.wait(sp, turn, 0)
                cT_loaded.send(sp.dma_start(cT[:, :, :], src[:, :, bass.ts(turn + 1, PER)]))

        @block.gpsimd
        def _(pool):
            banks.open(pool)
            pool.iota(row[:, :], pattern=[[P, C]], base=0, channel_multiplier=1,
                      allow_small_or_imprecise_dtypes=True).then_inc(row_ready, 1)
            with pool.Fori(0, TURNS) as turn:
                for j in range(QUAD):
                    stats_ready.wait(pool, turn, j)
                    pool.tensor_tensor(vare[:, j:j + 1], mv[:, j, 1:2], w["eps"][:, :], ALU.add)\
                        .then_inc(pool_step, 1)
                    pool.wait_ge(pool_step, turn * QUAD + (j + 1))
                    rstd_ready.send(pool.tensor_tensor(rstd[:, j:j + 1], vare[:, j:j + 1], w["power"][:, 0:1],
                                                       ALU.pow))
                cT_high.wait(pool, turn, 0)
                cT_low.send(pool.tensor_tensor(w["cTl"][:, :, bass.ts(turn, PER)], cT[:, :, :],
                                               w["cTh"][:, :, bass.ts(turn, PER)], ALU.subtract))

        @block.tensor
        def _(pe):
            with pe.Fori(0, TURNS) as turn:
                for j in range(QUAD):
                    xn_ready.wait(pe, turn, j)
                    banks.wait_free(pe, turn, "turn", j)
                    for c in range(C):
                        last = pe.transpose(banks.bank("turn", j)[:, c * P:(c + 1) * P],
                                            xn[:, j, c * P:(c + 1) * P], w["ident"][:, :])
                    banks.fill(last, "turn", j)
                for k, step in enumerate(("cos", "sin")):
                    hot_ready.wait(pe, turn, QUAD - 1)
                    banks.wait_free(pe, turn, step)
                    for c in range(C):
                        last = pe.matmul(banks.bank(step), table[:, k, c, :], one_hot[:, c, :],
                                         start=(c == 0), stop=(c == C - 1))
                    banks.fill(last, step)

        @block.scalar
        def _(act):
            with act.Fori(0, TURNS) as turn:
                cT_loaded.wait(act, turn, 0)
                cT_high.send(act.activation(w["cTh"][:, :, bass.ts(turn, PER)], cT[:, :, :], ACT.Copy))
                for j in range(QUAD):
                    banks.wait_filled(act, turn, "turn", j)
                    xT_high.send(act.activation(w["xTh"][:, :, bass.ts(turn * QUAD + j, P)],
                                                banks.bank("turn", j).rearrange("p (c n) -> p c n", c=C), ACT.Copy))
                for k, step in enumerate(("cos", "sin")):
                    banks.wait_filled(act, turn, step)
                    banks.drain(act.activation(w[step][:, bass.ts(turn, PER)], banks.bank(step), ACT.Copy), step)

        @block.vector
        def _(dve):
            apart = Apart(dve, row_ready, 1)
            dve.wait_ge(tables_loaded, 64)
            dve.tensor_copy(pos[:, :], pos_raw[:, :]).then_inc(once, 1)
            dve.wait_ge(once, 1)
            dve.tensor_scalar(wrap[:, :], pos[:, :], 0.0, float(POSITIONS), ALU.is_lt, ALU.mult).then_inc(once, 1)
            dve.wait_ge(once, 2)
            dve.tensor_tensor(pos[:, :], pos[:, :], wrap[:, :], ALU.add).then_inc(once, 1)
            dve.wait_ge(once, 3)
            dve.tensor_scalar(pos[:, :], pos[:, :], 0.0, float(POSITIONS - 1), ALU.max, ALU.min).then_inc(once, 1)
            dve.tensor_scalar(w["mask"][:, :, :], mask_raw[:, :, :], 0.0, MASKED, ALU.is_equal, ALU.mult)
            dve.wait_ge(once, 4)
            dve.wait_ge(x_loaded, 16)
            dve.wait_ge(row_ready, 1)
            with dve.Fori(0, TURNS) as turn:
                for j in range(QUAD):
                    dve.bn_stats(stats[:, j, :], w["X"][:, bass.ds(turn * QUAD + j, 1), :]).then_inc(dve_step, 1)
                for j in range(QUAD):
                    apart.wait_ge(dve_step, turn * QUAD + (j + 1))
                    stats_ready.send(dve.bn_aggr(mv[:, j, :], stats[:, j, :]))
                banks.wait_free(dve, turn, "cos")
                banks.wait_free(dve, turn, "sin")
                for c in range(C):
                    hot_ready.send(dve.tensor_scalar(one_hot[:, c, :], pos[:, bass.ts(turn, PER)],
                                                     row[:, c:c + 1], None, ALU.is_equal))
                for j in range(QUAD):
                    rstd_ready.wait(dve, turn, j)
                    xn_ready.send(dve.tensor_scalar(xn[:, j, :], w["X"][:, bass.ds(turn * QUAD + j, 1), :],
                                                    mv[:, j, 0:1], rstd[:, j:j + 1], ALU.subtract, ALU.mult))
                for j in range(QUAD):
                    xT_high.wait(dve, turn, j)
                    banks.drain(dve.tensor_tensor(w["xTl"][:, :, bass.ts(turn * QUAD + j, P)],
                                                  banks.bank("turn", j).rearrange("p (c n) -> p c n", c=C),
                                                  w["xTh"][:, :, bass.ts(turn * QUAD + j, P)], ALU.subtract),
                                "turn", j)


def last_attention(nc, io, w):
    PER = QUAD * P
    before = [(("q", "first", 0), 0), (("k", "first"), 1), (("q", "first", 1), 0), (("q", "first", 2), 1),
              (("q", "first", 3), 0), (("q", "first", 4), 1), (("v", "first"), 1), (("score", "first"), 2)]
    plan = []
    for n in range(QUAD):
        for u in range(QUAD):
            plan += [(("score", n, u), 2 + (u + 1) % 2), (("q", n, u), (0, 1, 0, 0)[u]), (("turn", n, u), 4)]
            if u == 0:
                plan.append((("k", n), 1))
            if u == QUAD - 1:
                plan.append((("v", n), 1))
            plan += [(("even", n, u), 5), (("odd", n, u), 6), (("out", n, u), 7)]
    with ExitStack() as ctx:
        def sb(name, shape, dt=F32):
            return ctx.enter_context(nc.sbuf_tensor("la_" + name, shape, dt))

        def signal(name, per_turn, by=1):
            return Signal(nc, w, "la_" + name, per_turn, by)

        raw_q, raw_kv, raw_o = sb("raw_q", [P, C, GROUP * HD]), sb("raw_kv", [P, 2, C, HD]), sb("raw_o", [P, GROUP, D])
        wqh, wql = sb("wqh", [P, C, GROUP * HD], HALF), sb("wql", [P, C, GROUP * HD], HALF)
        woh, wol = sb("woh", [P, GROUP, D], HALF), sb("wol", [P, GROUP, D], HALF)
        wkvh, wkvl = sb("wkvh", [P, 2, C, HD], HALF), sb("wkvl", [P, 2, C, HD], HALF)
        q, k = sb("q", [P, 2, GROUP, PER]), sb("k", [P, 2, PER])
        straight = sb("straight", [P, 2, PER])
        rot = sb("rot", [P, 2, PER])
        v2 = sb("v2", [P, 2, QUAD, 2, HD])
        s, p, pT = sb("s", [P, 2, GROUP, SEQ]), sb("p", [P, 2, GROUP, SEQ]), sb("pT", [P, 2, 2, P])
        mx, tot, rec = sb("mx", [P, 2, GROUP]), sb("tot", [P, 2, GROUP]), sb("rec", [P, 2, GROUP])
        oTh, oTl = sb("oTh", [P, 2, GROUP, P], HALF), sb("oTl", [P, 2, GROUP, P], HALF)

        banks = Banks(nc, ctx, w, "la", plan, before)
        q_loaded, o_loaded = signal("q_loaded", 1, 48), signal("o_loaded", 1, 16)
        q_high, q_low, o_high, o_low = signal("q_high", 6), signal("q_low", 6), signal("o_high", 4), signal("o_low", 4)
        rope_sum = signal("rope_sum", 20)
        first_step = new_semaphore(nc, w, "la_first_step")
        exp_ready, rec_ready, p_ready = signal("exp_ready", 16), signal("rec_ready", 16), signal("p_ready", 16)
        oT_high = signal("oT_high", 32)
        dve_step = new_semaphore(nc, w, "la_dve_step")
        block = ctx.enter_context(nc.Block())

        def tokens(n):
            return slice(n * PER, (n + 1) * PER)

        PIECES = ["q0", "k", "q1", "q2", "q3", "v"]
        SPLIT_IN = [("q0", "k"), ("q1",), ("q2",), ("q3", "v")]

        def raw_high_low(piece):
            if piece in ("k", "v"):
                i = ("k", "v").index(piece)
                return raw_kv[:, i, :, :], wkvh[:, i, :, :], wkvl[:, i, :, :]
            cols = slice(int(piece[1]) * HD, (int(piece[1]) + 1) * HD)
            return raw_q[:, :, cols], wqh[:, :, cols], wql[:, :, cols]

        FIRST = [(("q", "first", 0), 0, 0), (("k", "first"), None, 0), (("q", "first", 1), 1, 0),
                 (("q", "first", 2), 2, 0), (("q", "first", 3), 3, 0), (("q", "first", 4), 0, 1)]

        def projections(n, u, more):
            if u == QUAD - 1:
                found = [(5 * n + 4, ("q", n, u), 0, n + 2)]
            else:
                found = [(5 * n + u + 1, ("q", n, u), u + 1, n + 1)]
            if u == 0:
                found.insert(0, (5 * n, ("k", n), None, n + 1))
            return [(i, place, which, step % QUAD) for i, place, which, step in found if more or step < QUAD]

        @block.sync
        def _(sp):
            def load_qkv(head):
                sp.dma_start(raw_q[:, :, :], io["Wq3"].rearrange("(c p) n -> p c n", p=P)[:, :, bass.ts(head, GROUP * HD)])\
                  .then_inc(q_loaded.sem, 16)
                for i, name in enumerate(("Wk3", "Wv3")):
                    sp.dma_start(raw_kv[:, i, :, :],
                                 io[name].rearrange("(c p) n -> p c n", p=P)[:, :, bass.ts(head, HD)])\
                      .then_inc(q_loaded.sem, 16)

            def load_o(head):
                rows = io["Wo3"][bass.ts(head, GROUP * HD), :]
                o_loaded.send(sp.dma_start(raw_o[:, :, :], rows.rearrange("(h p) n -> p h n", p=P)))

            load_qkv(0)
            load_o(0)
            with sp.Fori(0, KV - 1) as turn:
                q_low.wait(sp, turn, len(PIECES) - 1)
                load_qkv(turn + 1)
                o_low.wait(sp, turn, GROUP - 1)
                load_o(turn + 1)

        @block.tensor
        def _(pe):
            def xs(t, n):
                return [t[:, c, tokens(n)] for c in range(C)]

            def next_piece(turn, piece):
                q_low.wait(pe, turn, len(PIECES) + PIECES.index(piece))

            def project_q(turn, step, n, u):
                banks.wait_free(pe, turn, *step)
                cols = slice(u * HD, (u + 1) * HD)
                banks.fill(three(pe, banks.bank(*step), [wqh[:, c, cols] for c in range(C)],
                                 [wql[:, c, cols] for c in range(C)], xs(w["xTh"], n), xs(w["xTl"], n)), *step)

            def project_k(turn, step, n):
                banks.wait_free(pe, turn, *step)
                banks.fill(three(pe, banks.bank(*step), [wkvh[:, 0, c, :] for c in range(C)],
                                 [wkvl[:, 0, c, :] for c in range(C)], xs(w["cTh"], n), xs(w["cTl"], n)), *step)

            def project_v(turn, step, n):
                banks.wait_free(pe, turn, *step)
                for t in range(QUAD):
                    cols = slice(n * PER + t * P, n * PER + (t + 1) * P)
                    last = three(pe, banks.bank(*step)[:, t * HD:(t + 1) * HD],
                                 [w["cTh"][:, c, cols] for c in range(C)], [w["cTl"][:, c, cols] for c in range(C)],
                                 [wkvh[:, 1, c, :] for c in range(C)], [wkvl[:, 1, c, :] for c in range(C)])
                banks.fill(last, *step)

            def out_projection(turn, n, u):
                for half in range(2):
                    banks.wait_drained(pe, turn, ("even", "odd")[half], n, u)
                if (n, u) == (0, 0):
                    o_low.wait(pe, turn, GROUP - 1)
                banks.wait_free(pe, turn, "out", n, u)
                banks.fill(three(pe, banks.bank("out", n, u), [oTh[:, u % 2, h, :] for h in range(GROUP)],
                                 [oTl[:, u % 2, h, :] for h in range(GROUP)], [woh[:, h, :] for h in range(GROUP)],
                                 [wol[:, h, :] for h in range(GROUP)]), "out", n, u)

            def scores(turn, place, n, u):
                m = n % 2
                banks.wait_free(pe, turn, *place)
                out = banks.bank(*place)[:, 0:GROUP * SEQ]
                pe.matmul(out, w["identh"][:, :],
                          w["mask"][:, n * QUAD + u, :].unsqueeze(1).to_broadcast([P, GROUP, SEQ]),
                          start=True, stop=True, skip_group_check=True)
                for b in range(2):
                    cols = slice(u * P + b * SEQ, u * P + (b + 1) * SEQ)
                    for h in range(GROUP):
                        last = pe.matmul(out[SEQ * b:SEQ * b + SEQ, h * SEQ:(h + 1) * SEQ], q[:, m, h, cols],
                                         k[:, m, cols], start=False, stop=True, skip_group_check=True)
                banks.fill(last, *place)

            def unit(turn, n, u, more):
                m = n % 2
                if more or (n, u) != (QUAD - 1, QUAD - 1):
                    if u == QUAD - 1:
                        rope_sum.wait(pe, turn, len(FIRST) + 5 * n + 3)
                    following = (QUAD * n + u + 1) % (QUAD * QUAD)
                    scores(turn, ("score", n, u), following // QUAD, following % QUAD)
                for _, place, which, step in projections(n, u, more):
                    if n == QUAD - 1 or (n, u) == (QUAD - 2, QUAD - 1):
                        next_piece(turn, "k" if which is None else f"q{which}")
                    if which is None:
                        project_k(turn, place, step)
                    else:
                        project_q(turn, place, step, which)
                p_ready.wait(pe, turn, QUAD * n + u)
                banks.wait_free(pe, turn, "turn", n, u)
                for hp in range(2):
                    last = pe.transpose(banks.bank("turn", n, u)[:, hp * P:(hp + 1) * P],
                                        p[:, u % 2, 2 * hp:2 * hp + 2, :].rearrange("p h k -> p (h k)"),
                                        w["ident"][:, :])
                banks.fill(last, "turn", n, u)
                if (n, u) != (0, 0):
                    out_projection(turn, n if u else n - 1, (u - 1) % QUAD)
                if u == QUAD - 1 and n < QUAD - 1:
                    project_v(turn, ("v", n), (n + 1) % QUAD)
                banks.wait_drained(pe, turn, "turn", n, u)
                if (n, u) == (0, 0):
                    banks.wait_all_drained(pe, turn, 1)
                elif u == 0:
                    banks.wait_drained(pe, turn, "v", n - 1)
                for half, name in enumerate(("even", "odd")):
                    banks.wait_free(pe, turn, name, n, u)
                    rows = slice(SEQ * half, SEQ * half + SEQ)
                    out = banks.bank(name, n, u)[:, 0:2 * P].rearrange("p (h t) -> p h t", h=2)
                    for b in range(2):
                        cols = slice(SEQ * b, SEQ * b + SEQ)
                        last = pe.matmul(out[:, :, cols], v2[rows, m, u, b, :], pT[rows, u % 2, :, cols],
                                         start=True, stop=True)
                    banks.fill(last, name, n, u)

            def body(turn, more):
                for n in range(QUAD):
                    for u in range(QUAD):
                        unit(turn, n, u, more)
                if more:
                    next_piece(turn, "v")
                    project_v(turn, ("v", QUAD - 1), 0)
                out_projection(turn, QUAD - 1, QUAD - 1)

            q_low.wait(pe, 0, len(PIECES) - 1)
            for place, which, step in FIRST:
                if which is None:
                    project_k(0, place, step)
                else:
                    project_q(0, place, step, which)
            project_v(0, ("v", "first"), 0)
            rope_sum.wait(pe, 0, 4)
            scores(0, ("score", "first"), 0, 0)
            with pe.Fori(0, KV - 1) as turn:
                body(turn, True)
            body(KV - 1, False)

        @block.scalar
        def _(act):
            def high_of(piece):
                raw, high, _ = raw_high_low(piece)
                q_high.send(act.activation(high, raw, ACT.Copy))

            def exponentials(turn, place, slot):
                flat = s[:, slot, :, :].rearrange("p h k -> p (h k)")
                banks.wait_drained(act, turn, *place)
                exp_ready.send(act.activation(flat, flat, ACT.Exp, scale=float(HD) ** -0.5))

            def copy_v(turn, step, m):
                banks.wait_filled(act, turn, *step)
                for half in range(2):
                    for b in range(2):
                        src = banks.bank(*step)[SEQ * b:SEQ * b + SEQ, :].rearrange("p (t n) -> p t n", t=QUAD)
                        last = act.activation(v2[SEQ * half:SEQ * half + SEQ, m, :, b, :], src, ACT.Copy)
                banks.drain(last, *step)

            def body(turn, more):
                for n in range(QUAD):
                    for u in range(QUAD):
                        if more or (n, u) != (QUAD - 1, QUAD - 1):
                            exponentials(turn, ("score", n, u), (u + 1) % 2)
                        if (n, u) == (0, 0):
                            o_loaded.wait(act, turn, 0)
                            banks.wait_all_filled(act, turn, 7)
                            for h in range(GROUP):
                                o_high.send(act.activation(woh[:, h, :], raw_o[:, h, :], ACT.Copy))
                        banks.wait_filled(act, turn, "turn", n, u)
                        banks.drain(act.activation(pT[:, u % 2, :, :].rearrange("p h k -> p (h k)"),
                                                   banks.bank("turn", n, u)[:, 0:2 * P], ACT.Copy), "turn", n, u)
                        if n < QUAD - 1 and u == QUAD - 1:
                            copy_v(turn, ("v", n), (n + 1) % 2)
                        for half, name in enumerate(("even", "odd")):
                            banks.wait_filled(act, turn, name, n, u)
                            oT_high.send(act.activation(
                                oTh[:, u % 2, :, :].rearrange("p (a b) t -> p a b t", b=2)[:, :, half, :],
                                banks.bank(name, n, u)[:, 0:2 * P].rearrange("p (h t) -> p h t", h=2), ACT.Copy))
                        if more and n == QUAD - 2:
                            if u == 0:
                                q_loaded.wait(act, turn, 1)
                            for piece in SPLIT_IN[u]:
                                if piece in ("k", "v"):
                                    banks.wait_filled(act, turn, piece, n)
                                elif piece == "q0":
                                    banks.wait_filled(act, turn, "q", n - 1, QUAD - 1)
                                else:
                                    banks.wait_filled(act, turn, "q", n, int(piece[1]) - 1)
                                high_of(piece)
                if more:
                    copy_v(turn, ("v", QUAD - 1), 0)

            q_loaded.wait(act, 0, 0)
            for piece in PIECES:
                high_of(piece)
            copy_v(0, ("v", "first"), 0)
            exponentials(0, ("score", "first"), 0)
            with act.Fori(0, KV - 1) as turn:
                body(turn, True)
            body(KV - 1, False)

        @block.gpsimd
        def _(pool):
            banks.open(pool)
            def add_rotation(turn, step, slot, dst):
                banks.wait_drained(pool, turn, *step)
                rope_sum.send(pool.tensor_tensor(dst, straight[:, slot, :], rot[:, slot, :], ALU.add))

            def low_of(turn, first, piece):
                q_high.wait(pool, turn, first + PIECES.index(piece))
                raw, high, low = raw_high_low(piece)
                q_low.send(pool.tensor_tensor(low, raw, high, ALU.subtract))

            def rotated(which, step):
                return k[:, step % 2, :] if which is None else q[:, step % 2, which, :]

            def divide(turn, i, slot):
                rec_ready.wait(pool, turn, i)
                p_ready.send(pool.tensor_tensor(p[:, slot, :, :], s[:, slot, :, :],
                                                rec[:, slot, :].unsqueeze(2).to_broadcast([P, GROUP, SEQ]),
                                                ALU.mult))

            def body(turn, more):
                for n in range(QUAD):
                    for u in range(QUAD):
                        if more or (n, u) != (QUAD - 1, QUAD - 1):
                            divide(turn, QUAD * n + u + 1, (u + 1) % 2)
                        if (n, u) == (0, 0):
                            for h in range(GROUP):
                                o_high.wait(pool, turn, h)
                                o_low.send(pool.tensor_tensor(wol[:, h, :], raw_o[:, h, :], woh[:, h, :],
                                                              ALU.subtract))
                        for i, place, which, step in projections(n, u, more):
                            add_rotation(turn, place, (len(FIRST) + i) % 2, rotated(which, step))
                        if more and n == QUAD - 2:
                            for piece in SPLIT_IN[u]:
                                low_of(turn, len(PIECES), piece)

            for piece in PIECES:
                low_of(0, 0, piece)
            for i, (place, which, step) in enumerate(FIRST):
                add_rotation(0, place, i % 2, rotated(which, step))
            divide(0, 0, 0)
            with pool.Fori(0, KV - 1) as turn:
                body(turn, True)
            body(KV - 1, False)

        @block.vector
        def _(dve):
            def rotate(turn, k_at, slot, step, n):
                if k_at >= 2:
                    rope_sum.wait(dve, turn, k_at - 2)
                banks.wait_filled(dve, turn, *step)
                src = banks.bank(*step)
                dve.tensor_tensor(straight[:, slot, :], src, w["cos"][:, tokens(n)], ALU.mult)
                dve.tensor_tensor(rot[0:64, slot, :], src[64:128, :], w["sin"][64:128, tokens(n)], ALU.mult)
                banks.drain(dve.tensor_tensor(rot[64:128, slot, :], src[0:64, :], w["sin"][0:64, tokens(n)],
                                              ALU.mult), *step)

            def softmax(turn, st, place, slot, i):
                banks.wait_filled(dve, turn, *place)
                scores = banks.bank(*place)[:, 0:GROUP * SEQ].rearrange("p (h k) -> p h k", k=SEQ)
                st.link(dve.tensor_reduce(mx[:, slot, :], scores, AX.X, ALU.max))
                banks.drain(dve.tensor_tensor(s[:, slot, :, :], scores,
                                              mx[:, slot, :].unsqueeze(2).to_broadcast([P, GROUP, SEQ]),
                                              ALU.subtract), *place)
                exp_ready.wait(dve, turn, i)
                st.link(dve.tensor_reduce(tot[:, slot, :], s[:, slot, :, :], AX.X, ALU.add))
                rec_ready.send(dve.reciprocal(rec[:, slot, :], tot[:, slot, :]))

            def lows(turn, n, u):
                for half, name in enumerate(("even", "odd")):
                    oT_high.wait(dve, turn, 2 * (QUAD * n + u) + half)
                    mine = [t[:, u % 2, :, :].rearrange("p (a b) t -> p a b t", b=2)[:, :, half, :] for t in (oTl, oTh)]
                    banks.drain(dve.tensor_tensor(
                        mine[0], banks.bank(name, n, u)[:, 0:2 * P].rearrange("p (h t) -> p h t", h=2), mine[1],
                        ALU.subtract), name, n, u)

            def add_out(turn, n, u):
                banks.wait_filled(dve, turn, "out", n, u)
                tile = w["X"][:, n * QUAD + u, :]
                banks.drain(dve.scalar_tensor_tensor(out=tile, in0=banks.bank("out", n, u),
                                                     scalar=w["gates"][:, 3:4], in1=tile, op0=ALU.mult, op1=ALU.add),
                            "out", n, u)

            def body(turn, more):
                st = Steps(dve, dve_step, LAST_STEPS, turn)
                banks.wait_all_drained(dve, turn, 7)
                for n in range(QUAD):
                    for u in range(QUAD):
                        if (n, u) != (0, 0):
                            prev = (n, u - 1) if u else (n - 1, QUAD - 1)
                            lows(turn, *prev)
                        if more or (n, u) != (QUAD - 1, QUAD - 1):
                            softmax(turn, st, ("score", n, u), (u + 1) % 2, QUAD * n + u + 1)
                        for i, place, _, step in projections(n, u, more):
                            rotate(turn, len(FIRST) + i, (len(FIRST) + i) % 2, place, step)
                        if (n, u) != (0, 0):
                            add_out(turn, *prev)
                lows(turn, QUAD - 1, QUAD - 1)
                add_out(turn, QUAD - 1, QUAD - 1)
                if more:
                    st.close()

            for i, (place, _, step) in enumerate(FIRST):
                rotate(0, i, i % 2, place, step)
            softmax(0, Steps(dve, first_step, 2, 0), ("score", "first"), 0, 0)
            with dve.Fori(0, KV - 1) as turn:
                body(turn, True)
            body(KV - 1, False)




def last_ffn(nc, io, w):
    plan = [(("turn", j), j % 2) for j in range(QUAD)]
    plan += [(("route", j), 2 + j % 2) for j in range(QUAD)]
    for j in range(QUAD):
        plan += [(("hturn", j), j % 2), (("out", j), 4 + j)]
    with ExitStack() as ctx:
        def sb(name, shape, dt=F32):
            return ctx.enter_context(nc.sbuf_tensor("lf_" + name, shape, dt))

        def signal(name, per_turn, by=1):
            return Signal(nc, w, "lf_" + name, per_turn, by)

        xn, xout = sb("xn", [P, QUAD, D]), sb("xout", [P, QUAD, D])
        stats, mv = sb("stats", [P, QUAD, 6]), sb("mv", [P, QUAD, 2])
        vare, rstd = sb("vare", [P, QUAD]), sb("rstd", [P, QUAD])
        xTh, xTl = sb("xTh", [P, QUAD, C, P], HALF), sb("xTl", [P, QUAD, C, P], HALF)
        e, pick = sb("e", [P, QUAD, 10]), sb("pick", [P, QUAD, 8])
        low4 = sb("low4", [P, QUAD, 8])
        top8, keep = sb("top8", [P, QUAD, 8]), sb("keep", [P, QUAD, 10])
        rh = sb("rh", [P, QUAD, R3 + LORA3])
        sel, comb = sb("sel", [P, QUAD, R3]), sb("comb", [P, QUAD, R3])
        nmax, tot, rec = sb("nmax", [P, QUAD]), sb("tot", [P, QUAD]), sb("rec", [P, QUAD])
        hs, hsT = sb("hs", [P, QUAD, LORA3]), sb("hsT", [LORA3, QUAD, P])
        banks = Banks(nc, ctx, w, "lf", plan)
        stats_ready, rstd_ready, xn_ready = signal("stats_ready", 4), signal("rstd_ready", 4), signal("xn_ready", 4)
        xT_high, logit_ready, expo_ready = signal("xT_high", 4), signal("logit_ready", 4), signal("expo_ready", 4)
        stored, hs_ready = signal("stored", 4, 16), signal("hs_ready", 4)
        dve_step = new_semaphore(nc, w, "lf_dve_step")
        pool_step = new_semaphore(nc, w, "lf_pool_step")
        pads = new_semaphore(nc, w, "lf_pads")
        block = ctx.enter_context(nc.Block())

        @block.sync
        def _(sp):
            with sp.Fori(0, TURNS) as turn:
                for j in range(QUAD):
                    banks.wait_drained(sp, turn, "out", j)
                    stored.send(sp.dma_start(io["out"][bass.ts(turn * QUAD + j, P), :], xout[:, j, :]))
            sp.wait_ge(stored.sem, TURNS * QUAD * 16 + 1)

        @block.gpsimd
        def _(pool):
            banks.open(pool)
            pool.sem_inc(stored.sem, 1)
            pool.memset(e[:, :, :], NEVER).then_inc(pads, 1)
            pool.memset(pick[:, :, :], NEVER).then_inc(pads, 1)
            pool.memset(low4[:, :, :], 0.0).then_inc(pads, 1)
            with pool.Fori(0, TURNS) as turn:
                for j in range(QUAD):
                    stats_ready.wait(pool, turn, j)
                    pool.tensor_tensor(vare[:, j:j + 1], mv[:, j, 1:2], w["eps"][:, :], ALU.add)\
                        .then_inc(pool_step, 1)
                    pool.wait_ge(pool_step, turn * QUAD + (j + 1))
                    rstd_ready.send(pool.tensor_tensor(rstd[:, j:j + 1], vare[:, j:j + 1], w["power"][:, 0:1],
                                                       ALU.pow))

        @block.tensor
        def _(pe):
            apart = Apart(pe, pads, 3)
            with pe.Fori(0, TURNS) as turn:
                for j in range(QUAD):
                    xn_ready.wait(pe, turn, j)
                    banks.wait_free(pe, turn, "turn", j)
                    for c in range(C):
                        last = pe.transpose(banks.bank("turn", j)[:, c * P:(c + 1) * P],
                                            xn[:, j, c * P:(c + 1) * P], w["ident"][:, :])
                    banks.fill(last, "turn", j)
                for j in range(QUAD):
                    banks.wait_drained(pe, turn, "turn", j)
                    banks.wait_free(pe, turn, "route", j)
                    banks.fill(three(pe, banks.bank("route", j)[:, 0:R3 + LORA3],
                                     [xTh[:, j, c, :] for c in range(C)], [xTl[:, j, c, :] for c in range(C)],
                                     [w["R3h"][:, c, :] for c in range(C)], [w["R3l"][:, c, :] for c in range(C)]),
                               "route", j)
                for j in range(QUAD):
                    hs_ready.wait(pe, turn, j)
                    banks.wait_free(apart, turn, "hturn", j)
                    banks.fill(pe.transpose(banks.bank("hturn", j)[0:LORA3, 0:P], hs[:, j, :], w["ident"][:, :]),
                               "hturn", j)
                    banks.wait_drained(pe, turn, "hturn", j)
                    banks.wait_free(pe, turn, "out", j)
                    banks.fill(pe.matmul(banks.bank("out", j), hsT[:, j, :], w["B3"][:, :], start=True, stop=True),
                               "out", j)

        @block.scalar
        def _(act):
            act.wait_ge(pads, 3)
            with act.Fori(0, TURNS) as turn:
                for j in range(QUAD):
                    banks.wait_filled(act, turn, "turn", j)
                    xT_high.send(act.activation(xTh[:, j, :, :].rearrange("p c n -> p (c n)"), banks.bank("turn", j),
                                                ACT.Copy))
                for j in range(QUAD):
                    banks.wait_filled(act, turn, "route", j)
                    banks.drain(act.activation(rh[:, j, :], banks.bank("route", j)[:, 0:R3 + LORA3], ACT.Copy),
                                "route", j)
                for j in range(QUAD):
                    logit_ready.wait(act, turn, j)
                    expo_ready.send(act.activation(e[:, j, 0:R3], rh[:, j, 0:R3], ACT.Exp, bias=nmax[:, j:j + 1]))
                for j in range(QUAD):
                    banks.wait_filled(act, turn, "hturn", j)
                    banks.drain(act.activation(hsT[:, j, :], banks.bank("hturn", j)[0:LORA3, 0:P], ACT.Copy),
                                "hturn", j)

        @block.vector
        def _(dve):
            apart = Apart(dve, pads, 3)
            dve.wait_ge(pads, 3)
            with dve.Fori(0, TURNS) as turn:
                st = Steps(dve, dve_step, FFN_STEPS, turn)

                def each(make, after=None):
                    made = []
                    for j in range(QUAD):
                        if after:
                            st.after(after[j], apart)
                        made.append(st.step(make(j)))
                    return made

                def x_of(j):
                    return w["X"][:, bass.ds(turn * QUAD + j, 1), :]
                got = each(lambda j: dve.bn_stats(stats[:, j, :], x_of(j)))
                for j in range(QUAD):
                    st.after(got[j], apart)
                    stats_ready.send(dve.bn_aggr(mv[:, j, :], stats[:, j, :]))
                for j in range(QUAD):
                    rstd_ready.wait(dve, turn, j)
                    xn_ready.send(dve.tensor_scalar(xn[:, j, :], x_of(j), mv[:, j, 0:1], rstd[:, j:j + 1],
                                                    ALU.subtract, ALU.mult))
                for j in range(QUAD):
                    xT_high.wait(dve, turn, j)
                    banks.drain(dve.tensor_tensor(xTl[:, j, :, :].rearrange("p c n -> p (c n)"),
                                                  banks.bank("turn", j),
                                                  xTh[:, j, :, :].rearrange("p c n -> p (c n)"), ALU.subtract),
                                "turn", j)

                for j in range(QUAD):
                    banks.wait_drained(dve, turn, "route", j)
                    logit_ready.send(dve.tensor_reduce(nmax[:, j:j + 1], rh[:, j, 0:R3], AX.X, ALU.max, negate=True))

                def copy4(j):
                    expo_ready.wait(dve, turn, j)
                    return dve.tensor_copy(low4[:, j, 0:R3], e[:, j, 0:R3])
                got = each(copy4)
                got = each(lambda j: dve.max(top8[:, j, :], low4[:, j, :]), got)
                each(lambda j: dve.tensor_tensor(tot[:, j:j + 1], top8[:, j, 0:1], top8[:, j, 1:2], ALU.add), got)
                got = each(lambda j: dve.tensor_copy(pick[:, j, 0:2], top8[:, j, 0:2]), got)
                got = each(lambda j: dve.reciprocal(rec[:, j:j + 1], tot[:, j:j + 1]), got)
                got = each(lambda j: dve.match_replace(keep[:, j, :], pick[:, j, :], e[:, j, :], 0.0), got)
                got = each(lambda j: dve.tensor_tensor(sel[:, j, :], e[:, j, 0:R3], keep[:, j, 0:R3],
                                                       ALU.subtract), got)
                got = each(lambda j: dve.tensor_scalar(comb[:, j, :], sel[:, j, :], rec[:, j:j + 1], 4.0,
                                                       ALU.mult, ALU.mult), got)
                for j in range(QUAD):
                    st.after(got[j])
                    hs_ready.send(dve.tensor_tensor(
                        hs[:, j, :].rearrange("p (e r) -> p e r", r=RANK),
                        rh[:, j, R3:R3 + LORA3].rearrange("p (e r) -> p e r", r=RANK),
                        comb[:, j, :].unsqueeze(2).to_broadcast([P, E3, RANK]), ALU.mult))
                for j in range(QUAD):
                    banks.wait_filled(dve, turn, "out", j)
                    dve.wait_ge(stored.sem, turn * (QUAD * 16) + 1)
                    banks.drain(dve.scalar_tensor_tensor(
                        out=xout[:, j, :].unsqueeze(1), in0=banks.bank("out", j).unsqueeze(1),
                        scalar=w["gates"][:, 7:8], in1=x_of(j), op0=ALU.mult, op1=ALU.add), "out", j)
                st.close()


def build(nc, io):
    with ExitStack() as whole:
        def keep(stack, name, shape, dt=F32):
            w[name] = stack.enter_context(nc.sbuf_tensor("w_" + name, shape, dt))

        w = {}
        for name, shape, dt in (("gates", [P, 8], F32), ("ident", [P, P], F32), ("identh", [P, P], BF16),
                                ("power", [P, 1], F32), ("eps", [P, 1], F32), ("R3h", [P, C, R3 + LORA3], HALF),
                                ("R3l", [P, C, R3 + LORA3], HALF), ("B3", [LORA3, D], F32)):
            keep(whole, name, shape, dt)
        io["x_mid"] = nc.dram_tensor("x_mid", (TOKENS, D), F32).ap()
        with ExitStack() as early:
            for name, cols in (("M", D), ("W0", D), ("W1", D), ("R0", R0 + LORA), ("R1", R1 + LORA), ("Wqd", 64),
                               ("Wkv", P)):
                for half in "hl":
                    keep(early, name + half, [P, C, cols], HALF)
            for name, shape, dt in (
                    ("ch", [P, C], HALF), ("cl", [P, C], HALF), ("r", [P, C], F32), ("s", [P, 1], F32),
                    ("bdmask", [P, P], F32), ("B0", [LORA, D], F32), ("B1", [LORA, D], F32),
                    ("L1W", [P, 4, P], F32), ("L1b", [P, 4], F32), ("rb1", [P, R1], F32),
                    ("route_to", [P, E01, R1], F32), ("expert_id", [P, E01, R1], F32), ("gbias", [P, 3, D], F32),
                    ("Wqk", [64, D], F32), ("Wvu", [L2K, D], F32), ("quarter", [P, 4], F32),
                    ("gate2", [P, C, E01], F32), ("ics", [E01, D], F32), ("ocs", [E01, D], F32),
                    ("sign2", [P, C, D], BF16)):
                keep(early, name, shape, dt)
            with stage(nc, w):
                prepare_weights(nc, io, w)
            with stage(nc, w):
                early_layers(nc, io, w)
        keep(whole, "X", [P, TILES, D])
        with ExitStack() as attention:
            for name in ("xTh", "xTl", "cTh", "cTl"):
                keep(attention, name, [P, C, TOKENS], HALF)
            keep(attention, "cos", [P, TOKENS])
            keep(attention, "sin", [P, TOKENS])
            keep(attention, "mask", [P, TILES, SEQ], BF16)
            with stage(nc, w):
                prepare_last(nc, io, w)
            with stage(nc, w):
                last_attention(nc, io, w)
        with stage(nc, w):
            last_ffn(nc, io, w)


def rope_tables():
    inv = (1.0 / np.float32(10000.0) ** (np.arange(0, HD, 2, dtype=np.float32) / np.float32(HD))).astype(np.float32)
    angle = np.arange(POSITIONS, dtype=np.float32)[:, None] * inv[None, :]
    cos, sin = np.cos(angle).astype(np.float32), np.sin(angle).astype(np.float32)
    return np.concatenate([cos, cos], 1), np.concatenate([sin, -sin], 1)


def layout(i):
    a = {k: np.asarray(v) for k, v in i.items()}
    cos, sin = rope_tables()
    two = (TOKENS, D)
    return {
        "x": a["x"].reshape(two), "ctx": a["ctx_4096"].reshape(two), "ctxT": a["ctx_4096"].reshape(two).T,
        "pos": a["pos_BxS2"].reshape(TOKENS), "mask": a["mask_BxSxS2_ik0"].reshape(TOKENS, SEQ),
        "gates": np.concatenate([a["g_xattn"], a["g_ffn"]]),
        "L0_Wq": a["L0_xattn_Wq"], "L0_Wk": a["L0_xattn_Wk"],
        "L0_bq": a["L0_xattn_bq"].reshape(C, P).T, "L0_bk": a["L0_xattn_bk"].reshape(C, P).T,
        "W0": a["L0_ffn_W_base"].T, "b0": a["L0_ffn_b_base"],
        "R0": np.concatenate([a["L0_ffn_W_router"], a["L0_ffn_A_stack"].reshape(LORA, D)]).T,
        "B0": a["L0_ffn_B_stack"].transpose(0, 2, 1).reshape(LORA, D),
        "L1W": np.stack([a["L1_xattn_" + n].T for n in ("Wq", "Wk", "Wv", "Wo")]),
        "L1b": np.stack([a["L1_xattn_" + n].reshape(SEQ, 1) for n in ("bq", "bk", "bv", "bo")]),
        "W1": a["L1_ffn_base_W"].T, "b1": a["L1_ffn_base_b"], "rb1": a["L1_ffn_router_b"],
        "R1": np.concatenate([a["L1_ffn_router_W"], a["L1_ffn_A"].reshape(LORA, D)]).T,
        "B1": a["L1_ffn_B"].transpose(0, 2, 1).reshape(LORA, D), "emap": a["L1_ffn_expert_map"],
        "Wqd": a["L2_xattn_Wq_d"], "Wkv": np.tile(a["L2_xattn_Wkv_d"], (1, 4)), "Wqk": a["L2_xattn_W_qk"],
        "Wvu": a["L2_xattn_Wv_u"].reshape(L2K, 8, 2, 32).transpose(0, 2, 1, 3).reshape(L2K, D),
        "W2": a["L2_ffn_weight"].T, "b2": a["L2_ffn_bias"], "gate2": a["L2_ffn_gate_w"].T,
        "ics": a["L2_ffn_in_channel_scale"], "ocs": a["L2_ffn_out_channel_scale"],
        "Wq3": a["L3_xattn_Wq"], "Wk3": a["L3_xattn_Wk"], "Wv3": a["L3_xattn_Wv"], "Wo3": a["L3_xattn_Wo"],
        "R3": np.concatenate([a["L3_ffn_Wr"], a["L3_ffn_A"].reshape(LORA3, D)]).T,
        "B3": a["L3_ffn_B"].transpose(0, 2, 1).reshape(LORA3, D),
        "cos": cos, "sin": sin,
    }


def kernel(**inputs):
    import concourse.bacc as bacc
    from concourse.bass_utils import run_bass_kernel_spmd

    nc = bacc.Bacc("TRN2", target_bir_lowering=False, num_devices=1)
    arrays, io = {}, {}
    for name, a in layout(inputs).items():
        a = np.ascontiguousarray(a)
        arrays["in_" + name] = a
        io[name] = nc.dram_tensor("in_" + name, a.shape, mybir.dt.from_np(a.dtype), kind="ExternalInput").ap()
    io["out"] = nc.dram_tensor("out_0", (TOKENS, D), F32, kind="ExternalOutput").ap()
    build(nc, io)
    result = run_bass_kernel_spmd(nc, [arrays], core_ids=[0])
    return result.results[0]["out_0"].reshape(BATCH, SEQ, D)
```

```python
from contextlib import ExitStack, contextmanager

import numpy as np

import concourse.bass as bass
from concourse import mybir

F32 = mybir.dt.float32
I32 = mybir.dt.int32
HALF = mybir.dt.bfloat16
BF16 = mybir.dt.bfloat16
ALU = mybir.AluOpType
ACT = mybir.ActivationFunctionType
AX = mybir.AxisListType

P = 128
D = 512
C = D // P
SEQ = 64
BATCH = 32
TOKENS = BATCH * SEQ
TILES = TOKENS // P
QUAD = 4
TURNS = TILES // QUAD
EIGHT = 8
EPS = 1e-5

R0, R1, R3 = 8, 15, 4
E01, RANK, E3 = 8, 16, 4
LORA, LORA3 = E01 * RANK, E3 * RANK

WIN, CH, TC = 16, 8, 8
TP = D // TC
PADDED = 8 + D + 8
HALO = TP + WIN

H2, L2K = 16, 32
KV, GROUP, HD = 8, 4, 128
POSITIONS = 512
MASKED = -float(2.0 ** 100)
NEVER = 4.0


def new_semaphore(nc, w, name):
    handle = w["stack"].enter_context(nc.semaphore(name))
    w["semaphores"].append(handle)
    return handle


@contextmanager
def stage(nc, w):
    with ExitStack() as stack:
        w["stack"], w["semaphores"] = stack, []
        yield
        for handle in w["semaphores"]:
            nc.gpsimd.sem_clear(handle)
        nc.all_engine_barrier()


def prepare_weights(nc, io, w):
    with ExitStack() as ctx:
        def sb(name, shape, dt=F32):
            return ctx.enter_context(nc.sbuf_tensor("prep_" + name, shape, dt))

        def sem(name):
            return new_semaphore(nc, w, "prep_" + name)

        raw = {}
        for name, cols in (("W0", D), ("W1", D), ("W2", D), ("R0", R0 + LORA), ("R1", R1 + LORA),
                           ("Wqd", 64), ("Wkv", P), ("R3", R3 + LORA3)):
            raw[name] = sb(name, [P, C, cols])
        wq, wk = sb("Wq", [P, C, D]), sb("Wk", [P, C, D])
        bq, bk = sb("bq", [P, C]), sb("bk", [P, C])
        gates_raw = sb("gates", [P, 8])
        bias_raw = sb("bias", [P, 3, D])
        emap, emap_f = sb("emap", [P, R1], I32), sb("emap_f", [P, R1])
        negative = sb("negative", [P, C, D])
        eight = sb("eight", [P, E01])
        ps = ctx.enter_context(nc.psum_tensor("prep_ps", [P, 8, D], F32))
        loaded, zeroed, made, product_ready = sem("loaded"), sem("zeroed"), sem("made"), sem("product_ready")
        split_high, pool_step, gate_ready = sem("split_high"), sem("pool_step"), sem("gate_ready")
        direct, raw_high = sem("direct"), sem("raw_high")

        RAW = ["W0", "R0", "W1", "R1", "Wqd", "Wkv", "R3"]
        raw_loaded = {name: sem(name + "_loaded") for name in RAW + ["W2"]}
        gates_loaded, rest_loaded = sem("gates_loaded"), sem("rest_loaded")
        FIRST = 4 * 16
        block = ctx.enter_context(nc.Block())

        @block.sync
        def _(sp):
            sp.dma_start(wq[:, :, :], io["L0_Wq"].rearrange("(c p) n -> p c n", p=P)).then_inc(loaded, 16)
            sp.dma_start(wk[:, :, :], io["L0_Wk"].rearrange("(c p) n -> p c n", p=P)).then_inc(loaded, 16)
            sp.dma_start(bq[:, :], io["L0_bq"]).then_inc(loaded, 16)
            sp.dma_start(bk[:, :], io["L0_bk"]).then_inc(loaded, 16)
            sp.dma_start(gates_raw[:, :], io["gates"].partition_broadcast(P)).then_inc(gates_loaded, 16)
            for name in RAW + ["W2"]:
                sp.dma_start(raw[name][:, :, :], io[name].rearrange("(c p) n -> p c n", p=P))\
                  .then_inc(raw_loaded[name], 16)
            for k, name in enumerate(("b0", "b1", "b2")):
                sp.dma_start(bias_raw[:, k, :], io[name].partition_broadcast(P)).then_inc(rest_loaded, 16)
            sp.dma_start(emap[:, :], io["emap"].partition_broadcast(P)).then_inc(rest_loaded, 16)
            for name in ("B0", "B1", "Wqk", "Wvu", "ics", "ocs", "B3"):
                sp.dma_start(w[name][:, :], io[name]).then_inc(direct, 16)
            sp.dma_start(w["gate2"][:, :, :], io["gate2"].rearrange("(c p) n -> p c n", p=P)).then_inc(direct, 16)
            sp.dma_start(w["rb1"][:, :], io["rb1"].partition_broadcast(P)).then_inc(direct, 16)
            sp.wait_ge(zeroed, 1)
            for b in range(2):
                rows = slice(SEQ * b, SEQ * b + SEQ)
                sp.dma_start(w["L1W"][rows, :, rows], io["L1W"].rearrange("k p n -> p k n")).then_inc(direct, 16)
                sp.dma_start(w["L1b"][rows, :], io["L1b"]).then_inc(direct, 16)
            sp.wait_ge(direct, 16 * (9 + 4))

        @block.gpsimd
        def _(pool):
            st = Steps(pool, pool_step, 12, 0)
            st.link(pool.memset(w["ident"][:, :], 0.0))
            st.link(pool.memset(w["bdmask"][:, :], MASKED))
            st.link(pool.memset(w["power"][:, :], -0.5))
            st.link(pool.memset(w["eps"][:, :], EPS))
            st.link(pool.memset(w["quarter"][:, :], 1.0))
            st.link(pool.iota(w["expert_id"][:, :, :], pattern=[[1, E01], [0, R1]], base=0, channel_multiplier=0,
                              allow_small_or_imprecise_dtypes=True))
            st.link(pool.affine_select(out=w["ident"][:, :], in_=w["ident"][:, :], compare_op=ALU.not_equal,
                                       fill=1.0, base=0, pattern=[[-1, P]], channel_multiplier=1))
            for b in range(2):
                rows = w["bdmask"][SEQ * b:SEQ * b + SEQ, SEQ * b:SEQ * b + SEQ]
                st.link(pool.memset(rows, 0.0))
            st.link(pool.affine_select(out=w["quarter"][:, :], in_=w["quarter"][:, :], compare_op=ALU.is_ge,
                                       fill=0.0, base=0, pattern=[[-L2K, 4]], channel_multiplier=1))
            st.link(pool.affine_select(out=w["quarter"][:, :], in_=w["quarter"][:, :], compare_op=ALU.is_ge,
                                       fill=0.0, base=L2K - 1, pattern=[[L2K, 4]], channel_multiplier=-1))
            st.link(pool.tensor_copy(w["identh"][:, :], w["ident"][:, :]))
            st.close()

        @block.tensor
        def _(pe):
            pe.wait_ge(loaded, FIRST)
            for m in range(C):
                for c in range(C):
                    last = pe.matmul(ps[:, m, :], wq[:, c, m * P:(m + 1) * P], wk[:, c, :],
                                     start=(c == 0), stop=(c == C - 1))
                last.then_inc(product_ready, 1)
            for m in range(C):
                for c in range(C):
                    pe.matmul(ps[:, 4, m:m + 1], wk[:, c, m * P:(m + 1) * P], bq[:, c:c + 1],
                              start=(c == 0), stop=(c == C - 1))
            for m in range(C):
                for c in range(C):
                    pe.matmul(ps[:, 5, m:m + 1], wq[:, c, m * P:(m + 1) * P], bk[:, c:c + 1],
                              start=(c == 0), stop=(c == C - 1))
            for c in range(C):
                last = pe.matmul(ps[:, 6, 0:1], bq[:, c:c + 1].to_broadcast([P, P]), bk[:, c:c + 1],
                                 start=(c == 0), stop=(c == C - 1))
            last.then_inc(product_ready, 1)

        @block.scalar
        def _(act):
            act.wait_ge(gates_loaded, 16)
            act.activation(w["gates"][:, :], gates_raw[:, :], ACT.Tanh).then_inc(gate_ready, 1)
            for name in RAW:
                act.wait_ge(raw_loaded[name], 16)
                act.activation(w[name + "h"][:, :, :], raw[name][:, :, :], ACT.Copy).then_inc(raw_high, 1)
            for m in range(C):
                act.wait_ge(product_ready, m + 1)
                act.activation(w["Mh"][:, m, :], ps[:, m, :], ACT.Copy).then_inc(split_high, 1)
            act.wait_ge(product_ready, C + 1)
            act.activation(w["ch"][:, :], ps[:, 5, 0:C], ACT.Copy).then_inc(split_high, 1)

        @block.vector
        def _(dve):
            dve.memset(w["L1W"][:, :, :], 0.0).then_inc(zeroed, 1)
            for k, name in enumerate(RAW):
                dve.wait_ge(raw_high, k + 1)
                dve.tensor_tensor(w[name + "l"][:, :, :], raw[name][:, :, :], w[name + "h"][:, :, :], ALU.subtract)
            dve.wait_ge(raw_loaded["W2"], 16)
            dve.tensor_scalar(negative[:, :, :], raw["W2"][:, :, :], 0.0, None, ALU.is_lt).then_inc(made, 1)
            dve.wait_ge(made, 1)
            dve.scalar_tensor_tensor(out=w["sign2"][:, :, :], in0=raw["W2"][:, :, :], scalar=0.0,
                                     in1=negative[:, :, :], op0=ALU.is_gt, op1=ALU.subtract)
            dve.wait_ge(gate_ready, 1)
            dve.wait_ge(rest_loaded, 64)
            for k in range(3):
                dve.tensor_scalar(w["gbias"][:, k, :], bias_raw[:, k, :], w["gates"][:, 4 + k:5 + k], None,
                                  ALU.mult)
            dve.tensor_copy(emap_f[:, :], emap[:, :]).then_inc(made, 1)
            dve.wait_ge(made, 2)
            dve.wait_ge(pool_step, 6)
            dve.tensor_tensor(w["route_to"][:, :, :], w["expert_id"][:, :, :],
                              emap_f[:, :].unsqueeze(1).to_broadcast([P, E01, R1]), ALU.is_equal)
            for m in range(C):
                dve.wait_ge(split_high, m + 1)
                dve.tensor_tensor(w["Ml"][:, m, :], ps[:, m, :], w["Mh"][:, m, :], ALU.subtract)
            dve.wait_ge(split_high, C + 1)
            dve.tensor_tensor(w["cl"][:, :], ps[:, 5, 0:C], w["ch"][:, :], ALU.subtract)
            dve.tensor_copy(w["r"][:, :], ps[:, 4, 0:C])
            dve.tensor_copy(w["s"][:, :], ps[:, 6, 0:1])


class Banks:

    def __init__(self, nc, ctx, w, prefix, plan, before=()):
        used = sorted({bank for _, bank in plan})
        self.filled = {b: new_semaphore(nc, w, f"{prefix}_filled{b}") for b in used}
        self.drained = {b: new_semaphore(nc, w, f"{prefix}_drained{b}") for b in used}
        self.ps = ctx.enter_context(nc.psum_tensor(f"{prefix}_ps", [P, 8, D], F32))
        self.at, self.uses = {}, [0] * 8
        self.before = [0] * 8
        for step, bank in before:
            self.at[step] = (bank, self.before[bank])
            self.before[bank] += 1
        for step, bank in plan:
            self.at[step] = (bank, self.before[bank] + self.uses[bank])
            self.uses[bank] += 1

    def open(self, pool):
        for b in self.filled:
            pool.sem_inc(self.filled[b], 1)
            pool.sem_inc(self.drained[b], 1)

    def bank(self, *step):
        return self.ps[:, self.at[step][0], :]

    def wait_free(self, eng, turn, *step):
        b, k = self.at[step]
        eng.wait_ge(self.drained[b], turn * self.uses[b] + (k + 1))

    def wait_filled(self, eng, turn, *step):
        b, k = self.at[step]
        eng.wait_ge(self.filled[b], turn * self.uses[b] + (k + 2))

    def wait_drained(self, eng, turn, *step):
        b, k = self.at[step]
        eng.wait_ge(self.drained[b], turn * self.uses[b] + (k + 2))

    def wait_all_drained(self, eng, turn, b):
        eng.wait_ge(self.drained[b], turn * self.uses[b] + (self.before[b] + 1))

    def wait_all_filled(self, eng, turn, b):
        eng.wait_ge(self.filled[b], turn * self.uses[b] + (self.before[b] + 1))

    def fill(self, ins, *step):
        ins.then_inc(self.filled[self.at[step][0]], 1)

    def drain(self, ins, *step):
        ins.then_inc(self.drained[self.at[step][0]], 1)


class Signal:

    def __init__(self, nc, w, name, per_turn, by=1):
        self.sem, self.per_turn, self.by = new_semaphore(nc, w, name), per_turn, by

    def send(self, ins):
        ins.then_inc(self.sem, self.by)

    def wait(self, eng, turn, k):
        eng.wait_ge(self.sem, turn * (self.per_turn * self.by) + (k + 1) * self.by)


class Steps:

    def __init__(self, eng, sem, per_turn, turn):
        self.eng, self.sem, self.per_turn, self.turn, self.n = eng, sem, per_turn, turn, 0

    def step(self, ins):
        self.n += 1
        ins.then_inc(self.sem, 1)
        return self.n

    def after(self, n, eng=None):
        (eng or self.eng).wait_ge(self.sem, self.turn * self.per_turn + n)

    def link(self, ins):
        self.after(self.step(ins))

    def close(self):
        assert self.n == self.per_turn, ("steps of a turn", self.n)


def three(pe, out, lh, ll, rh, rl, first=True, last=True):
    n = len(lh)
    for c in range(n):
        pe.matmul(out, lh[c], rh[c], start=(first and c == 0), stop=False)
        pe.matmul(out, lh[c], rl[c], start=False, stop=False)
        ins = pe.matmul(out, ll[c], rh[c], start=False, stop=(last and c == n - 1))
    return ins


class Apart:

    def __init__(self, eng, once, n):
        self.eng, self.once, self.n = eng, once, n

    def wait_ge(self, sem, value):
        with self.eng.register() as held:
            self.eng.reg_alu(held, value, 0, ALU.max)
            self.eng.wait_ge(self.once, self.n)
            self.eng.wait_ge(sem, held)


DVE_STEPS, LAST_STEPS, FFN_STEPS = 113, 32, 30


def early_layers(nc, io, w):
    plan = []
    for j in range(QUAD):
        plan.append((("turn", 0, j), j))
    for j in range(QUAD):
        plan.append((("proj0", j), j % 2))
    for j in range(QUAD):
        plan.append((("score0", j), 2 + j % 2))
    for j in range(QUAD):
        plan.append((("prob0", j), j % 2))
        plan.append((("out0", j), 4 + j))
    for f, layer in ((0, 1), (1, 3)):
        if f == 1:
            for j in range(QUAD):
                plan += [(("q1", j), 0), (("k1", j), 1), (("v1", j), 2)]
            for j in range(QUAD):
                plan += [(("dot1", j, 0), 4 + 2 * (j % 2)), (("dot1", j, 1), 5 + 2 * (j % 2)), (("out1", j), 3)]
        for j in range(QUAD):
            plan.append((("turn", layer, j), j))
        for j in range(QUAD):
            plan += [(("route", f, j), j % 2), (("base", f, j), 4 + j)]
        for j in range(QUAD):
            plan.append((("hturn", f, j), 2 + j % 2))
    for j in range(QUAD):
        plan.append((("turn", 4, j), j))
    for j in range(QUAD + 1):
        if j < QUAD:
            plan += [(("low2", j), 2), (("qup2", j), 3), (("vup2", j), 4)]
            plan += [(("score2", j, 0), 6), (("score2", j, 1), 7)]
        if j >= 1:
            plan += [(("prob2", j - 1, 0), 0), (("prob2", j - 1, 1), 1)]
            plan += [(("out2", j - 1, 0), 5), (("out2", j - 1, 1), 4)]
    for j in range(QUAD):
        plan.append((("turn", 5, j), j))
    for j in range(QUAD):
        plan.append((("gate2", j), j % 2))
    for j in range(QUAD):
        plan += [(("gturn", j), (0, 1, 3, 2)[j]), (("scale_in", j), 4 + j % 2), (("scale_out", j), 6 + j % 2)]
    for j in range(QUAD):
        plan.append((("sign2", j), 4 + j))

    with ExitStack() as ctx:
        def sb(name, shape, dt=F32, stack=ctx):
            return stack.enter_context(nc.sbuf_tensor("early_" + name, shape, dt))

        def signal(name, per_turn, by=1):
            return Signal(nc, w, "early_" + name, per_turn, by)

        xq, xn = sb("xq", [P, QUAD, D]), sb("xn", [P, QUAD, D])
        ctxt = sb("ctxt", [P, QUAD, D])
        cTh, cTl = sb("cTh", [P, QUAD, C, P], HALF), sb("cTl", [P, QUAD, C, P], HALF)
        stats, mv, rstd = sb("stats", [P, QUAD, 6]), sb("mv", [P, QUAD, 2]), sb("rstd", [P, QUAD])
        vare = sb("vare", [P, QUAD])
        u = sb("u", [P, QUAD])
        nmax, tot, rec = sb("nmax", [P, QUAD]), sb("tot", [P, QUAD]), sb("rec", [P, QUAD])
        rh = sb("rh", [P, QUAD, R1 + LORA])
        rkeep, rsel = sb("rkeep", [P, QUAD, 16]), sb("rsel", [P, QUAD, 16])
        e0, e1, e2 = sb("e0", [P, QUAD, 14]), sb("e1", [P, QUAD, R1]), sb("e2", [P, QUAD, E01])
        top8, pick0 = sb("top8", [P, QUAD, 8]), sb("pick0", [P, QUAD, 8])
        rmix = sb("rmix", [P, QUAD, E01, R1])
        comb = sb("comb", [P, QUAD, E01])
        hs, hsT = sb("hs", [P, QUAD, LORA]), sb("hsT", [P, QUAD, P])
        kp, vp = sb("kp", [P, 2, PADDED]), sb("vp", [P, 2, PADDED])
        with ExitStack() as mine:
            qs = sb("qs", [P, 2, D], stack=mine)
            qL = sb("qL", [P, 2, CH, TP], stack=mine)
            kL, vL = sb("kL", [P, 2, CH, HALO], stack=mine), sb("vL", [P, 2, CH, HALO], stack=mine)
            qk = [sb(f"qk{h}", [P, CH, TP // 2, WIN], stack=mine) for h in range(2)]
            pv = [sb(f"pv{h}", [P, CH, TP // 2, WIN], stack=mine) for h in range(2)]
            ee, mx1 = sb("ee", [P, TP, WIN], stack=mine), sb("mx1", [P, TP], stack=mine)
            sum1, rec1 = sb("sum1", [P, TP], stack=mine), sb("rec1", [P, TP], stack=mine)
            oL, oS = sb("oL", [P, 2, CH, TP], stack=mine), sb("oS", [P, 2, D], stack=mine)
            y1 = xn
        xin = sb("xin", [P, QUAD, D])
        cT = sb("cT", [P, QUAD, C, P])
        xTh, xTl = sb("xTh", [P, QUAD, C, P], HALF), sb("xTl", [P, QUAD, C, P], HALF)
        sm, pr, prT = sb("sm", [P, QUAD, P]), sb("pr", [P, QUAD, P]), sb("prT", [P, QUAD, P])
        aT = sb("aT", [P, 2, C, P])
        aTh, aTl = sb("aTh", [P, QUAD, C, P], HALF), sb("aTl", [P, QUAD, C, P], HALF)
        cqT, ckv = sb("cqT", [64, 2, P]), sb("ckv", [P, 2, 2, 4, SEQ])
        qT2, v2 = sb("qT2", [P, 2, 4, P]), sb("v2", [P, 2, 2, 256])
        s2, p2T = sb("s2", [P, 2, H2, SEQ]), sb("p2T", [P, 2, H2 // 2, P])
        mx2, sum2, rec2 = sb("mx2", [P, 2, H2]), sb("sum2", [P, 2, H2]), sb("rec2", [P, 2, H2])
        o2 = sb("o2", [P, 2, H2, 32])
        rT2, osb = sb("rT2", [E01, QUAD, P]), sb("osb", [P, QUAD, D])
        xTf = sb("xTf", [P, QUAD, C, P])
        scr_q = nc.dram_tensor("scr_q", (QUAD, TC, P, TP), F32).ap()
        scr_k = nc.dram_tensor("scr_k", (QUAD, TC, P, HALO), F32).ap()
        scr_v = nc.dram_tensor("scr_v", (QUAD, TC, P, HALO), F32).ap()
        scr_o = nc.dram_tensor("scr_o", (QUAD, P, CH * TP), F32).ap()

        banks = Banks(nc, ctx, w, "early", plan)
        x_loaded = [signal(f"x_loaded{j}", 1, 16) for j in range(QUAD)]
        ctx_loaded = [signal(f"ctx_loaded{j}", 1, 16) for j in range(QUAD)]
        cT_loaded = [signal(f"cT_loaded{j}", 1, 16) for j in range(QUAD)]
        cT_high, cT_split = signal("cT_high", QUAD), signal("cT_split", QUAD)
        stats_ready, rstd_ready, xn_ready = signal("stats_ready", 24), signal("rstd_ready", 24), signal("xn_ready", 24)
        xT_high = signal("xT_high", 16)
        aT_high, aT_split = signal("aT_high", 4), signal("aT_split", 4)
        sm0_ready, pr0_ready = signal("sm0_ready", 4), signal("pr0_ready", 4)
        logit_ready, expo_ready = signal("logit_ready", 12), signal("expo_ready", 12)
        xbias_ready, hs_ready = signal("xbias_ready", 12), signal("hs_ready", 8)
        qk_written, v_written = signal("qk_written", 4, 32), signal("v_written", 4, 16)
        qk_in = [signal(f"qk_in{p}", 2, 32) for p in range(2)]
        v_in = [signal(f"v_in{p}", 2, 16) for p in range(2)]
        qk_dve, qk_pool, pv_pool = signal("qk_dve", 4), signal("qk_pool", 4), signal("pv_pool", 4)
        exp1_ready = signal("exp1_ready", 4)
        oL_ready, o_written = signal("oL_ready", 4), signal("o_written", 4, 16)
        oS_in = [signal(f"oS_in{p}", 2, 16) for p in range(2)]
        cq_ready = signal("cq_ready", 4)
        exp2_ready = signal("exp2_ready", 4)
        route2_ready = signal("route2_ready", 1)
        y2_high, y2_split = signal("y2_high", 4), signal("y2_split", 4)
        x_done = signal("x_done", 4)
        stored = signal("stored", 4, 16)
        dve_step, pads = new_semaphore(nc, w, "early_dve_step"), new_semaphore(nc, w, "early_pads")
        pool_step, ahead_step = new_semaphore(nc, w, "early_pool_step"), new_semaphore(nc, w, "early_ahead_step")

        def times_q(j, half):
            q = qL[:, j % 2, :, half * (TP // 2):(half + 1) * (TP // 2)]
            return q.unsqueeze(3).to_broadcast([P, CH, TP // 2, WIN])

        def windows(t, j, half):
            a = t[:, j % 2, :, half * (TP // 2):half * (TP // 2) + WIN]
            return bass.AP(a.tensor, a.offset, [list(a.ap[0]), [HALO, CH], [1, TP // 2], [1, WIN]])

        def weights(half):
            e = ee[:, half * (TP // 2):(half + 1) * (TP // 2), :]
            return e.unsqueeze(1).to_broadcast([P, CH, TP // 2, WIN])

        block = ctx.enter_context(nc.Block())

        @block.sync
        def _(sp):
            apart = Apart(sp, pads, 4)
            def load_x(j, tile):
                x_loaded[j].send(sp.dma_start(xin[:, j, :], io["x"][bass.ts(tile, P), :]))

            def load_ctx(j, tile):
                ctx_loaded[j].send(sp.dma_start(ctxt[:, j, :], io["ctx"][bass.ts(tile, P), :]))

            def load_cT(j, tile):
                src = io["ctxT"].rearrange("(c p) n -> p c n", p=P)
                cT_loaded[j].send(sp.dma_start(cT[:, j, :, :], src[:, :, bass.ts(tile, P)]))

            def attention1(turn):
                out_by_channel(turn, 0)
                qk_by_time(turn, 0)
                v_by_time(turn, 0)
                out_by_channel(turn, 1)
                qk_by_time(turn, 1)
                v_by_time(turn, 1)
                out_by_channel(turn, 2)
                for j in range(QUAD):
                    if j + 2 < QUAD:
                        qk_dve.wait(apart, turn, j)
                        qk_pool.wait(sp, turn, j)
                        qk_by_time(turn, j + 2)
                    oL_ready.wait(apart, turn, j)
                    if j + 2 < QUAD:
                        v_by_time(turn, j + 2)
                    back(turn, j)
                    if j + 3 < QUAD:
                        out_by_channel(turn, j + 3)

            def store(turn):
                for j in range(QUAD):
                    x_done.wait(apart, turn, j)
                    stored.send(sp.dma_start(io["x_mid"][bass.ts(turn * QUAD + j, P), :], xq[:, j, :]))

            def out_by_channel(turn, j):
                banks.wait_drained(apart, turn, "q1", j)
                banks.wait_drained(sp, turn, "k1", j)
                banks.wait_drained(sp, turn, "v1", j)
                for scr, src, step in ((scr_q, qs, TP), (scr_k, kp, HALO), (scr_v, vp, HALO)):
                    s = src[:, j % 2, :]
                    windows = bass.AP(s.tensor, s.offset, [[s.ap[0][0], P], [TP, TC], [1, step]])
                    sp.dma_start(scr[j].rearrange("c p t -> p c t"), windows)\
                      .then_inc(v_written.sem if src is vp else qk_written.sem, 16)

            def by_time(scr, dst, j):
                return sp.dma_start(dst[:, j % 2, :, :].rearrange("p d t -> p (d t)"),
                                    scr[j].rearrange("c (g d) t -> (c g) (d t)", d=CH))

            def qk_by_time(turn, j):
                qk_written.wait(apart, turn, j)
                by_time(scr_q, qL, j).then_inc(qk_in[j % 2].sem, 16)
                by_time(scr_k, kL, j).then_inc(qk_in[j % 2].sem, 16)

            def v_by_time(turn, j):
                v_written.wait(apart, turn, j)
                v_in[j % 2].send(by_time(scr_v, vL, j))

            def back(turn, j):
                o_written.send(sp.dma_start(scr_o[j], oL[:, j % 2, :, :].rearrange("p d t -> p (d t)")))
                o_written.wait(sp, turn, j)
                if j >= 2:
                    banks.wait_filled(sp, turn, "out1", j - 2)
                oS_in[j % 2].send(sp.dma_start(
                    oS[:, j % 2, :].rearrange("p (c t) -> p c t", c=TC),
                    scr_o[j].rearrange("(c g) (d t) -> (g d) c t", c=TC, d=CH)))

            sp.wait_ge(pads, 4)
            for j in range(QUAD):
                load_x(j, j)
                load_cT(j, j)
                load_ctx(j, j)
            with sp.Fori(0, TURNS - 1) as turn:
                attention1(turn)
                banks.wait_filled(apart, turn, "out1", QUAD - 1)
                for j in range(QUAD):
                    load_x(j, turn * QUAD + (QUAD + j))
                    load_cT(j, turn * QUAD + (QUAD + j))
                    load_ctx(j, turn * QUAD + (QUAD + j))
                store(turn)
            attention1(TURNS - 1)
            store(TURNS - 1)
            sp.wait_ge(stored.sem, TURNS * QUAD * 16 + 1)

        @block.tensor
        def _(pe):
            apart = Apart(pe, pads, 4)
            ident = w["ident"][:, :]

            def chunks(t, j):
                return [t[:, j, c, :] for c in range(C)]

            def turn_tile(turn, layer, j, src=None):
                xn_ready.wait(pe, turn, 4 * layer + j)
                banks.wait_free(pe, turn, "turn", layer, j)
                out = banks.bank("turn", layer, j)
                for c in range(C):
                    last = pe.transpose(out[:, c * P:(c + 1) * P], xn[:, j, c * P:(c + 1) * P], ident)
                banks.fill(last, "turn", layer, j)

            def lora_ffn(turn, f, layer):
                nr, wname, rname, bname = ((R0, "W0", "R0", "B0"), (R1, "W1", "R1", "B1"))[f]
                for j in range(QUAD):
                    turn_tile(turn, layer, j)
                for j in range(QUAD):
                    banks.wait_drained(pe, turn, "turn", layer, j)
                    banks.wait_free(pe, turn, "route", f, j)
                    n = nr + LORA
                    last = three(pe, banks.bank("route", f, j)[:, 0:n], chunks(xTh, j), chunks(xTl, j),
                                 [w[rname + "h"][:, c, :] for c in range(C)],
                                 [w[rname + "l"][:, c, :] for c in range(C)])
                    banks.fill(last, "route", f, j)
                def base(j):
                    banks.wait_free(pe, turn, "base", f, j)
                    three(pe, banks.bank("base", f, j), chunks(xTh, j), chunks(xTl, j),
                          [w[wname + "h"][:, c, :] for c in range(C)],
                          [w[wname + "l"][:, c, :] for c in range(C)], last=False)

                def turn_hs(j):
                    hs_ready.wait(pe, turn, 4 * f + j)
                    banks.wait_free(pe, turn, "hturn", f, j)
                    banks.fill(pe.transpose(banks.bank("hturn", f, j)[:, 0:P], hs[:, j, :], ident), "hturn", f, j)

                def add_experts(j):
                    banks.wait_drained(pe, turn, "hturn", f, j)
                    banks.fill(pe.matmul(banks.bank("base", f, j), hsT[:, j, :], w[bname][:, :],
                                         start=False, stop=True), "base", f, j)
                base(0)
                base(1)
                turn_hs(0)
                turn_hs(1)
                base(2)
                add_experts(0)
                turn_hs(2)
                add_experts(1)
                turn_hs(3)
                base(3)
                add_experts(2)
                add_experts(3)

            def ahead(turn):
                for j in range(QUAD):
                    turn_tile(turn, 0, j)

            def attention0(turn):
                for j in range(QUAD):
                    banks.wait_drained(pe, turn, "turn", 0, j)
                    banks.wait_free(pe, turn, "proj0", j)
                    out = banks.bank("proj0", j)
                    for m in range(C):
                        last = three(pe, out[:, m * P:(m + 1) * P],
                                     [w["Mh"][:, c, m * P:(m + 1) * P] for c in range(C)],
                                     [w["Ml"][:, c, m * P:(m + 1) * P] for c in range(C)],
                                     chunks(xTh, j), chunks(xTl, j))
                    banks.fill(last, "proj0", j)
                for j in range(QUAD):
                    aT_split.wait(pe, turn, j)
                    cT_split.wait(pe, turn, j)
                    banks.wait_free(pe, turn, "score0", j)
                    out = banks.bank("score0", j)
                    three(pe, out[:, P:P + 1], chunks(xTh, j), chunks(xTl, j),
                          [w["ch"][:, c:c + 1] for c in range(C)], [w["cl"][:, c:c + 1] for c in range(C)])
                    last = three(pe, out[:, 0:P], chunks(aTh, j), chunks(aTl, j), chunks(cTh, j), chunks(cTl, j))
                    banks.fill(last, "score0", j)
                for j in range(QUAD):
                    pr0_ready.wait(pe, turn, j)
                    banks.wait_free(pe, turn, "prob0", j)
                    banks.fill(pe.transpose(banks.bank("prob0", j)[:, 0:P], pr[:, j, :], ident), "prob0", j)
                    banks.wait_drained(pe, turn, "prob0", j)
                    ctx_loaded[j].wait(pe, turn, 0)
                    banks.wait_free(pe, turn, "out0", j)
                    banks.fill(pe.matmul(banks.bank("out0", j), prT[:, j, :], ctxt[:, j, :], start=True, stop=True),
                               "out0", j)

            def attention1(turn):
                for j in range(QUAD):
                    for k, (step, src) in enumerate((("q1", xn), ("k1", ctxt), ("v1", ctxt))):
                        if k == 0:
                            xn_ready.wait(pe, turn, 8 + j)
                        banks.wait_free(pe, turn, step, j)
                        banks.fill(pe.matmul(banks.bank(step, j), w["L1W"][:, k, :], src[:, j, :],
                                             start=True, stop=True), step, j)
                dots1(turn, 0)
                for j in range(QUAD):
                    if j + 1 < QUAD:
                        dots1(turn, j + 1)
                    if j >= 1:
                        out_proj1(turn, j - 1)
                out_proj1(turn, QUAD - 1)

            def dots1(turn, j):
                for h in range(2):
                    (qk_dve, qk_pool)[h].wait(pe, turn, j)
                    banks.wait_free(pe, turn, "dot1", j, h)
                    out = banks.bank("dot1", j, h)
                    for d in range(CH):
                        last = pe.matmul(out, ident, qk[h][:, d, :, :].rearrange("p t w -> p (t w)"),
                                         start=(d == 0), stop=(d == CH - 1))
                    banks.fill(last, "dot1", j, h)

            def out_proj1(turn, j):
                oS_in[j % 2].wait(pe, turn, j // 2)
                banks.wait_free(pe, turn, "out1", j)
                banks.fill(pe.matmul(banks.bank("out1", j), w["L1W"][:, 3, :], oS[:, j % 2, :],
                                     start=True, stop=True), "out1", j)

            def attention2(turn):
                for j in range(QUAD):
                    turn_tile(turn, 4, j)

                def low(j):
                    if j == 0:
                        for jj in range(QUAD):
                            banks.wait_drained(pe, turn, "turn", 4, jj)
                    banks.wait_free(pe, turn, "low2", j)
                    out = banks.bank("low2", j)
                    three(pe, out[0:64, 0:P], [w["Wqdh"][:, c, :] for c in range(C)],
                          [w["Wqdl"][:, c, :] for c in range(C)], chunks(xTh, j), chunks(xTl, j))
                    last = three(pe, out[:, P:2 * P], [w["Wkvh"][:, c, :] for c in range(C)],
                                 [w["Wkvl"][:, c, :] for c in range(C)], chunks(cTh, j), chunks(cTl, j))
                    banks.fill(last, "low2", j)

                def up(j):
                    s = j % 2
                    cq_ready.wait(pe, turn, j)
                    banks.wait_free(pe, turn, "qup2", j)
                    for m in range(4):
                        last = pe.matmul(banks.bank("qup2", j)[:, m * P:(m + 1) * P],
                                         w["Wqk"][:, m * P:(m + 1) * P], cqT[:, s, :], start=True, stop=True)
                    banks.fill(last, "qup2", j)
                    banks.wait_drained(pe, turn, "low2", j)
                    banks.wait_free(pe, turn, "vup2", j)
                    for half in range(2):
                        for b in range(2):
                            last = pe.matmul(banks.bank("vup2", j)[SEQ * half:SEQ * half + SEQ, b * 256:(b + 1) * 256],
                                             ckv[0:32, s, b, 0, :], w["Wvu"][:, half * 256:(half + 1) * 256],
                                             start=True, stop=True)
                    banks.fill(last, "vup2", j)

                def scores(j):
                    s = j % 2
                    banks.wait_drained(pe, turn, "qup2", j)
                    for half in range(2):
                        banks.wait_free(pe, turn, "score2", j, half)
                        for mm in range(2):
                            for b in range(2):
                                last = pe.matmul(
                                    banks.bank("score2", j, half)[SEQ * b:SEQ * b + SEQ, mm * 256:(mm + 1) * 256],
                                    qT2[:, s, 2 * half + mm, SEQ * b:SEQ * b + SEQ],
                                    ckv[:, s, b, :, :].rearrange("p i k -> p (i k)"), start=True, stop=True)
                        banks.fill(last, "score2", j, half)

                def turn_weights(j):
                    s = j % 2
                    exp2_ready.wait(pe, turn, j)
                    for half in range(2):
                        banks.wait_free(pe, turn, "prob2", j, half)
                        for n in range(4):
                            hp = 4 * half + n
                            src = s2[:, s, 2 * hp:2 * hp + 2, :].rearrange("p h k -> p (h k)")
                            last = pe.transpose(banks.bank("prob2", j, half)[:, n * P:(n + 1) * P], src, ident)
                        banks.fill(last, "prob2", j, half)

                def attend(j):
                    s = j % 2
                    banks.wait_drained(pe, turn, "vup2", j)
                    banks.wait_drained(pe, turn, "prob2", j, 0)
                    banks.wait_drained(pe, turn, "prob2", j, 1)
                    for half in range(2):
                        banks.wait_free(apart, turn, "out2", j, half)
                        rows = slice(SEQ * half, SEQ * half + SEQ)
                        for b in range(2):
                            for hp in range(H2 // 2):
                                last = pe.matmul(
                                    banks.bank("out2", j, half)[SEQ * b:SEQ * b + SEQ, hp * 32:(hp + 1) * 32],
                                    p2T[rows, s, hp, SEQ * b:SEQ * b + SEQ],
                                    v2[rows, s, b, hp * 32:(hp + 1) * 32], start=True, stop=True)
                        banks.fill(last, "out2", j, half)

                for j in range(QUAD + 1):
                    if j < QUAD:
                        low(j)
                    if j >= 1:
                        turn_weights(j - 1)
                    if j < QUAD:
                        up(j)
                    if j >= 1:
                        attend(j - 1)
                    if j < QUAD:
                        scores(j)

            def ffn2(turn, more):
                for j in range(QUAD):
                    turn_tile(turn, 5, j)
                for j in range(QUAD):
                    banks.wait_drained(pe, turn, "turn", 5, j)
                    banks.wait_free(pe, turn, "gate2", j)
                    for c in range(C):
                        last = pe.matmul(banks.bank("gate2", j)[:, 0:E01], xTf[:, j, c, :], w["gate2"][:, c, :],
                                         start=(c == 0), stop=(c == C - 1))
                    banks.fill(last, "gate2", j)
                for j in range(QUAD):
                    route2_ready.wait(pe, turn, 0)
                    banks.wait_free(pe, turn, "gturn", j)
                    banks.fill(pe.transpose(banks.bank("gturn", j)[0:E01, 0:P], comb[:, j, :], ident), "gturn", j)
                for j in range(QUAD):
                    banks.wait_drained(pe, turn, "gturn", j)
                    banks.wait_free(pe, turn, "scale_in", j)
                    for c in range(C):
                        last = pe.matmul(banks.bank("scale_in", j)[:, c * P:(c + 1) * P],
                                         w["ics"][:, c * P:(c + 1) * P], rT2[:, j, :], start=True, stop=True)
                    banks.fill(last, "scale_in", j)
                    banks.wait_free(pe, turn, "scale_out", j)
                    banks.fill(pe.matmul(banks.bank("scale_out", j), rT2[:, j, :], w["ocs"][:, :],
                                         start=True, stop=True), "scale_out", j)
                if more:
                    ahead(turn + 1)
                for j in range(QUAD):
                    y2_split.wait(pe, turn, j)
                    banks.wait_free(pe, turn, "sign2", j)
                    for c in range(C):
                        pe.matmul(banks.bank("sign2", j), xTh[:, j, c, :], w["sign2"][:, c, :],
                                  start=(c == 0), stop=False)
                        last = pe.matmul(banks.bank("sign2", j), xTl[:, j, c, :], w["sign2"][:, c, :],
                                         start=False, stop=(c == C - 1))
                    banks.fill(last, "sign2", j)

            def body(turn, more):
                attention0(turn)
                lora_ffn(turn, 0, 1)
                attention1(turn)
                lora_ffn(turn, 1, 3)
                attention2(turn)
                ffn2(turn, more)

            ahead(0)
            with pe.Fori(0, TURNS - 1) as turn:
                body(turn, True)
            body(TURNS - 1, False)

        @block.scalar
        def _(act):
            def high_of(turn, layer, n, j):
                banks.wait_filled(act, turn, "turn", layer, j)
                xT_high.send(act.activation(xTh[:, j, :, :].rearrange("p c n -> p (c n)"),
                                            banks.bank("turn", layer, j), ACT.Copy))

            def high(turn, layer, n):
                for j in range(QUAD):
                    high_of(turn, layer, n, j)

            def route_exp(turn, f, e, nr):
                step, n = (("route", 0), nr + LORA) if f == 0 else (("route", 1), nr + LORA) if f == 1 else (("gate2",), nr)
                for j in range(QUAD):
                    banks.wait_filled(act, turn, *step, j)
                    banks.drain(act.activation(rh[:, j, 0:n], banks.bank(*step, j)[:, 0:n], ACT.Copy), *step, j)
                for j in range(QUAD):
                    logit_ready.wait(act, turn, 4 * f + j)
                    expo_ready.send(act.activation(e[:, j, 0:nr], rh[:, j, 0:nr], ACT.Exp,
                                                   bias=nmax[:, j:j + 1], accum_out=tot[:, j:j + 1]))

            def hsT_copy(turn, f):
                for j in range(QUAD):
                    banks.wait_filled(act, turn, "hturn", f, j)
                    banks.drain(act.activation(hsT[:, j, :], banks.bank("hturn", f, j)[:, 0:P], ACT.Copy),
                                "hturn", f, j)

            def y1_copy(turn, j):
                banks.wait_filled(act, turn, "out1", j)
                banks.drain(act.activation(y1[:, j, :], banks.bank("out1", j), ACT.Identity,
                                           bias=w["L1b"][:, 3:4]), "out1", j)

            def low2_copy(turn, j):
                s = j % 2
                banks.wait_filled(act, turn, "low2", j)
                cq_ready.send(act.activation(cqT[:, s, :], banks.bank("low2", j)[0:64, 0:P], ACT.Copy))

            def attention2_before(turn, j):
                s = j % 2
                banks.wait_filled(act, turn, "qup2", j)
                banks.drain(act.activation(qT2[:, s, :, :].rearrange("p m n -> p (m n)"), banks.bank("qup2", j),
                                           ACT.Copy), "qup2", j)
                banks.wait_filled(act, turn, "vup2", j)
                banks.drain(act.activation(v2[:, s, :, :].rearrange("p b n -> p (b n)"), banks.bank("vup2", j),
                                           ACT.Copy), "vup2", j)
                banks.wait_drained(act, turn, "score2", j, 0)
                banks.wait_drained(act, turn, "score2", j, 1)
                flat = s2[:, s, :, :].rearrange("p h k -> p (h k)")
                exp2_ready.send(act.activation(flat, flat, ACT.Exp, scale=float(L2K) ** -0.5))

            def attention2_after(turn, j):
                for half in range(2):
                    banks.wait_filled(act, turn, "prob2", j, half)
                    banks.drain(act.activation(p2T[:, j % 2, 4 * half:4 * half + 4, :].rearrange("p h n -> p (h n)"),
                                               banks.bank("prob2", j, half), ACT.Copy), "prob2", j, half)

            def ahead(turn, before):
                for j in range(QUAD):
                    cT_loaded[j].wait(act, turn, 0)
                    cT_high.send(act.activation(cTh[:, j, :, :], cT[:, j, :, :], ACT.Copy))
                for j in range(QUAD):
                    if before is not None:
                        banks.wait_filled(act, before, "sign2", j)
                    high_of(turn, 0, 0, j)

            def body(turn, more):
                for j in range(QUAD):
                    banks.wait_drained(act, turn, "proj0", j)
                    aT_high.send(act.activation(aTh[:, j, :, :], aT[:, j % 2, :, :], ACT.Copy))
                for j in range(QUAD):
                    sm0_ready.wait(act, turn, j)
                    pr0_ready.send(act.activation(pr[:, j, :], sm[:, j, :], ACT.Exp, bias=nmax[:, j:j + 1],
                                                  scale=float(D) ** -0.5, accum_out=tot[:, j:j + 1]))
                for j in range(QUAD):
                    banks.wait_filled(act, turn, "prob0", j)
                    banks.drain(act.activation(prT[:, j, :], banks.bank("prob0", j)[:, 0:P], ACT.Copy), "prob0", j)
                high(turn, 1, 1)
                route_exp(turn, 0, e0, R0)
                hsT_copy(turn, 0)
                for j in range(QUAD):
                    if j >= 2:
                        qk_written.wait(act, turn, j - 2)
                        v_written.wait(act, turn, j - 2)
                    for k, (step, dst, lo) in enumerate((("q1", qs, 0), ("k1", kp, 8), ("v1", vp, 8))):
                        banks.wait_filled(act, turn, step, j)
                        banks.drain(act.activation(dst[:, j % 2, lo:lo + D], banks.bank(step, j), ACT.Identity,
                                                   bias=w["L1b"][:, k:k + 1]), step, j)
                for j in range(QUAD):
                    banks.wait_drained(act, turn, "dot1", j, 0)
                    banks.wait_drained(act, turn, "dot1", j, 1)
                    exp1_ready.send(act.activation(ee[:, :, :], ee[:, :, :], ACT.Exp, scale=float(CH) ** -0.5))
                    if j >= 1:
                        y1_copy(turn, j - 1)
                y1_copy(turn, QUAD - 1)
                high(turn, 3, 2)
                route_exp(turn, 1, e1, R1)
                hsT_copy(turn, 1)
                high(turn, 4, 3)
                for j in range(QUAD + 1):
                    if j < QUAD:
                        low2_copy(turn, j)
                    if j >= 1:
                        attention2_after(turn, j - 1)
                    if j < QUAD:
                        attention2_before(turn, j)
                for j in range(QUAD):
                    banks.wait_filled(act, turn, "turn", 5, j)
                    banks.drain(act.activation(xTf[:, j, :, :].rearrange("p c n -> p (c n)"),
                                               banks.bank("turn", 5, j), ACT.Copy), "turn", 5, j)
                route_exp(turn, 2, e2, E01)
                for j in range(QUAD):
                    banks.wait_filled(act, turn, "gturn", j)
                    banks.drain(act.activation(rT2[:, j, :], banks.bank("gturn", j)[0:E01, 0:P], ACT.Copy),
                                "gturn", j)
                for j in range(QUAD):
                    banks.wait_filled(act, turn, "scale_out", j)
                    banks.drain(act.activation(osb[:, j, :], banks.bank("scale_out", j), ACT.Copy,
                                               scale=w["gates"][:, 6:7]), "scale_out", j)
                    banks.wait_drained(act, turn, "scale_in", j)
                    y2_high.send(act.activation(xTh[:, j, :, :], xTf[:, j, :, :], ACT.Copy))
                if more:
                    ahead(turn + 1, turn)

            act.wait_ge(pads, 4)
            ahead(0, None)
            with act.Fori(0, TURNS - 1) as turn:
                body(turn, True)
            body(TURNS - 1, False)

        @block.gpsimd
        def _(pool):
            banks.open(pool)
            pool.sem_inc(stored.sem, 1)
            def rstd_of(turn, layer):
                for j in range(QUAD):
                    stats_ready.wait(pool, turn, 4 * layer + j)
                    pool.tensor_tensor(vare[:, j:j + 1], mv[:, j, 1:2], w["eps"][:, :], ALU.add)\
                        .then_inc(pool_step, 1)
                    pool.wait_ge(pool_step, turn * 24 + (4 * layer + j + 1))
                    rstd_ready.send(pool.tensor_tensor(rstd[:, j:j + 1], vare[:, j:j + 1], w["power"][:, 0:1],
                                                       ALU.pow))

            def add_bias(turn, f, layer):
                for j in range(QUAD):
                    xn_ready.wait(pool, turn, 4 * layer + j)
                    xbias_ready.send(pool.tensor_tensor(xq[:, j, :], xq[:, j, :], w["gbias"][:, f, :], ALU.add))

            for t in (kp, vp):
                pool.memset(t[:, :, :], 0.0).then_inc(pads, 1)
            pool.memset(e0[:, :, :], NEVER).then_inc(pads, 1)
            pool.memset(pick0[:, :, :], NEVER).then_inc(pads, 1)
            def ahead(turn):
                for j in range(QUAD):
                    cT_high.wait(pool, turn, j)
                    cT_split.send(pool.tensor_tensor(cTl[:, j, :, :], cT[:, j, :, :], cTh[:, j, :, :], ALU.subtract))

            def body(turn, more):
                for j in range(QUAD):
                    aT_high.wait(pool, turn, j)
                    aT_split.send(pool.tensor_tensor(aTl[:, j, :, :], aT[:, j % 2, :, :], aTh[:, j, :, :],
                                                     ALU.subtract))
                rstd_of(turn, 1)
                add_bias(turn, 0, 1)
                rstd_of(turn, 2)
                def times_k(j):
                    qk_in[j % 2].wait(pool, turn, j // 2)
                    if j >= 1:
                        banks.wait_filled(pool, turn, "dot1", j - 1, 1)
                    qk_pool.send(pool.tensor_tensor(qk[1][:, :, :, :], times_q(j, 1), windows(kL, j, 1), ALU.mult))
                times_k(0)
                for j in range(QUAD):
                    if j + 1 < QUAD:
                        times_k(j + 1)
                    exp1_ready.wait(pool, turn, j)
                    if j >= 1:
                        oL_ready.wait(pool, turn, j - 1)
                    v_in[j % 2].wait(pool, turn, j // 2)
                    pv_pool.send(pool.tensor_tensor(pv[1][:, :, :, :], weights(1), windows(vL, j, 1), ALU.mult))
                rstd_of(turn, 3)
                add_bias(turn, 1, 3)
                rstd_of(turn, 4)
                rstd_of(turn, 5)
                if more:
                    rstd_of(turn + 1, 0)
                add_bias(turn, 2, 5)
                for j in range(QUAD):
                    y2_high.wait(pool, turn, j)
                    y2_split.send(pool.tensor_tensor(xTl[:, j, :, :], xTf[:, j, :, :], xTh[:, j, :, :], ALU.subtract))
                if more:
                    ahead(turn + 1)

            rstd_of(0, 0)
            ahead(0)
            with pool.Fori(0, TURNS - 1) as turn:
                body(turn, True)
            body(TURNS - 1, False)

        @block.vector
        def _(dve):
            apart = Apart(dve, pads, 4)
            def body(turn, more, part="all"):
                st = Steps(dve, dve_step, DVE_STEPS, turn)

                def low(layer, n, j):
                    xT_high.wait(dve, turn, 4 * n + j)
                    banks.drain(dve.tensor_tensor(xTl[:, j, :, :].rearrange("p c n -> p (c n)"),
                                                  banks.bank("turn", layer, j),
                                                  xTh[:, j, :, :].rearrange("p c n -> p (c n)"), ALU.subtract),
                                "turn", layer, j)

                def statistics(x, j):
                    n = st.step(dve.bn_stats(stats[:, j, :], x[:, j, :]))
                    st.after(n, apart)
                    stats_ready.send(dve.bn_aggr(mv[:, j, :], stats[:, j, :]))

                def apply(layer, x, j):
                    rstd_ready.wait(dve, turn, 4 * layer + j)
                    xn_ready.send(dve.tensor_scalar(xn[:, j, :], x[:, j, :], mv[:, j, 0:1], rstd[:, j:j + 1],
                                                    ALU.subtract, ALU.mult))

                def normalise(layer, x, x_stands, update=None, halves=None):
                    for j in range(QUAD + 1):
                        if j < QUAD:
                            if update:
                                update(j)
                            x_stands(j)
                            statistics(x, j)
                        if j >= 1:
                            apply(layer, x, j - 1)
                    if halves is not None:
                        for j in range(QUAD):
                            low(layer, halves, j)

                def logits(f, step, nr, add=None):
                    for j in range(QUAD):
                        banks.wait_drained(dve, turn, *step, j)
                        if add is not None:
                            st.link(dve.tensor_tensor(rh[:, j, 0:nr], rh[:, j, 0:nr], add, ALU.add))
                        logit_ready.send(dve.tensor_reduce(nmax[:, j:j + 1], rh[:, j, 0:nr], AX.X, ALU.max,
                                                           negate=True))

                def expo(f, j, eng=dve):
                    expo_ready.wait(eng, turn, 4 * f + j)

                def lora(f, nr):
                    for j in range(QUAD):
                        hs_ready.send(dve.tensor_tensor(
                            hs[:, j, :].rearrange("p (e r) -> p e r", r=RANK),
                            rh[:, j, nr:nr + LORA].rearrange("p (e r) -> p e r", r=RANK),
                            comb[:, j, :].unsqueeze(2).to_broadcast([P, E01, RANK]), ALU.mult))

                def add_ffn(f, j):
                    banks.wait_filled(dve, turn, "base", f, j)
                    xbias_ready.wait(dve, turn, 4 * f + j)
                    banks.drain(dve.scalar_tensor_tensor(
                        out=xq[:, j, :], in0=banks.bank("base", f, j), scalar=w["gates"][:, 4 + f:5 + f],
                        in1=xq[:, j, :], op0=ALU.mult, op1=ALU.add), "base", f, j)

                if part == "statistics":
                    own = Steps(dve, ahead_step, QUAD, turn)
                    for j in range(QUAD):
                        x_loaded[j].wait(dve, turn, 0)
                        n = own.step(dve.bn_stats(stats[:, j, :], xin[:, j, :]))
                        own.after(n, apart)
                        stats_ready.send(dve.bn_aggr(mv[:, j, :], stats[:, j, :]))
                    return
                if part == "normalised":
                    for j in range(QUAD):
                        apply(0, xin, j)
                    return
                if part == "lows":
                    for j in range(QUAD):
                        low(0, 0, j)
                    return

                for j in range(QUAD):
                    banks.wait_filled(dve, turn, "proj0", j)
                    if j >= 2:
                        aT_split.wait(dve, turn, j - 2)
                    banks.drain(dve.tensor_tensor(aT[:, j % 2, :, :],
                                                  banks.bank("proj0", j).rearrange("p (c n) -> p c n", c=C),
                                                  w["r"][:, :].unsqueeze(2).to_broadcast([P, C, P]), ALU.add),
                                "proj0", j)

                def row_term(j):
                    banks.wait_filled(dve, turn, "score0", j)
                    return dve.tensor_tensor(u[:, j:j + 1], banks.bank("score0", j)[:, P:P + 1], w["s"][:, :], ALU.add)
                for j in range(QUAD):
                    st.link(row_term(j))
                    banks.drain(dve.scalar_tensor_tensor(
                        out=sm[:, j, :], in0=banks.bank("score0", j)[:, 0:P], scalar=u[:, j:j + 1],
                        in1=w["bdmask"][:, :], op0=ALU.add, op1=ALU.add), "score0", j)
                    banks.wait_drained(dve, turn, "score0", j)
                    st.link(dve.tensor_reduce(nmax[:, j:j + 1], sm[:, j, :], AX.X, ALU.max, negate=True))
                    sm0_ready.send(dve.tensor_scalar(nmax[:, j:j + 1], nmax[:, j:j + 1], float(D) ** -0.5, None,
                                                     ALU.mult))

                pr0_ready.wait(dve, turn, QUAD - 1)
                st.link(dve.reciprocal(rec[:, :], tot[:, :]))
                n = st.step(dve.tensor_scalar(rec[:, :], rec[:, :], w["gates"][:, 0:1], None, ALU.mult))

                def add0(j):
                    st.after(n)
                    banks.wait_filled(dve, turn, "out0", j)
                    dve.wait_ge(stored.sem, turn * (QUAD * 16) + 1)
                    banks.drain(dve.scalar_tensor_tensor(
                        out=xq[:, j, :], in0=banks.bank("out0", j), scalar=rec[:, j:j + 1], in1=xin[:, j, :],
                        op0=ALU.mult, op1=ALU.add), "out0", j)

                normalise(1, xq, lambda j: banks.wait_drained(dve, turn, "out0", j), add0, halves=1)
                logits(0, ("route", 0), R0)

                def top(e, f):
                    for j in range(QUAD):
                        expo(f, j, apart)
                        n = st.step(dve.max(top8[:, j, :], e[:, j, 0:(R0, R1)[f]]))
                    return n

                def scaled(src):
                    st.link(dve.scalar_tensor_tensor(
                        out=comb[:, :, :], in0=src, scalar=2.0,
                        in1=rec[:, :].unsqueeze(2).to_broadcast([P, QUAD, E01]), op0=ALU.mult, op1=ALU.mult))
                st.after(top(e0, 0))
                n = st.step(dve.tensor_copy(pick0[:, :, 0:2], top8[:, :, 0:2]))
                summed = st.step(dve.tensor_tensor(tot[:, :], top8[:, :, 0], top8[:, :, 1], ALU.add))
                st.after(n, apart)
                for j in range(QUAD):
                    n = st.step(dve.match_replace(rkeep[:, j, 0:14], pick0[:, j, :], e0[:, j, :], 0.0))
                st.after(summed)
                st.step(dve.reciprocal(rec[:, :], tot[:, :]))
                st.after(n)
                st.link(dve.tensor_tensor(rsel[:, :, 0:R0], e0[:, :, 0:R0], rkeep[:, :, 0:R0], ALU.subtract))
                scaled(rsel[:, :, 0:R0])
                lora(0, R0)

                normalise(2, xq, lambda j: banks.wait_drained(dve, turn, "base", 0, j), lambda j: add_ffn(0, j))
                def times_k(j):
                    qk_in[j % 2].wait(dve, turn, j // 2)
                    if j >= 1:
                        banks.wait_filled(dve, turn, "dot1", j - 1, 0)
                    qk_dve.send(dve.tensor_tensor(qk[0][:, :, :, :], times_q(j, 0), windows(kL, j, 0), ALU.mult))
                times_k(0)
                for j in range(QUAD):
                    for h in range(2):
                        banks.wait_filled(dve, turn, "dot1", j, h)
                        at = slice(h * (TP // 2), (h + 1) * (TP // 2))
                        dots = banks.bank("dot1", j, h).rearrange("p (t w) -> p t w", w=WIN)
                        st.link(dve.tensor_reduce(mx1[:, at], dots, AX.X, ALU.max))
                        ins = dve.tensor_tensor(ee[:, at, :], dots,
                                                mx1[:, at].unsqueeze(2).to_broadcast([P, TP // 2, WIN]), ALU.subtract)
                        banks.drain(ins, "dot1", j, h)
                    if j + 1 < QUAD:
                        times_k(j + 1)
                    exp1_ready.wait(dve, turn, j)
                    v_in[j % 2].wait(dve, turn, j // 2)
                    st.step(dve.tensor_tensor(pv[0][:, :, :, :], weights(0), windows(vL, j, 0), ALU.mult))
                    st.link(dve.tensor_reduce(sum1[:, :], ee[:, :, :], AX.X, ALU.add))
                    st.link(dve.reciprocal(rec1[:, :], sum1[:, :]))
                    if j >= 2:
                        o_written.wait(dve, turn, j - 2)
                    st.link(dve.tensor_reduce(oL[:, j % 2, :, 0:TP // 2], pv[0][:, :, :, :], AX.X, ALU.add))
                    pv_pool.wait(dve, turn, j)
                    st.link(dve.tensor_reduce(oL[:, j % 2, :, TP // 2:TP], pv[1][:, :, :, :], AX.X, ALU.add))
                    oL_ready.send(dve.tensor_tensor(oL[:, j % 2, :, :], oL[:, j % 2, :, :],
                                                    rec1[:, :].unsqueeze(1).to_broadcast([P, CH, TP]), ALU.mult))

                def add1(j):
                    banks.wait_drained(dve, turn, "out1", j)
                    st.link(dve.scalar_tensor_tensor(out=xq[:, j, :], in0=y1[:, j, :], scalar=w["gates"][:, 1:2],
                                                     in1=xq[:, j, :], op0=ALU.mult, op1=ALU.add))

                normalise(3, xq, lambda j: None, add1, halves=2)
                logits(1, ("route", 1), R1, w["rb1"][:, :])
                st.after(top(e1, 1), apart)
                for j in range(QUAD):
                    n = st.step(dve.match_replace(rkeep[:, j, 0:R1], top8[:, j, :], e1[:, j, :], 0.0))
                st.step(dve.reciprocal(rec[:, :], tot[:, :]))
                st.after(n)
                st.link(dve.tensor_tensor(rsel[:, :, 0:R1], e1[:, :, :], rkeep[:, :, 0:R1], ALU.subtract))
                st.link(dve.tensor_tensor(rmix[:, :, :, :],
                                          rsel[:, :, 0:R1].unsqueeze(2).to_broadcast([P, QUAD, E01, R1]),
                                          w["route_to"][:, :, :].unsqueeze(1).to_broadcast([P, QUAD, E01, R1]),
                                          ALU.mult))
                st.link(dve.tensor_reduce(comb[:, :, :], rmix[:, :, :, :], AX.X, ALU.add))
                scaled(comb[:, :, :])
                lora(1, R1)

                normalise(4, xq, lambda j: banks.wait_drained(dve, turn, "base", 1, j), lambda j: add_ffn(1, j),
                          halves=3)

                def spread_keys(j):
                    s = j % 2
                    cq_ready.wait(dve, turn, j)
                    low_keys = banks.bank("low2", j)[:, P:2 * P].rearrange("p (b k) -> p b k", b=2)
                    banks.drain(dve.tensor_tensor(
                        ckv[:, s, :, :, :], low_keys.unsqueeze(2).to_broadcast([P, 2, 4, SEQ]),
                        w["quarter"][:, :].unsqueeze(1).unsqueeze(3).to_broadcast([P, 2, 4, SEQ]), ALU.mult), "low2", j)

                def attention2_before(j):
                    s = j % 2
                    for half in range(2):
                        heads = slice(8 * half, 8 * half + 8)
                        banks.wait_filled(dve, turn, "score2", j, half)
                        scores = banks.bank("score2", j, half).rearrange("p (h k) -> p h k", k=SEQ)
                        st.link(dve.tensor_reduce(mx2[:, s, heads], scores, AX.X, ALU.max))
                        banks.drain(dve.tensor_tensor(s2[:, s, heads, :], scores,
                                                      mx2[:, s, heads].unsqueeze(2).to_broadcast([P, 8, SEQ]),
                                                      ALU.subtract), "score2", j, half)

                def attention2_after(j):
                    s = j % 2
                    exp2_ready.wait(dve, turn, j)
                    st.link(dve.tensor_reduce(sum2[:, s, :], s2[:, s, :, :], AX.X, ALU.add))
                    st.link(dve.reciprocal(rec2[:, s, :], sum2[:, s, :]))
                    for half in range(2):
                        banks.wait_filled(dve, turn, "out2", j, half)
                        mine = o2[:, s, :, :].rearrange("p (a b) k -> p a b k", b=2)[:, :, half, :]
                        over = rec2[:, s, :].rearrange("p (a b) -> p a b", b=2)[:, :, half]
                        banks.drain(dve.tensor_tensor(
                            mine, banks.bank("out2", j, half)[:, 0:256].rearrange("p (a k) -> p a k", k=32),
                            over.unsqueeze(2).to_broadcast([P, 8, 32]), ALU.mult), "out2", j, half)
                    banks.wait_drained(dve, turn, "out2", j, 0)
                    banks.wait_drained(dve, turn, "out2", j, 1)
                    return st.step(dve.scalar_tensor_tensor(
                        out=xq[:, j, :], in0=o2[:, s, :, :].rearrange("p h k -> p (h k)"),
                        scalar=w["gates"][:, 2:3], in1=xq[:, j, :], op0=ALU.mult, op1=ALU.add))

                for j in range(QUAD + 1):
                    if j < QUAD:
                        spread_keys(j)
                    if j >= 1:
                        st.after(attention2_after(j - 1))
                        statistics(xq, j - 1)
                    if j < QUAD:
                        attention2_before(j)
                    if j >= 1:
                        apply(5, xq, j - 1)


                if more:
                    body(turn + 1, True, "statistics")
                logits(2, ("gate2",), E01)

                expo(2, QUAD - 1)
                st.link(dve.reciprocal(rec[:, :], tot[:, :]))
                route2_ready.send(dve.tensor_tensor(comb[:, :, :], e2[:, :, :],
                                                    rec[:, :].unsqueeze(2).to_broadcast([P, QUAD, E01]), ALU.mult))
                if more:
                    body(turn + 1, True, "normalised")
                for j in range(QUAD):
                    banks.wait_filled(dve, turn, "scale_in", j)
                    flat = xTf[:, j, :, :].rearrange("p c n -> p (c n)")
                    banks.drain(dve.tensor_tensor(flat, banks.bank("scale_in", j), flat, ALU.mult), "scale_in", j)
                for j in range(QUAD):
                    banks.wait_filled(dve, turn, "sign2", j)
                    banks.drain(dve.tensor_tensor(osb[:, j, :], banks.bank("sign2", j), osb[:, j, :], ALU.mult),
                                "sign2", j)
                if more:
                    body(turn + 1, True, "lows")
                for j in range(QUAD):
                    banks.wait_drained(dve, turn, "sign2", j)
                    xbias_ready.wait(dve, turn, 8 + j)
                    x_done.send(dve.tensor_tensor(xq[:, j, :], xq[:, j, :], osb[:, j, :], ALU.add))
                st.close()

            dve.wait_ge(pads, 4)
            body(0, True, "statistics")
            body(0, True, "normalised")
            body(0, True, "lows")
            with dve.Fori(0, TURNS - 1) as turn:
                body(turn, True)
            body(TURNS - 1, False)


def prepare_last(nc, io, w):
    plan = []
    for j in range(QUAD):
        plan.append((("turn", j), j))
    plan += [(("cos",), 4), (("sin",), 5)]
    with ExitStack() as ctx:
        def sb(name, shape, dt=F32):
            return ctx.enter_context(nc.sbuf_tensor("pl_" + name, shape, dt))

        def signal(name, per_turn, by=1):
            return Signal(nc, w, "pl_" + name, per_turn, by)

        xn, cT = sb("xn", [P, QUAD, D]), sb("cT", [P, C, QUAD * P])
        stats, mv = sb("stats", [P, QUAD, 6]), sb("mv", [P, QUAD, 2])
        vare, rstd = sb("vare", [P, QUAD]), sb("rstd", [P, QUAD])
        mask_raw = sb("mask", [P, TILES, SEQ], I32)
        pos_raw, pos = sb("pos_raw", [P, TOKENS], I32), sb("pos", [P, TOKENS])
        wrap = sb("wrap", [P, TOKENS])
        row = sb("row", [P, C])
        one_hot = sb("one_hot", [P, C, QUAD * P])
        table = sb("table", [P, 2, C, P])
        banks = Banks(nc, ctx, w, "pl", plan)
        x_loaded = new_semaphore(nc, w, "pl_x_loaded")
        pos_loaded, tables_loaded = new_semaphore(nc, w, "pl_pos_loaded"), new_semaphore(nc, w, "pl_tables_loaded")
        mask_loaded, heads_loaded = new_semaphore(nc, w, "pl_mask_loaded"), new_semaphore(nc, w, "pl_heads_loaded")
        row_ready = new_semaphore(nc, w, "pl_row_ready")
        once = new_semaphore(nc, w, "pl_once")
        cT_loaded, cT_high, cT_low = signal("cT_loaded", 1, 16), signal("cT_high", 1), signal("cT_low", 1)
        stats_ready, rstd_ready, xn_ready = signal("stats_ready", 4), signal("rstd_ready", 4), signal("xn_ready", 4)
        xT_high, hot_ready = signal("xT_high", 4), signal("hot_ready", 4)
        dve_step = new_semaphore(nc, w, "pl_dve_step")
        pool_step = new_semaphore(nc, w, "pl_pool_step")
        block = ctx.enter_context(nc.Block())
        PER = QUAD * P

        @block.sync
        def _(sp):
            sp.dma_start(pos_raw[:, :], io["pos"].partition_broadcast(P)).then_inc(pos_loaded, 16)
            sp.dma_start(table[:, 0, :, :], io["cos"].rearrange("(c p) n -> p c n", p=P)).then_inc(tables_loaded, 16)
            sp.dma_start(table[:, 1, :, :], io["sin"].rearrange("(c p) n -> p c n", p=P)).then_inc(tables_loaded, 16)
            sp.dma_start(w["X"][:, :, :], io["x_mid"].rearrange("(t p) n -> p t n", p=P)).then_inc(x_loaded, 16)
            src = io["ctxT"].rearrange("(c p) n -> p c n", p=P)
            cT_loaded.send(sp.dma_start(cT[:, :, :], src[:, :, 0:PER]))
            sp.dma_start(mask_raw[:, :, :], io["mask"].rearrange("(t p) n -> p t n", p=P)).then_inc(mask_loaded, 16)
            with sp.Fori(0, TURNS - 1) as turn:
                cT_low.wait(sp, turn, 0)
                cT_loaded.send(sp.dma_start(cT[:, :, :], src[:, :, bass.ts(turn + 1, PER)]))
            for load in load_qkv(sp, io, w, 0):
                load.then_inc(heads_loaded, 16)
            load_o(sp, io, w, 0).then_inc(heads_loaded, 16)
            sp.wait_ge(heads_loaded, 64)

        @block.gpsimd
        def _(pool):
            banks.open(pool)
            pool.iota(row[:, :], pattern=[[P, C]], base=0, channel_multiplier=1,
                      allow_small_or_imprecise_dtypes=True).then_inc(row_ready, 1)
            with pool.Fori(0, TURNS) as turn:
                for j in range(QUAD):
                    stats_ready.wait(pool, turn, j)
                    pool.tensor_tensor(vare[:, j:j + 1], mv[:, j, 1:2], w["eps"][:, :], ALU.add)\
                        .then_inc(pool_step, 1)
                    pool.wait_ge(pool_step, turn * QUAD + (j + 1))
                    rstd_ready.send(pool.tensor_tensor(rstd[:, j:j + 1], vare[:, j:j + 1], w["power"][:, 0:1],
                                                       ALU.pow))
                cT_high.wait(pool, turn, 0)
                cT_low.send(pool.tensor_tensor(w["cTl"][:, :, bass.ts(turn, PER)], cT[:, :, :],
                                               w["cTh"][:, :, bass.ts(turn, PER)], ALU.subtract))

        @block.tensor
        def _(pe):
            pe.wait_ge(tables_loaded, 32)
            with pe.Fori(0, TURNS) as turn:
                for k, step in enumerate(("cos", "sin")):
                    hot_ready.wait(pe, turn, QUAD - 1)
                    banks.wait_free(pe, turn, step)
                    for c in range(C):
                        last = pe.matmul(banks.bank(step), table[:, k, c, :], one_hot[:, c, :],
                                         start=(c == 0), stop=(c == C - 1))
                    banks.fill(last, step)
                for j in range(QUAD):
                    xn_ready.wait(pe, turn, j)
                    banks.wait_free(pe, turn, "turn", j)
                    for c in range(C):
                        last = pe.transpose(banks.bank("turn", j)[:, c * P:(c + 1) * P],
                                            xn[:, j, c * P:(c + 1) * P], w["ident"][:, :])
                    banks.fill(last, "turn", j)

        @block.scalar
        def _(act):
            with act.Fori(0, TURNS) as turn:
                cT_loaded.wait(act, turn, 0)
                cT_high.send(act.activation(w["cTh"][:, :, bass.ts(turn, PER)], cT[:, :, :], ACT.Copy))
                for k, step in enumerate(("cos", "sin")):
                    banks.wait_filled(act, turn, step)
                    banks.drain(act.activation(w[step][:, bass.ts(turn, PER)], banks.bank(step), ACT.Copy), step)
                for j in range(QUAD):
                    banks.wait_filled(act, turn, "turn", j)
                    xT_high.send(act.activation(w["xTh"][:, :, bass.ts(turn * QUAD + j, P)],
                                                banks.bank("turn", j).rearrange("p (c n) -> p c n", c=C), ACT.Copy))

        @block.vector
        def _(dve):
            apart = Apart(dve, row_ready, 1)
            dve.wait_ge(pos_loaded, 16)
            dve.tensor_copy(pos[:, :], pos_raw[:, :]).then_inc(once, 1)
            dve.wait_ge(once, 1)
            dve.tensor_scalar(wrap[:, :], pos[:, :], 0.0, float(POSITIONS), ALU.is_lt, ALU.mult).then_inc(once, 1)
            dve.wait_ge(once, 2)
            dve.tensor_tensor(pos[:, :], pos[:, :], wrap[:, :], ALU.add).then_inc(once, 1)
            dve.wait_ge(once, 3)
            dve.tensor_scalar(pos[:, :], pos[:, :], 0.0, float(POSITIONS - 1), ALU.max, ALU.min).then_inc(once, 1)
            dve.wait_ge(once, 4)
            dve.wait_ge(row_ready, 1)
            def hot(turn):
                banks.wait_free(dve, turn, "cos")
                banks.wait_free(dve, turn, "sin")
                for c in range(C):
                    hot_ready.send(dve.tensor_scalar(one_hot[:, c, :], pos[:, bass.ts(turn, PER)],
                                                     row[:, c:c + 1], None, ALU.is_equal))

            def body(turn, more):
                for j in range(QUAD):
                    dve.bn_stats(stats[:, j, :], w["X"][:, bass.ds(turn * QUAD + j, 1), :]).then_inc(dve_step, 1)
                for j in range(QUAD):
                    apart.wait_ge(dve_step, turn * QUAD + (j + 1))
                    stats_ready.send(dve.bn_aggr(mv[:, j, :], stats[:, j, :]))
                for j in range(QUAD):
                    rstd_ready.wait(dve, turn, j)
                    xn_ready.send(dve.tensor_scalar(xn[:, j, :], w["X"][:, bass.ds(turn * QUAD + j, 1), :],
                                                    mv[:, j, 0:1], rstd[:, j:j + 1], ALU.subtract, ALU.mult))
                if more:
                    hot(turn + 1)
                for j in range(QUAD):
                    xT_high.wait(dve, turn, j)
                    banks.drain(dve.tensor_tensor(w["xTl"][:, :, bass.ts(turn * QUAD + j, P)],
                                                  banks.bank("turn", j).rearrange("p (c n) -> p c n", c=C),
                                                  w["xTh"][:, :, bass.ts(turn * QUAD + j, P)], ALU.subtract),
                                "turn", j)
            hot(0)
            dve.wait_ge(x_loaded, 16)
            with dve.Fori(0, TURNS - 1) as turn:
                body(turn, True)
            body(TURNS - 1, False)
            dve.wait_ge(mask_loaded, 16)
            dve.tensor_scalar(w["mask"][:, :, :], mask_raw[:, :, :], 0.0, MASKED, ALU.is_equal, ALU.mult)


def load_qkv(sp, io, w, head):
    def columns(name, width):
        return io[name].rearrange("(c p) n -> p c n", p=P)[:, :, bass.ts(head, width)]
    yield sp.dma_start(w["raw_q"][:, :, :], columns("Wq3", GROUP * HD))
    yield sp.dma_start(w["raw_kv"][:, 0, :, :], columns("Wk3", HD))
    yield sp.dma_start(w["raw_kv"][:, 1, :, :], columns("Wv3", HD))


def load_o(sp, io, w, head):
    return sp.dma_start(w["raw_o"][:, :, :],
                        io["Wo3"][bass.ts(head, GROUP * HD), :].rearrange("(h p) n -> p h n", p=P))


def last_attention(nc, io, w):
    PER = QUAD * P
    before = [(("q", "first", 0), 0), (("k", "first"), 1), (("q", "first", 1), 0), (("q", "first", 2), 1),
              (("q", "first", 3), 0), (("q", "first", 4), 1), (("v", "first"), 1), (("score", "first"), 2)]
    plan = []
    for n in range(QUAD):
        for u in range(QUAD):
            plan += [(("score", n, u), 2 + (u + 1) % 2), (("q", n, u), (0, 1, 0, 0)[u]), (("turn", n, u), 4)]
            if u == 0:
                plan.append((("k", n), 1))
            if u == QUAD - 1:
                plan.append((("v", n), 1))
            plan += [(("even", n, u), 5), (("odd", n, u), 6), (("out", n, u), 7)]
    with ExitStack() as ctx:
        def sb(name, shape, dt=F32):
            return ctx.enter_context(nc.sbuf_tensor("la_" + name, shape, dt))

        def signal(name, per_turn, by=1):
            return Signal(nc, w, "la_" + name, per_turn, by)

        raw_q, raw_kv, raw_o = w["raw_q"], w["raw_kv"], w["raw_o"]
        wqh, wql = sb("wqh", [P, C, GROUP * HD], HALF), sb("wql", [P, C, GROUP * HD], HALF)
        woh, wol = sb("woh", [P, GROUP, D], HALF), sb("wol", [P, GROUP, D], HALF)
        wkvh, wkvl = sb("wkvh", [P, 2, C, HD], HALF), sb("wkvl", [P, 2, C, HD], HALF)
        q, k = sb("q", [P, 2, GROUP, PER]), sb("k", [P, 2, PER])
        straight = sb("straight", [P, 2, PER])
        rot = sb("rot", [P, 2, PER])
        v2 = sb("v2", [P, 2, QUAD, 2, HD])
        s, p, pT = sb("s", [P, 2, GROUP, SEQ]), sb("p", [P, 2, GROUP, SEQ]), sb("pT", [P, 2, 2, P])
        mx, tot, rec = sb("mx", [P, 2, GROUP]), sb("tot", [P, 2, GROUP]), sb("rec", [P, 2, GROUP])
        oTh, oTl = sb("oTh", [P, 2, GROUP, P], HALF), sb("oTl", [P, 2, GROUP, P], HALF)

        banks = Banks(nc, ctx, w, "la", plan, before)
        q_loaded, o_loaded = signal("q_loaded", 1, 48), signal("o_loaded", 1, 16)
        q_high, q_low, o_high, o_low = signal("q_high", 6), signal("q_low", 6), signal("o_high", 4), signal("o_low", 4)
        rope_sum = signal("rope_sum", 20)
        first_step = new_semaphore(nc, w, "la_first_step")
        exp_ready, rec_ready, p_ready = signal("exp_ready", 16), signal("rec_ready", 16), signal("p_ready", 16)
        oT_high = signal("oT_high", 32)
        dve_step = new_semaphore(nc, w, "la_dve_step")
        block = ctx.enter_context(nc.Block())

        def tokens(n):
            return slice(n * PER, (n + 1) * PER)

        PIECES = ["q0", "k", "q1", "q2", "q3", "v"]
        SPLIT_IN = [("q0", "k"), ("q1",), ("q2",), ("q3", "v")]

        def raw_high_low(piece):
            if piece in ("k", "v"):
                i = ("k", "v").index(piece)
                return raw_kv[:, i, :, :], wkvh[:, i, :, :], wkvl[:, i, :, :]
            cols = slice(int(piece[1]) * HD, (int(piece[1]) + 1) * HD)
            return raw_q[:, :, cols], wqh[:, :, cols], wql[:, :, cols]

        FIRST = [(("q", "first", 0), 0, 0), (("k", "first"), None, 0), (("q", "first", 1), 1, 0),
                 (("q", "first", 2), 2, 0), (("q", "first", 3), 3, 0), (("q", "first", 4), 0, 1)]

        def projections(n, u, more):
            if u == QUAD - 1:
                found = [(5 * n + 4, ("q", n, u), 0, n + 2)]
            else:
                found = [(5 * n + u + 1, ("q", n, u), u + 1, n + 1)]
            if u == 0:
                found.insert(0, (5 * n, ("k", n), None, n + 1))
            return [(i, place, which, step % QUAD) for i, place, which, step in found if more or step < QUAD]

        @block.sync
        def _(sp):
            sp.sem_inc(o_loaded.sem, 16)
            with sp.Fori(0, KV - 1) as turn:
                q_low.wait(sp, turn, len(PIECES) - 1)
                for load in load_qkv(sp, io, w, turn + 1):
                    load.then_inc(q_loaded.sem, 16)
                o_low.wait(sp, turn, GROUP - 1)
                o_loaded.send(load_o(sp, io, w, turn + 1))

        @block.tensor
        def _(pe):
            def xs(t, n):
                return [t[:, c, tokens(n)] for c in range(C)]

            def next_piece(turn, piece):
                q_low.wait(pe, turn, len(PIECES) + PIECES.index(piece))

            def project_q(turn, step, n, u):
                banks.wait_free(pe, turn, *step)
                cols = slice(u * HD, (u + 1) * HD)
                banks.fill(three(pe, banks.bank(*step), [wqh[:, c, cols] for c in range(C)],
                                 [wql[:, c, cols] for c in range(C)], xs(w["xTh"], n), xs(w["xTl"], n)), *step)

            def project_k(turn, step, n):
                banks.wait_free(pe, turn, *step)
                banks.fill(three(pe, banks.bank(*step), [wkvh[:, 0, c, :] for c in range(C)],
                                 [wkvl[:, 0, c, :] for c in range(C)], xs(w["cTh"], n), xs(w["cTl"], n)), *step)

            def project_v(turn, step, n):
                banks.wait_free(pe, turn, *step)
                for t in range(QUAD):
                    cols = slice(n * PER + t * P, n * PER + (t + 1) * P)
                    last = three(pe, banks.bank(*step)[:, t * HD:(t + 1) * HD],
                                 [w["cTh"][:, c, cols] for c in range(C)], [w["cTl"][:, c, cols] for c in range(C)],
                                 [wkvh[:, 1, c, :] for c in range(C)], [wkvl[:, 1, c, :] for c in range(C)])
                banks.fill(last, *step)

            def out_projection(turn, n, u):
                for half in range(2):
                    banks.wait_drained(pe, turn, ("even", "odd")[half], n, u)
                if (n, u) == (0, 0):
                    o_low.wait(pe, turn, GROUP - 1)
                banks.wait_free(pe, turn, "out", n, u)
                banks.fill(three(pe, banks.bank("out", n, u), [oTh[:, u % 2, h, :] for h in range(GROUP)],
                                 [oTl[:, u % 2, h, :] for h in range(GROUP)], [woh[:, h, :] for h in range(GROUP)],
                                 [wol[:, h, :] for h in range(GROUP)]), "out", n, u)

            def scores(turn, place, n, u):
                m = n % 2
                banks.wait_free(pe, turn, *place)
                out = banks.bank(*place)[:, 0:GROUP * SEQ]
                pe.matmul(out, w["identh"][:, :],
                          w["mask"][:, n * QUAD + u, :].unsqueeze(1).to_broadcast([P, GROUP, SEQ]),
                          start=True, stop=True, skip_group_check=True)
                for b in range(2):
                    cols = slice(u * P + b * SEQ, u * P + (b + 1) * SEQ)
                    for h in range(GROUP):
                        last = pe.matmul(out[SEQ * b:SEQ * b + SEQ, h * SEQ:(h + 1) * SEQ], q[:, m, h, cols],
                                         k[:, m, cols], start=False, stop=True, skip_group_check=True)
                banks.fill(last, *place)

            def unit(turn, n, u, more):
                m = n % 2
                if more or (n, u) != (QUAD - 1, QUAD - 1):
                    if u == QUAD - 1:
                        rope_sum.wait(pe, turn, len(FIRST) + 5 * n + 3)
                    following = (QUAD * n + u + 1) % (QUAD * QUAD)
                    scores(turn, ("score", n, u), following // QUAD, following % QUAD)
                for _, place, which, step in projections(n, u, more):
                    if n == QUAD - 1 or (n, u) == (QUAD - 2, QUAD - 1):
                        next_piece(turn, "k" if which is None else f"q{which}")
                    if which is None:
                        project_k(turn, place, step)
                    else:
                        project_q(turn, place, step, which)
                p_ready.wait(pe, turn, QUAD * n + u)
                banks.wait_free(pe, turn, "turn", n, u)
                for hp in range(2):
                    last = pe.transpose(banks.bank("turn", n, u)[:, hp * P:(hp + 1) * P],
                                        p[:, u % 2, 2 * hp:2 * hp + 2, :].rearrange("p h k -> p (h k)"),
                                        w["ident"][:, :])
                banks.fill(last, "turn", n, u)
                if (n, u) != (0, 0):
                    out_projection(turn, n if u else n - 1, (u - 1) % QUAD)
                if u == QUAD - 1 and n < QUAD - 1:
                    project_v(turn, ("v", n), (n + 1) % QUAD)
                banks.wait_drained(pe, turn, "turn", n, u)
                if (n, u) == (0, 0):
                    banks.wait_all_drained(pe, turn, 1)
                elif u == 0:
                    banks.wait_drained(pe, turn, "v", n - 1)
                for half, name in enumerate(("even", "odd")):
                    banks.wait_free(pe, turn, name, n, u)
                    rows = slice(SEQ * half, SEQ * half + SEQ)
                    out = banks.bank(name, n, u)[:, 0:2 * P].rearrange("p (h t) -> p h t", h=2)
                    for b in range(2):
                        cols = slice(SEQ * b, SEQ * b + SEQ)
                        last = pe.matmul(out[:, :, cols], v2[rows, m, u, b, :], pT[rows, u % 2, :, cols],
                                         start=True, stop=True)
                    banks.fill(last, name, n, u)

            def body(turn, more):
                for n in range(QUAD):
                    for u in range(QUAD):
                        unit(turn, n, u, more)
                if more:
                    next_piece(turn, "v")
                    project_v(turn, ("v", QUAD - 1), 0)
                out_projection(turn, QUAD - 1, QUAD - 1)

            for place, which, step in FIRST:
                q_low.wait(pe, 0, PIECES.index("k" if which is None else f"q{which}"))
                if which is None:
                    project_k(0, place, step)
                else:
                    project_q(0, place, step, which)
            q_low.wait(pe, 0, PIECES.index("v"))
            project_v(0, ("v", "first"), 0)
            rope_sum.wait(pe, 0, 4)
            scores(0, ("score", "first"), 0, 0)
            with pe.Fori(0, KV - 1) as turn:
                body(turn, True)
            body(KV - 1, False)

        @block.scalar
        def _(act):
            def high_of(piece):
                raw, high, _ = raw_high_low(piece)
                q_high.send(act.activation(high, raw, ACT.Copy))

            def exponentials(turn, place, slot):
                flat = s[:, slot, :, :].rearrange("p h k -> p (h k)")
                banks.wait_drained(act, turn, *place)
                exp_ready.send(act.activation(flat, flat, ACT.Exp, scale=float(HD) ** -0.5))

            def copy_v(turn, step, m):
                banks.wait_filled(act, turn, *step)
                for half in range(2):
                    for b in range(2):
                        src = banks.bank(*step)[SEQ * b:SEQ * b + SEQ, :].rearrange("p (t n) -> p t n", t=QUAD)
                        last = act.activation(v2[SEQ * half:SEQ * half + SEQ, m, :, b, :], src, ACT.Copy)
                banks.drain(last, *step)

            def body(turn, more):
                for n in range(QUAD):
                    for u in range(QUAD):
                        if more or (n, u) != (QUAD - 1, QUAD - 1):
                            exponentials(turn, ("score", n, u), (u + 1) % 2)
                        if (n, u) == (0, 0):
                            o_loaded.wait(act, turn, 0)
                            banks.wait_all_filled(act, turn, 7)
                            for h in range(GROUP):
                                o_high.send(act.activation(woh[:, h, :], raw_o[:, h, :], ACT.Copy))
                        banks.wait_filled(act, turn, "turn", n, u)
                        banks.drain(act.activation(pT[:, u % 2, :, :].rearrange("p h k -> p (h k)"),
                                                   banks.bank("turn", n, u)[:, 0:2 * P], ACT.Copy), "turn", n, u)
                        if n < QUAD - 1 and u == QUAD - 1:
                            copy_v(turn, ("v", n), (n + 1) % 2)
                        for half, name in enumerate(("even", "odd")):
                            banks.wait_filled(act, turn, name, n, u)
                            oT_high.send(act.activation(
                                oTh[:, u % 2, :, :].rearrange("p (a b) t -> p a b t", b=2)[:, :, half, :],
                                banks.bank(name, n, u)[:, 0:2 * P].rearrange("p (h t) -> p h t", h=2), ACT.Copy))
                        if more and n == QUAD - 2:
                            if u == 0:
                                q_loaded.wait(act, turn, 0)
                            for piece in SPLIT_IN[u]:
                                if piece in ("k", "v"):
                                    banks.wait_filled(act, turn, piece, n)
                                elif piece == "q0":
                                    banks.wait_filled(act, turn, "q", n - 1, QUAD - 1)
                                else:
                                    banks.wait_filled(act, turn, "q", n, int(piece[1]) - 1)
                                high_of(piece)
                if more:
                    copy_v(turn, ("v", QUAD - 1), 0)

            for piece in PIECES:
                high_of(piece)
            copy_v(0, ("v", "first"), 0)
            exponentials(0, ("score", "first"), 0)
            with act.Fori(0, KV - 1) as turn:
                body(turn, True)
            body(KV - 1, False)

        @block.gpsimd
        def _(pool):
            banks.open(pool)
            def add_rotation(turn, step, slot, dst):
                banks.wait_drained(pool, turn, *step)
                rope_sum.send(pool.tensor_tensor(dst, straight[:, slot, :], rot[:, slot, :], ALU.add))

            def low_of(turn, first, piece):
                q_high.wait(pool, turn, first + PIECES.index(piece))
                raw, high, low = raw_high_low(piece)
                q_low.send(pool.tensor_tensor(low, raw, high, ALU.subtract))

            def rotated(which, step):
                return k[:, step % 2, :] if which is None else q[:, step % 2, which, :]

            def divide(turn, i, slot):
                rec_ready.wait(pool, turn, i)
                p_ready.send(pool.tensor_tensor(p[:, slot, :, :], s[:, slot, :, :],
                                                rec[:, slot, :].unsqueeze(2).to_broadcast([P, GROUP, SEQ]),
                                                ALU.mult))

            def body(turn, more):
                for n in range(QUAD):
                    for u in range(QUAD):
                        if more or (n, u) != (QUAD - 1, QUAD - 1):
                            divide(turn, QUAD * n + u + 1, (u + 1) % 2)
                        if (n, u) == (0, 0):
                            for h in range(GROUP):
                                o_high.wait(pool, turn, h)
                                o_low.send(pool.tensor_tensor(wol[:, h, :], raw_o[:, h, :], woh[:, h, :],
                                                              ALU.subtract))
                        for i, place, which, step in projections(n, u, more):
                            add_rotation(turn, place, (len(FIRST) + i) % 2, rotated(which, step))
                        if more and n == QUAD - 2:
                            for piece in SPLIT_IN[u]:
                                low_of(turn, len(PIECES), piece)

            for piece in PIECES:
                low_of(0, 0, piece)
            for i, (place, which, step) in enumerate(FIRST):
                add_rotation(0, place, i % 2, rotated(which, step))
            divide(0, 0, 0)
            with pool.Fori(0, KV - 1) as turn:
                body(turn, True)
            body(KV - 1, False)

        @block.vector
        def _(dve):
            def rotate(turn, k_at, slot, step, n):
                if k_at >= 2:
                    rope_sum.wait(dve, turn, k_at - 2)
                banks.wait_filled(dve, turn, *step)
                src = banks.bank(*step)
                dve.tensor_tensor(straight[:, slot, :], src, w["cos"][:, tokens(n)], ALU.mult)
                dve.tensor_tensor(rot[0:64, slot, :], src[64:128, :], w["sin"][64:128, tokens(n)], ALU.mult)
                banks.drain(dve.tensor_tensor(rot[64:128, slot, :], src[0:64, :], w["sin"][0:64, tokens(n)],
                                              ALU.mult), *step)

            def softmax(turn, st, place, slot, i):
                banks.wait_filled(dve, turn, *place)
                scores = banks.bank(*place)[:, 0:GROUP * SEQ].rearrange("p (h k) -> p h k", k=SEQ)
                st.link(dve.tensor_reduce(mx[:, slot, :], scores, AX.X, ALU.max))
                banks.drain(dve.tensor_tensor(s[:, slot, :, :], scores,
                                              mx[:, slot, :].unsqueeze(2).to_broadcast([P, GROUP, SEQ]),
                                              ALU.subtract), *place)
                exp_ready.wait(dve, turn, i)
                st.link(dve.tensor_reduce(tot[:, slot, :], s[:, slot, :, :], AX.X, ALU.add))
                rec_ready.send(dve.reciprocal(rec[:, slot, :], tot[:, slot, :]))

            def lows(turn, n, u):
                for half, name in enumerate(("even", "odd")):
                    oT_high.wait(dve, turn, 2 * (QUAD * n + u) + half)
                    mine = [t[:, u % 2, :, :].rearrange("p (a b) t -> p a b t", b=2)[:, :, half, :] for t in (oTl, oTh)]
                    banks.drain(dve.tensor_tensor(
                        mine[0], banks.bank(name, n, u)[:, 0:2 * P].rearrange("p (h t) -> p h t", h=2), mine[1],
                        ALU.subtract), name, n, u)

            def add_out(turn, n, u):
                banks.wait_filled(dve, turn, "out", n, u)
                tile = w["X"][:, n * QUAD + u, :]
                banks.drain(dve.scalar_tensor_tensor(out=tile, in0=banks.bank("out", n, u),
                                                     scalar=w["gates"][:, 3:4], in1=tile, op0=ALU.mult, op1=ALU.add),
                            "out", n, u)

            def body(turn, more):
                st = Steps(dve, dve_step, LAST_STEPS, turn)
                banks.wait_all_drained(dve, turn, 7)
                for n in range(QUAD):
                    for u in range(QUAD):
                        if (n, u) != (0, 0):
                            prev = (n, u - 1) if u else (n - 1, QUAD - 1)
                            lows(turn, *prev)
                        if more or (n, u) != (QUAD - 1, QUAD - 1):
                            softmax(turn, st, ("score", n, u), (u + 1) % 2, QUAD * n + u + 1)
                        for i, place, _, step in projections(n, u, more):
                            rotate(turn, len(FIRST) + i, (len(FIRST) + i) % 2, place, step)
                        if (n, u) != (0, 0):
                            add_out(turn, *prev)
                lows(turn, QUAD - 1, QUAD - 1)
                add_out(turn, QUAD - 1, QUAD - 1)
                if more:
                    st.close()

            for i, (place, _, step) in enumerate(FIRST):
                rotate(0, i, i % 2, place, step)
            softmax(0, Steps(dve, first_step, 2, 0), ("score", "first"), 0, 0)
            with dve.Fori(0, KV - 1) as turn:
                body(turn, True)
            body(KV - 1, False)


def last_ffn(nc, io, w):
    plan = [(("turn", j), j % 4) for j in range(EIGHT)]
    plan += [(("route", j), j % 4) for j in range(EIGHT)]
    for j in range(EIGHT):
        plan += [(("hturn", j), j % 4), (("out", j), 4 + j % 4)]
    with ExitStack() as ctx:
        def sb(name, shape, dt=F32):
            return ctx.enter_context(nc.sbuf_tensor("lf_" + name, shape, dt))

        def signal(name, per_turn, by=1):
            return Signal(nc, w, "lf_" + name, per_turn, by)

        xn, xout = sb("xn", [P, EIGHT, D]), sb("xout", [P, EIGHT, D])
        stats, mv = sb("stats", [P, EIGHT, 6]), sb("mv", [P, EIGHT, 2])
        vare, rstd = sb("vare", [P, EIGHT]), sb("rstd", [P, EIGHT])
        xTh, xTl = sb("xTh", [P, EIGHT, C, P], HALF), sb("xTl", [P, EIGHT, C, P], HALF)
        e, pick = sb("e", [P, EIGHT, 10]), sb("pick", [P, EIGHT, 8])
        low4 = sb("low4", [P, EIGHT, 8])
        top8, keep = sb("top8", [P, EIGHT, 8]), sb("keep", [P, EIGHT, 10])
        rh = sb("rh", [P, EIGHT, R3 + LORA3])
        sel, comb = sb("sel", [P, EIGHT, R3]), sb("comb", [P, EIGHT, R3])
        nmax, tot, rec = sb("nmax", [P, EIGHT]), sb("tot", [P, EIGHT]), sb("rec", [P, EIGHT])
        hs, hsT = sb("hs", [P, EIGHT, LORA3]), sb("hsT", [LORA3, EIGHT, P])
        banks = Banks(nc, ctx, w, "lf", plan)
        stats_ready, rstd_ready, xn_ready = signal("stats_ready", EIGHT), signal("rstd_ready", EIGHT), signal("xn_ready", EIGHT)
        xT_high, logit_ready, expo_ready = signal("xT_high", EIGHT), signal("logit_ready", EIGHT), signal("expo_ready", EIGHT)
        stored, hs_ready = signal("stored", EIGHT, 16), signal("hs_ready", EIGHT)
        dve_step = new_semaphore(nc, w, "lf_dve_step")
        pool_step = new_semaphore(nc, w, "lf_pool_step")
        pads = new_semaphore(nc, w, "lf_pads")
        block = ctx.enter_context(nc.Block())

        @block.sync
        def _(sp):
            with sp.Fori(0, TILES // EIGHT) as turn:
                for j in range(EIGHT):
                    banks.wait_drained(sp, turn, "out", j)
                    stored.send(sp.dma_start(io["out"][bass.ts(turn * EIGHT + j, P), :], xout[:, j, :]))
            sp.wait_ge(stored.sem, TILES // EIGHT * EIGHT * 16 + 1)

        @block.gpsimd
        def _(pool):
            banks.open(pool)
            pool.sem_inc(stored.sem, 1)
            pool.memset(e[:, :, :], NEVER).then_inc(pads, 1)
            pool.memset(pick[:, :, :], NEVER).then_inc(pads, 1)
            pool.memset(low4[:, :, :], 0.0).then_inc(pads, 1)
            with pool.Fori(0, TILES // EIGHT) as turn:
                for j in range(EIGHT):
                    stats_ready.wait(pool, turn, j)
                    pool.tensor_tensor(vare[:, j:j + 1], mv[:, j, 1:2], w["eps"][:, :], ALU.add)\
                        .then_inc(pool_step, 1)
                    pool.wait_ge(pool_step, turn * EIGHT + (j + 1))
                    rstd_ready.send(pool.tensor_tensor(rstd[:, j:j + 1], vare[:, j:j + 1], w["power"][:, 0:1],
                                                       ALU.pow))

        @block.tensor
        def _(pe):
            apart = Apart(pe, pads, 3)
            with pe.Fori(0, TILES // EIGHT) as turn:
                for j in range(EIGHT):
                    xn_ready.wait(pe, turn, j)
                    banks.wait_free(pe, turn, "turn", j)
                    for c in range(C):
                        last = pe.transpose(banks.bank("turn", j)[:, c * P:(c + 1) * P],
                                            xn[:, j, c * P:(c + 1) * P], w["ident"][:, :])
                    banks.fill(last, "turn", j)
                for j in range(EIGHT):
                    banks.wait_drained(pe, turn, "turn", j)
                    banks.wait_free(pe, turn, "route", j)
                    banks.fill(three(pe, banks.bank("route", j)[:, 0:R3 + LORA3],
                                     [xTh[:, j, c, :] for c in range(C)], [xTl[:, j, c, :] for c in range(C)],
                                     [w["R3h"][:, c, :] for c in range(C)], [w["R3l"][:, c, :] for c in range(C)]),
                               "route", j)
                def turn_hs(j):
                    hs_ready.wait(pe, turn, j)
                    banks.wait_free(apart, turn, "hturn", j)
                    banks.fill(pe.transpose(banks.bank("hturn", j)[0:LORA3, 0:P], hs[:, j, :], w["ident"][:, :]),
                               "hturn", j)
                turn_hs(0)
                for j in range(EIGHT):
                    if j + 1 < EIGHT:
                        turn_hs(j + 1)
                    banks.wait_drained(pe, turn, "hturn", j)
                    banks.wait_free(pe, turn, "out", j)
                    banks.fill(pe.matmul(banks.bank("out", j), hsT[:, j, :], w["B3"][:, :], start=True, stop=True),
                               "out", j)

        @block.scalar
        def _(act):
            act.wait_ge(pads, 3)
            with act.Fori(0, TILES // EIGHT) as turn:
                for j in range(EIGHT):
                    banks.wait_filled(act, turn, "turn", j)
                    xT_high.send(act.activation(xTh[:, j, :, :].rearrange("p c n -> p (c n)"), banks.bank("turn", j),
                                                ACT.Copy))
                for j in range(EIGHT):
                    banks.wait_filled(act, turn, "route", j)
                    banks.drain(act.activation(rh[:, j, :], banks.bank("route", j)[:, 0:R3 + LORA3], ACT.Copy),
                                "route", j)
                for j in range(EIGHT):
                    logit_ready.wait(act, turn, j)
                    expo_ready.send(act.activation(e[:, j, 0:R3], rh[:, j, 0:R3], ACT.Exp, bias=nmax[:, j:j + 1]))
                for j in range(EIGHT):
                    banks.wait_filled(act, turn, "hturn", j)
                    banks.drain(act.activation(hsT[:, j, :], banks.bank("hturn", j)[0:LORA3, 0:P], ACT.Copy),
                                "hturn", j)

        @block.vector
        def _(dve):
            apart = Apart(dve, pads, 3)
            dve.wait_ge(pads, 3)
            with dve.Fori(0, TILES // EIGHT) as turn:
                st = Steps(dve, dve_step, FFN_STEPS, turn)
                def x_of(j):
                    return w["X"][:, bass.ds(turn * EIGHT + j, 1), :]

                def statistics(j):
                    n = st.step(dve.bn_stats(stats[:, j, :], x_of(j)))
                    st.after(n, apart)
                    stats_ready.send(dve.bn_aggr(mv[:, j, :], stats[:, j, :]))

                def low(j):
                    xT_high.wait(dve, turn, j)
                    banks.drain(dve.tensor_tensor(xTl[:, j, :, :].rearrange("p c n -> p (c n)"),
                                                  banks.bank("turn", j),
                                                  xTh[:, j, :, :].rearrange("p c n -> p (c n)"), ALU.subtract),
                                "turn", j)

                statistics(0)
                for j in range(EIGHT):
                    if j + 1 < EIGHT:
                        statistics(j + 1)
                    rstd_ready.wait(dve, turn, j)
                    xn_ready.send(dve.tensor_scalar(xn[:, j, :], x_of(j), mv[:, j, 0:1], rstd[:, j:j + 1],
                                                    ALU.subtract, ALU.mult))
                    if j >= 1:
                        low(j - 1)
                low(EIGHT - 1)

                for j in range(EIGHT):
                    banks.wait_drained(dve, turn, "route", j)
                    logit_ready.send(dve.tensor_reduce(nmax[:, j:j + 1], rh[:, j, 0:R3], AX.X, ALU.max, negate=True))

                expo_ready.wait(dve, turn, EIGHT - 1)
                n = st.step(dve.tensor_copy(low4[:, :, 0:R3], e[:, :, 0:R3]))
                st.after(n, apart)
                for j in range(EIGHT):
                    n = st.step(dve.max(top8[:, j, :], low4[:, j, :]))
                st.after(n)
                n = st.step(dve.tensor_copy(pick[:, :, 0:2], top8[:, :, 0:2]))
                summed = st.step(dve.tensor_tensor(tot[:, :], top8[:, :, 0], top8[:, :, 1], ALU.add))
                st.after(n, apart)
                for j in range(EIGHT):
                    n = st.step(dve.match_replace(keep[:, j, :], pick[:, j, :], e[:, j, :], 0.0))
                st.after(summed)
                st.step(dve.reciprocal(rec[:, :], tot[:, :]))
                st.after(n)
                st.link(dve.tensor_tensor(sel[:, :, :], e[:, :, 0:R3], keep[:, :, 0:R3], ALU.subtract))
                st.link(dve.scalar_tensor_tensor(
                    out=comb[:, :, :], in0=sel[:, :, :], scalar=4.0,
                    in1=rec[:, :].unsqueeze(2).to_broadcast([P, EIGHT, R3]), op0=ALU.mult, op1=ALU.mult))
                for j in range(EIGHT):
                    hs_ready.send(dve.tensor_tensor(
                        hs[:, j, :].rearrange("p (e r) -> p e r", r=RANK),
                        rh[:, j, R3:R3 + LORA3].rearrange("p (e r) -> p e r", r=RANK),
                        comb[:, j, :].unsqueeze(2).to_broadcast([P, E3, RANK]), ALU.mult))
                for j in range(EIGHT):
                    banks.wait_filled(dve, turn, "out", j)
                    dve.wait_ge(stored.sem, turn * (EIGHT * 16) + 1)
                    banks.drain(dve.scalar_tensor_tensor(
                        out=xout[:, j, :].unsqueeze(1), in0=banks.bank("out", j).unsqueeze(1),
                        scalar=w["gates"][:, 7:8], in1=x_of(j), op0=ALU.mult, op1=ALU.add), "out", j)
                st.close()


def build(nc, io):
    with ExitStack() as whole:
        def keep(stack, name, shape, dt=F32):
            w[name] = stack.enter_context(nc.sbuf_tensor("w_" + name, shape, dt))

        w = {}
        for name, shape, dt in (("gates", [P, 8], F32), ("ident", [P, P], F32), ("identh", [P, P], BF16),
                                ("power", [P, 1], F32), ("eps", [P, 1], F32), ("R3h", [P, C, R3 + LORA3], HALF),
                                ("R3l", [P, C, R3 + LORA3], HALF), ("B3", [LORA3, D], F32)):
            keep(whole, name, shape, dt)
        io["x_mid"] = nc.dram_tensor("x_mid", (TOKENS, D), F32).ap()
        with ExitStack() as early:
            for name, cols in (("M", D), ("W0", D), ("W1", D), ("R0", R0 + LORA), ("R1", R1 + LORA), ("Wqd", 64),
                               ("Wkv", P)):
                for half in "hl":
                    keep(early, name + half, [P, C, cols], HALF)
            for name, shape, dt in (
                    ("ch", [P, C], HALF), ("cl", [P, C], HALF), ("r", [P, C], F32), ("s", [P, 1], F32),
                    ("bdmask", [P, P], F32), ("B0", [LORA, D], F32), ("B1", [LORA, D], F32),
                    ("L1W", [P, 4, P], F32), ("L1b", [P, 4], F32), ("rb1", [P, R1], F32),
                    ("route_to", [P, E01, R1], F32), ("expert_id", [P, E01, R1], F32), ("gbias", [P, 3, D], F32),
                    ("Wqk", [64, D], F32), ("Wvu", [L2K, D], F32), ("quarter", [P, 4], F32),
                    ("gate2", [P, C, E01], F32), ("ics", [E01, D], F32), ("ocs", [E01, D], F32),
                    ("sign2", [P, C, D], BF16)):
                keep(early, name, shape, dt)
            with stage(nc, w):
                prepare_weights(nc, io, w)
            with stage(nc, w):
                early_layers(nc, io, w)
        keep(whole, "X", [P, TILES, D])
        with ExitStack() as attention:
            for name in ("xTh", "xTl", "cTh", "cTl"):
                keep(attention, name, [P, C, TOKENS], HALF)
            for name, shape in (("raw_q", [P, C, GROUP * HD]), ("raw_kv", [P, 2, C, HD]), ("raw_o", [P, GROUP, D])):
                keep(attention, name, shape)
            keep(attention, "cos", [P, TOKENS])
            keep(attention, "sin", [P, TOKENS])
            keep(attention, "mask", [P, TILES, SEQ], BF16)
            with stage(nc, w):
                prepare_last(nc, io, w)
            with stage(nc, w):
                last_attention(nc, io, w)
        with stage(nc, w):
            last_ffn(nc, io, w)


def rope_tables():
    inv = (1.0 / np.float32(10000.0) ** (np.arange(0, HD, 2, dtype=np.float32) / np.float32(HD))).astype(np.float32)
    angle = np.arange(POSITIONS, dtype=np.float32)[:, None] * inv[None, :]
    cos, sin = np.cos(angle).astype(np.float32), np.sin(angle).astype(np.float32)
    return np.concatenate([cos, cos], 1), np.concatenate([sin, -sin], 1)


def layout(i):
    a = {k: np.asarray(v) for k, v in i.items()}
    cos, sin = rope_tables()
    two = (TOKENS, D)
    return {
        "x": a["x"].reshape(two), "ctx": a["ctx_4096"].reshape(two), "ctxT": a["ctx_4096"].reshape(two).T,
        "pos": a["pos_BxS2"].reshape(TOKENS), "mask": a["mask_BxSxS2_ik0"].reshape(TOKENS, SEQ),
        "gates": np.concatenate([a["g_xattn"], a["g_ffn"]]),
        "L0_Wq": a["L0_xattn_Wq"], "L0_Wk": a["L0_xattn_Wk"],
        "L0_bq": a["L0_xattn_bq"].reshape(C, P).T, "L0_bk": a["L0_xattn_bk"].reshape(C, P).T,
        "W0": a["L0_ffn_W_base"].T, "b0": a["L0_ffn_b_base"],
        "R0": np.concatenate([a["L0_ffn_W_router"], a["L0_ffn_A_stack"].reshape(LORA, D)]).T,
        "B0": a["L0_ffn_B_stack"].transpose(0, 2, 1).reshape(LORA, D),
        "L1W": np.stack([a["L1_xattn_" + n].T for n in ("Wq", "Wk", "Wv", "Wo")]),
        "L1b": np.stack([a["L1_xattn_" + n] for n in ("bq", "bk", "bv", "bo")], 1),
        "W1": a["L1_ffn_base_W"].T, "b1": a["L1_ffn_base_b"], "rb1": a["L1_ffn_router_b"],
        "R1": np.concatenate([a["L1_ffn_router_W"], a["L1_ffn_A"].reshape(LORA, D)]).T,
        "B1": a["L1_ffn_B"].transpose(0, 2, 1).reshape(LORA, D), "emap": a["L1_ffn_expert_map"],
        "Wqd": a["L2_xattn_Wq_d"], "Wkv": np.tile(a["L2_xattn_Wkv_d"], (1, 4)), "Wqk": a["L2_xattn_W_qk"],
        "Wvu": a["L2_xattn_Wv_u"].reshape(L2K, 8, 2, 32).transpose(0, 2, 1, 3).reshape(L2K, D),
        "W2": a["L2_ffn_weight"].T, "b2": a["L2_ffn_bias"], "gate2": a["L2_ffn_gate_w"].T,
        "ics": a["L2_ffn_in_channel_scale"], "ocs": a["L2_ffn_out_channel_scale"],
        "Wq3": a["L3_xattn_Wq"], "Wk3": a["L3_xattn_Wk"], "Wv3": a["L3_xattn_Wv"], "Wo3": a["L3_xattn_Wo"],
        "R3": np.concatenate([a["L3_ffn_Wr"], a["L3_ffn_A"].reshape(LORA3, D)]).T,
        "B3": a["L3_ffn_B"].transpose(0, 2, 1).reshape(LORA3, D),
        "cos": cos, "sin": sin,
    }


def kernel(**inputs):
    import concourse.bacc as bacc
    from concourse.bass_utils import run_bass_kernel_spmd

    nc = bacc.Bacc("TRN2", target_bir_lowering=False, num_devices=1)
    arrays, io = {}, {}
    for name, a in layout(inputs).items():
        a = np.ascontiguousarray(a)
        arrays["in_" + name] = a
        io[name] = nc.dram_tensor("in_" + name, a.shape, mybir.dt.from_np(a.dtype), kind="ExternalInput").ap()
    io["out"] = nc.dram_tensor("out_0", (TOKENS, D), F32, kind="ExternalOutput").ap()
    build(nc, io)
    result = run_bass_kernel_spmd(nc, [arrays], core_ids=[0])
    return result.results[0]["out_0"].reshape(BATCH, SEQ, D)
```
